# Optimizing a Trainium2 kernel written in Bass

```python
import numpy as np
import jax
import jax.numpy as jnp

def _softmax(x, axis=-1):
    return jax.nn.softmax(x, axis=axis)

def _gelu(x):
    return jax.nn.gelu(x, approximate=True)

def _silu(x):
    return jax.nn.silu(x)

def _sigmoid(x):
    return jax.nn.sigmoid(x)

def _layernorm(x, axis=-1, eps=1e-05):
    m = jnp.mean(x, axis=axis, keepdims=True)
    v = jnp.var(x, axis=axis, keepdims=True)
    return (x - m) / jnp.sqrt(v + eps)

def _scatter_add(tgt, idx, src, axis=0):
    return tgt.at[idx].add(src)

def _segment_sum(src, seg, n):
    return jax.ops.segment_sum(src, seg, n)
kernel_name = 'mk_flamingo_gated_d4_seqx_r8_a0c88b'

def setup_inputs(seed: int=0):
    np.random.seed(seed)
    _w = jnp.asarray

    def _rec_inputs():
        import jax
        import jax.numpy as jnp
        _rk = jax.random.key(seed)
        x = 7.22e-05 + 1 * jax.random.normal(jax.random.fold_in(_rk, 1), (8, 256, 128), jnp.float32)
        _lenS = 256 - jax.random.randint(jax.random.fold_in(_rk, 7), (8,), 0, max(1, 256 // 4) + 1, jnp.int32)
        _lenS2 = 256 - jax.random.randint(jax.random.fold_in(_rk, 8), (8,), 0, max(1, 256 // 4) + 1, jnp.int32)
        _ctx_1024P = jax.random.normal(jax.random.fold_in(_rk, 11), (8, 16, 128), jnp.float32)
        _ctx_1024c = jax.random.dirichlet(jax.random.fold_in(_rk, 511), 0.3 * jnp.ones((16,), jnp.float32), (8, 256))
        _ctx_1024t = jnp.einsum('bsk,bkd->bsd', _ctx_1024c, _ctx_1024P)
        _ctx_1024t = _ctx_1024t * jax.lax.rsqrt(jnp.mean(jnp.square(_ctx_1024t)) + 1e-12) * 0.953939
        ctx_1024 = 4.13588e-05 + 0.999923 * (_ctx_1024t + 0.3 * jax.random.normal(jax.random.fold_in(_rk, 611), (8, 256, 128), jnp.float32))
        _g = jax.random.normal(jax.random.fold_in(_rk, 9001), (2, 4), jnp.float32)
        _g = jnp.sign(_g) * jnp.maximum(jnp.abs(_g), 1.0) + (_g == 0) * 1.0
        g_xattn = _g[0]
        g_ffn = _g[1]
        return (x, ctx_1024, g_xattn, g_ffn)
    x, ctx_1024, g_xattn, g_ffn = _rec_inputs()

    def _L0_xattn_setup():
        import jax, jax.numpy as jnp
        import numpy as np
        D_MODEL = 128
        NUM_HEADS = 16
        KERNEL_EPS = 0.0001
        NORM_STAB = 1e-06

        def _performer_forward(query, key, value, random_features):
            B, L, dm = query.shape
            h = NUM_HEADS
            d = dm // h
            m = random_features.shape[1]

            def split_heads(x):
                return x.reshape(B, L, h, d).transpose(0, 2, 1, 3)
            q, k, v = (split_heads(query), split_heads(key), split_heads(value))
            scale = dm ** (-0.25)
            q = q * scale
            k = k * scale
            proj_q = jnp.einsum('bhld,dm->bhlm', q, random_features)
            proj_k = jnp.einsum('bhld,dm->bhlm', k, random_features)
            h_q = -0.5 * jnp.sum(q * q, axis=-1, keepdims=True)
            h_k = -0.5 * jnp.sum(k * k, axis=-1, keepdims=True)
            q_stab = h_q
            k_stab = jnp.max(h_k)
            q_kernel = jnp.exp(h_q + (proj_q - q_stab))
            k_kernel = jnp.exp(h_k + (proj_k - k_stab))
            nc = m ** (-0.5)
            q_prime = nc * (q_kernel + KERNEL_EPS)
            k_prime = nc * (k_kernel + KERNEL_EPS)
            qp = q_prime.transpose(2, 0, 1, 3)
            kp = k_prime.transpose(2, 0, 1, 3)
            vp = v.transpose(2, 0, 1, 3)

            def step(carry, inp):
                S, Z = carry
                qt, kt, vt = inp
                S = S + kt[..., :, None] * vt[..., None, :]
                Z = Z + kt
                num = jnp.einsum('bhm,bhmd->bhd', qt, S)
                den = jnp.einsum('bhm,bhm->bh', qt, Z)
                return ((S, Z), (num, den))
            S0 = jnp.zeros((B, h, m, d), q_prime.dtype)
            Z0 = jnp.zeros((B, h, m), q_prime.dtype)
            _, (nums, dens) = jax.lax.scan(step, (S0, Z0), (qp, kp, vp))
            nums = nums.transpose(1, 2, 0, 3)
            dens = dens.transpose(1, 2, 0)[..., None]
            extreme = (jnp.abs(dens) <= NORM_STAB).astype(dens.dtype)
            dens = dens + 2.0 * NORM_STAB * extreme
            out = nums / dens
            return out.transpose(0, 2, 1, 3).reshape(B, L, dm)
        key = jax.random.key(seed)
        k1, k2, k3, k4 = jax.random.split(key, 4)
        B, L = (4, 256)
        d_head, m = (D_MODEL // NUM_HEADS, 32)
        return {'query': jax.random.normal(k1, (B, L, D_MODEL), jnp.float32), 'key': jax.random.normal(k2, (B, L, D_MODEL), jnp.float32), 'value': jax.random.normal(k3, (B, L, D_MODEL), jnp.float32), 'random_features': jax.random.normal(k4, (d_head, m), jnp.float32)}
    _L0_xattn_all = _L0_xattn_setup()
    _L0_xattn_in = {k: v for k, v in _L0_xattn_all.items() if k in ('random_features',)}
    del _L0_xattn_all

    def _L0_ffn_setup():
        import jax, jax.numpy as jnp
        import numpy as np
        NUM_HEADS = 16
        TOP_K = 2
        key = jax.random.key(seed)
        ks = jax.random.split(key, 5)
        B, S, D, E = (4, 256, 128, 8)
        scale = 0.02
        return {'x': jax.random.normal(ks[0], (B, S, D), dtype=jnp.float32), 'W_qkv': jax.random.normal(ks[1], (D, 3 * D), dtype=jnp.float32) * scale, 'b_qkv': jnp.zeros((3 * D,), dtype=jnp.float32), 'W_gate': jax.random.normal(ks[2], (D, E), dtype=jnp.float32) * scale, 'b_gate': jnp.zeros((E,), dtype=jnp.float32), 'W_experts': jax.random.normal(ks[3], (E, D, D), dtype=jnp.float32) * scale, 'b_experts': jnp.zeros((E, D), dtype=jnp.float32)}
    _L0_ffn_all = _L0_ffn_setup()
    _L0_ffn_in = {k: v for k, v in _L0_ffn_all.items() if k in ('W_qkv', 'b_qkv', 'W_gate', 'b_gate', 'W_experts', 'b_experts')}
    del _L0_ffn_all

    def _L1_xattn_setup():
        import jax, jax.numpy as jnp
        import numpy as np
        HEADS = 8
        DIM_HEAD = 64
        key = jax.random.key(seed)
        ks = jax.random.split(key, 6)
        B, Nq, Nk, Dq = (4, 256, 256, 128)
        inner = HEADS * DIM_HEAD
        return {'x': jax.random.normal(ks[0], (B, Nq, Dq), jnp.float32), 'context': jax.random.normal(ks[1], (B, Nk, Dq), jnp.float32), 'Wq': jax.random.normal(ks[2], (Dq, inner), jnp.float32) * 0.02, 'Wkv': jax.random.normal(ks[3], (Dq, 2 * inner), jnp.float32) * 0.02, 'Wout': jax.random.normal(ks[4], (inner, Dq), jnp.float32) * 0.02, 'bout': jax.random.normal(ks[5], (Dq,), jnp.float32) * 0.02, 'topk': 64}
    _L1_xattn_all = _L1_xattn_setup()
    _L1_xattn_in = {k: v for k, v in _L1_xattn_all.items() if k in ('Wq', 'Wkv', 'Wout', 'bout')}
    del _L1_xattn_all

    def _L1_ffn_setup():
        import jax, jax.numpy as jnp
        import numpy as np
        E = 8
        TOPK = 2
        H = 128
        I = 128
        ISH = I * 2
        B, S = (2, 128)
        key = jax.random.key(seed)
        ks = jax.random.split(key, 7)
        s = 0.02
        return {'hidden_states': jax.random.normal(ks[0], (B, S, H), jnp.float32), 'w_router': jax.random.normal(ks[1], (H, E), jnp.float32) * s, 'fc1_w': jax.random.normal(ks[2], (E, H, 2 * I), jnp.float32) * s, 'fc2_w': jax.random.normal(ks[3], (E, I, H), jnp.float32) * s, 'gate_w': jax.random.normal(ks[4], (H, ISH), jnp.float32) * s, 'up_w': jax.random.normal(ks[5], (H, ISH), jnp.float32) * s, 'down_w': jax.random.normal(ks[6], (ISH, H), jnp.float32) * s}
    _L1_ffn_all = _L1_ffn_setup()
    _L1_ffn_in = {k: v for k, v in _L1_ffn_all.items() if k in ('w_router', 'fc1_w', 'fc2_w', 'gate_w', 'up_w', 'down_w')}
    del _L1_ffn_all

    def _L2_xattn_setup():
        import jax, jax.numpy as jnp
        import numpy as np
        D_MODEL = 128
        NHEAD = 16
        D_K = D_MODEL // NHEAD
        key = jax.random.key(seed)
        ks = jax.random.split(key, 11)
        B, S = (2, 256)
        scale = 1.0 / np.sqrt(D_MODEL)
        inp = {'q': jax.random.normal(ks[0], (B, S, D_MODEL), jnp.float32), 'k': jax.random.normal(ks[1], (B, S, D_MODEL), jnp.float32), 'v': jax.random.normal(ks[2], (B, S, D_MODEL), jnp.float32), 'Wq': jax.random.normal(ks[3], (D_MODEL, D_MODEL), jnp.float32) * scale, 'bq': jnp.zeros((D_MODEL,), jnp.float32), 'Wk': jax.random.normal(ks[4], (D_MODEL, D_MODEL), jnp.float32) * scale, 'bk': jnp.zeros((D_MODEL,), jnp.float32), 'Wv': jax.random.normal(ks[5], (D_MODEL, D_MODEL), jnp.float32) * scale, 'bv': jnp.zeros((D_MODEL,), jnp.float32), 'Wo': jax.random.normal(ks[6], (D_MODEL, D_MODEL), jnp.float32) * scale, 'bo': jnp.zeros((D_MODEL,), jnp.float32)}
        return inp
    _L2_xattn_all = _L2_xattn_setup()
    _L2_xattn_in = {k: v for k, v in _L2_xattn_all.items() if k in ('Wq', 'bq', 'Wk', 'bk', 'Wv', 'bv', 'Wo', 'bo')}
    del _L2_xattn_all

    def _L2_ffn_setup():
        import jax, jax.numpy as jnp
        import numpy as np
        D_MODEL = 128
        D_FF = 512
        N_EXP = 8
        TOP_K = 2

        def _gelu(x):
            return jax.nn.gelu(x, approximate=False)
        key = jax.random.key(seed)
        ks = jax.random.split(key, 12)
        s = 0.02
        return {'x': jax.random.normal(ks[0], (4, 256, D_MODEL), dtype=jnp.float32), 'shared_w1': jax.random.normal(ks[1], (D_MODEL, D_FF), dtype=jnp.float32) * s, 'shared_b1': jnp.zeros((D_FF,), jnp.float32), 'shared_w2': jax.random.normal(ks[2], (D_FF, D_MODEL), dtype=jnp.float32) * s, 'shared_b2': jnp.zeros((D_MODEL,), jnp.float32), 'router_w': jax.random.normal(ks[3], (D_MODEL, N_EXP), dtype=jnp.float32) * s, 'router_b': jnp.zeros((N_EXP,), jnp.float32), 'exp_w1': jax.random.normal(ks[4], (N_EXP, D_MODEL, D_FF), dtype=jnp.float32) * s, 'exp_b1': jnp.zeros((N_EXP, D_FF), jnp.float32), 'exp_w2': jax.random.normal(ks[5], (N_EXP, D_FF, D_MODEL), dtype=jnp.float32) * s, 'exp_b2': jnp.zeros((N_EXP, D_MODEL), jnp.float32)}
    _L2_ffn_all = _L2_ffn_setup()
    _L2_ffn_in = {k: v for k, v in _L2_ffn_all.items() if k in ('shared_w1', 'shared_b1', 'shared_w2', 'shared_b2', 'router_w', 'router_b', 'exp_w1', 'exp_b1', 'exp_w2', 'exp_b2')}
    del _L2_ffn_all

    def _L3_xattn_setup():
        import jax, jax.numpy as jnp
        import numpy as np
        import math
        D_MODEL = 128
        N_HEADS = 16
        HEAD_DIM = D_MODEL // N_HEADS
        TOP_K = 32
        SCALE = math.sqrt(HEAD_DIM)

        def _split_heads(t, n):
            B, L, _ = t.shape
            return t.reshape(B, L, N_HEADS, HEAD_DIM).transpose(0, 2, 1, 3)
        key = jax.random.key(seed)
        ks = jax.random.split(key, 12)
        B, S, N = (2, 256, 256)
        std = 1.0 / math.sqrt(D_MODEL)
        inp = {'x': jax.random.normal(ks[0], (B, S, D_MODEL), dtype=jnp.float32), 'knowledge_embeddings': jax.random.normal(ks[1], (B, N, D_MODEL), dtype=jnp.float32), 'Wq': jax.random.normal(ks[2], (D_MODEL, D_MODEL), dtype=jnp.float32) * std, 'bq': jnp.zeros((D_MODEL,), dtype=jnp.float32), 'Wk': jax.random.normal(ks[3], (D_MODEL, D_MODEL), dtype=jnp.float32) * std, 'bk': jnp.zeros((D_MODEL,), dtype=jnp.float32), 'Wv': jax.random.normal(ks[4], (D_MODEL, D_MODEL), dtype=jnp.float32) * std, 'bv': jnp.zeros((D_MODEL,), dtype=jnp.float32), 'Wo': jax.random.normal(ks[5], (D_MODEL, D_MODEL), dtype=jnp.float32) * std, 'bo': jnp.zeros((D_MODEL,), dtype=jnp.float32)}
        return inp
    _L3_xattn_all = _L3_xattn_setup()
    _L3_xattn_in = {k: v for k, v in _L3_xattn_all.items() if k in ('Wq', 'bq', 'Wk', 'bk', 'Wv', 'bv', 'Wo', 'bo')}
    del _L3_xattn_all

    def _L3_ffn_setup():
        import jax, jax.numpy as jnp
        import numpy as np
        B, T, C, H, E, MIN_E = (4, 256, 128, 128, 16, 2)
        IS_CAUSAL = False

        def _forward(hidden_states, sim_matrix, gates, q_proj, k_proj, v_proj, o_proj):
            b, t, c = hidden_states.shape
            n = b * t
            x = hidden_states.reshape(n, c)
            xn = x / jnp.maximum(jnp.linalg.norm(x, axis=-1, keepdims=True), 1e-12)
            sn = sim_matrix / jnp.maximum(jnp.linalg.norm(sim_matrix, axis=0, keepdims=True), 1e-12)
            logits = xn @ sn - jax.nn.sigmoid(gates)
            gated = jax.nn.relu(logits)
            hard = (gated > 0).astype(gated.dtype)
            mask = gated + jax.lax.stop_gradient(hard - gated)
            inactive = jnp.sum(hard, axis=1) == 0
            _, fb_idx = jax.lax.top_k(logits, MIN_E)
            fb = jnp.zeros((n, logits.shape[1]), gated.dtype).at[jnp.arange(n)[:, None], fb_idx].set(1.0)
            put = jax.lax.stop_gradient(inactive[:, None].astype(gated.dtype) * fb)
            mask = mask * (1.0 - put) + put
            masked = jnp.where(mask > 0, gated, -jnp.inf)
            w = jax.nn.softmax(masked, axis=-1)

            def moe_proj(p):
                y = jnp.einsum('nc,ech->neh', x, p)
                return jnp.einsum('ne,neh->nh', w, y)
            q = moe_proj(q_proj).reshape(b, t, -1)
            k = moe_proj(k_proj).reshape(b, t, -1)
            v = moe_proj(v_proj).reshape(b, t, -1)
            h = q.shape[-1]
            scores = jnp.einsum('bth,bsh->bts', q, k) / jnp.sqrt(jnp.asarray(h, q.dtype))
            if IS_CAUSAL and t > 1:
                causal = jnp.tril(jnp.ones((t, t), bool))
                scores = jnp.where(causal[None], scores, -jnp.inf)
            attn = jax.nn.softmax(scores, axis=-1)
            o = jnp.einsum('bts,bsh->bth', attn, v).reshape(n, h)
            z = jnp.einsum('ne,nh->enh', w, o)
            out = jnp.einsum('enh,ehc->nc', z, o_proj)
            return out.reshape(b, t, c)
        key = jax.random.key(seed)
        ks = jax.random.split(key, 6)
        lim_qkv = float(np.sqrt(6.0 / (C + H)))
        inp = {'hidden_states': jax.random.normal(ks[0], (B, T, C), jnp.float32), 'sim_matrix': jax.random.normal(ks[1], (C, E), jnp.float32), 'gates': jnp.zeros((E,), jnp.float32), 'q_proj': jax.random.uniform(ks[2], (E, C, H), jnp.float32, -lim_qkv, lim_qkv), 'k_proj': jax.random.uniform(ks[3], (E, C, H), jnp.float32, -lim_qkv, lim_qkv), 'v_proj': jax.random.uniform(ks[4], (E, C, H), jnp.float32, -lim_qkv, lim_qkv), 'o_proj': jax.random.uniform(ks[5], (E, H, C), jnp.float32, -lim_qkv, lim_qkv)}
        return inp
    _L3_ffn_all = _L3_ffn_setup()
    _L3_ffn_in = {k: v for k, v in _L3_ffn_all.items() if k in ('sim_matrix', 'gates', 'q_proj', 'k_proj', 'v_proj', 'o_proj')}
    del _L3_ffn_all
    return {'x': x, 'ctx_1024': ctx_1024, 'g_xattn': g_xattn, 'g_ffn': g_ffn, 'L0_xattn_random_features': _L0_xattn_in['random_features'], 'L0_ffn_W_qkv': _L0_ffn_in['W_qkv'], 'L0_ffn_b_qkv': _L0_ffn_in['b_qkv'], 'L0_ffn_W_gate': _L0_ffn_in['W_gate'], 'L0_ffn_b_gate': _L0_ffn_in['b_gate'], 'L0_ffn_W_experts': _L0_ffn_in['W_experts'], 'L0_ffn_b_experts': _L0_ffn_in['b_experts'], 'L1_xattn_Wq': _L1_xattn_in['Wq'], 'L1_xattn_Wkv': _L1_xattn_in['Wkv'], 'L1_xattn_Wout': _L1_xattn_in['Wout'], 'L1_xattn_bout': _L1_xattn_in['bout'], 'L1_ffn_w_router': _L1_ffn_in['w_router'], 'L1_ffn_fc1_w': _L1_ffn_in['fc1_w'], 'L1_ffn_fc2_w': _L1_ffn_in['fc2_w'], 'L1_ffn_gate_w': _L1_ffn_in['gate_w'], 'L1_ffn_up_w': _L1_ffn_in['up_w'], 'L1_ffn_down_w': _L1_ffn_in['down_w'], 'L2_xattn_Wq': _L2_xattn_in['Wq'], 'L2_xattn_bq': _L2_xattn_in['bq'], 'L2_xattn_Wk': _L2_xattn_in['Wk'], 'L2_xattn_bk': _L2_xattn_in['bk'], 'L2_xattn_Wv': _L2_xattn_in['Wv'], 'L2_xattn_bv': _L2_xattn_in['bv'], 'L2_xattn_Wo': _L2_xattn_in['Wo'], 'L2_xattn_bo': _L2_xattn_in['bo'], 'L2_ffn_shared_w1': _L2_ffn_in['shared_w1'], 'L2_ffn_shared_b1': _L2_ffn_in['shared_b1'], 'L2_ffn_shared_w2': _L2_ffn_in['shared_w2'], 'L2_ffn_shared_b2': _L2_ffn_in['shared_b2'], 'L2_ffn_router_w': _L2_ffn_in['router_w'], 'L2_ffn_router_b': _L2_ffn_in['router_b'], 'L2_ffn_exp_w1': _L2_ffn_in['exp_w1'], 'L2_ffn_exp_b1': _L2_ffn_in['exp_b1'], 'L2_ffn_exp_w2': _L2_ffn_in['exp_w2'], 'L2_ffn_exp_b2': _L2_ffn_in['exp_b2'], 'L3_xattn_Wq': _L3_xattn_in['Wq'], 'L3_xattn_bq': _L3_xattn_in['bq'], 'L3_xattn_Wk': _L3_xattn_in['Wk'], 'L3_xattn_bk': _L3_xattn_in['bk'], 'L3_xattn_Wv': _L3_xattn_in['Wv'], 'L3_xattn_bv': _L3_xattn_in['bv'], 'L3_xattn_Wo': _L3_xattn_in['Wo'], 'L3_xattn_bo': _L3_xattn_in['bo'], 'L3_ffn_sim_matrix': _L3_ffn_in['sim_matrix'], 'L3_ffn_gates': _L3_ffn_in['gates'], 'L3_ffn_q_proj': _L3_ffn_in['q_proj'], 'L3_ffn_k_proj': _L3_ffn_in['k_proj'], 'L3_ffn_v_proj': _L3_ffn_in['v_proj'], 'L3_ffn_o_proj': _L3_ffn_in['o_proj']}

def reference(x, ctx_1024, g_xattn, g_ffn, L0_xattn_random_features, L0_ffn_W_qkv, L0_ffn_b_qkv, L0_ffn_W_gate, L0_ffn_b_gate, L0_ffn_W_experts, L0_ffn_b_experts, L1_xattn_Wq, L1_xattn_Wkv, L1_xattn_Wout, L1_xattn_bout, L1_ffn_w_router, L1_ffn_fc1_w, L1_ffn_fc2_w, L1_ffn_gate_w, L1_ffn_up_w, L1_ffn_down_w, L2_xattn_Wq, L2_xattn_bq, L2_xattn_Wk, L2_xattn_bk, L2_xattn_Wv, L2_xattn_bv, L2_xattn_Wo, L2_xattn_bo, L2_ffn_shared_w1, L2_ffn_shared_b1, L2_ffn_shared_w2, L2_ffn_shared_b2, L2_ffn_router_w, L2_ffn_router_b, L2_ffn_exp_w1, L2_ffn_exp_b1, L2_ffn_exp_w2, L2_ffn_exp_b2, L3_xattn_Wq, L3_xattn_bq, L3_xattn_Wk, L3_xattn_bk, L3_xattn_Wv, L3_xattn_bv, L3_xattn_Wo, L3_xattn_bo, L3_ffn_sim_matrix, L3_ffn_gates, L3_ffn_q_proj, L3_ffn_k_proj, L3_ffn_v_proj, L3_ffn_o_proj):
    import jax
    import jax.numpy as jnp

    def _L0_xattn_ref(query, key, value, random_features):
        import jax, jax.numpy as jnp
        import numpy as np
        D_MODEL = 128
        NUM_HEADS = 16
        KERNEL_EPS = 0.0001
        NORM_STAB = 1e-06

        def _performer_forward(query, key, value, random_features):
            B, L, dm = query.shape
            h = NUM_HEADS
            d = dm // h
            m = random_features.shape[1]

            def split_heads(x):
                return x.reshape(B, L, h, d).transpose(0, 2, 1, 3)
            q, k, v = (split_heads(query), split_heads(key), split_heads(value))
            scale = dm ** (-0.25)
            q = q * scale
            k = k * scale
            proj_q = jnp.einsum('bhld,dm->bhlm', q, random_features)
            proj_k = jnp.einsum('bhld,dm->bhlm', k, random_features)
            h_q = -0.5 * jnp.sum(q * q, axis=-1, keepdims=True)
            h_k = -0.5 * jnp.sum(k * k, axis=-1, keepdims=True)
            q_stab = h_q
            k_stab = jnp.max(h_k)
            q_kernel = jnp.exp(h_q + (proj_q - q_stab))
            k_kernel = jnp.exp(h_k + (proj_k - k_stab))
            nc = m ** (-0.5)
            q_prime = nc * (q_kernel + KERNEL_EPS)
            k_prime = nc * (k_kernel + KERNEL_EPS)
            qp = q_prime.transpose(2, 0, 1, 3)
            kp = k_prime.transpose(2, 0, 1, 3)
            vp = v.transpose(2, 0, 1, 3)

            def step(carry, inp):
                S, Z = carry
                qt, kt, vt = inp
                S = S + kt[..., :, None] * vt[..., None, :]
                Z = Z + kt
                num = jnp.einsum('bhm,bhmd->bhd', qt, S)
                den = jnp.einsum('bhm,bhm->bh', qt, Z)
                return ((S, Z), (num, den))
            S0 = jnp.zeros((B, h, m, d), q_prime.dtype)
            Z0 = jnp.zeros((B, h, m), q_prime.dtype)
            _, (nums, dens) = jax.lax.scan(step, (S0, Z0), (qp, kp, vp))
            nums = nums.transpose(1, 2, 0, 3)
            dens = dens.transpose(1, 2, 0)[..., None]
            extreme = (jnp.abs(dens) <= NORM_STAB).astype(dens.dtype)
            dens = dens + 2.0 * NORM_STAB * extreme
            out = nums / dens
            return out.transpose(0, 2, 1, 3).reshape(B, L, dm)
        return _performer_forward(query, key, value, random_features)

    def _L0_ffn_ref(x, W_qkv, b_qkv, W_gate, b_gate, W_experts, b_experts):
        import jax, jax.numpy as jnp
        import numpy as np
        NUM_HEADS = 16
        TOP_K = 2
        B, S, D = x.shape
        H = NUM_HEADS
        hd = D // H
        E = W_gate.shape[-1]
        qkv = (x @ W_qkv + b_qkv).reshape(B, S, 3, H, hd)
        q, k, v = (qkv[:, :, 0], qkv[:, :, 1], qkv[:, :, 2])
        attn = jnp.einsum('bqhd,bkhd->bhqk', q, k) / jnp.sqrt(jnp.asarray(hd, x.dtype))
        attn = jax.nn.softmax(attn, axis=-1)
        attn_out = jnp.einsum('bhqk,bkhd->bqhd', attn, v).reshape(B, S, D)
        gate = jax.nn.softmax(x @ W_gate + b_gate, axis=-1)
        top_g, top_i = jax.lax.top_k(gate, TOP_K)
        combine = jnp.sum(jax.nn.one_hot(top_i, E, dtype=x.dtype) * top_g[..., None], axis=2)
        expert_out = jnp.einsum('bsd,edf->bsef', x, W_experts) + b_experts
        moe_out = jnp.einsum('bsef,bse->bsf', expert_out, combine)
        return attn_out + moe_out

    def _L1_xattn_ref(x, context, Wq, Wkv, Wout, bout, topk):
        import jax, jax.numpy as jnp
        import numpy as np
        HEADS = 8
        DIM_HEAD = 64
        B, Nq, _ = x.shape
        Nk = context.shape[1]
        H, D = (HEADS, DIM_HEAD)
        scale = D ** (-0.5)
        q = (x @ Wq).reshape(B, Nq, H, D).transpose(0, 2, 1, 3)
        kv = context @ Wkv
        k, v = jnp.split(kv, 2, axis=-1)
        k = k.reshape(B, Nk, H, D).transpose(0, 2, 1, 3)
        v = v.reshape(B, Nk, H, D).transpose(0, 2, 1, 3)
        sim = jnp.einsum('bhid,bhjd->bhij', q, k) * scale
        k_eff = min(int(topk), Nk)
        _, idx = jax.lax.top_k(sim, k_eff)
        keep = jnp.zeros(sim.shape, dtype=bool)
        bi = jnp.arange(B)[:, None, None, None]
        hi = jnp.arange(H)[None, :, None, None]
        qi = jnp.arange(Nq)[None, None, :, None]
        keep = keep.at[bi, hi, qi, idx].set(True)
        max_neg = -jnp.finfo(sim.dtype).max
        sim = jnp.where(keep, sim, max_neg)
        attn = jax.nn.softmax(sim, axis=-1)
        out = jnp.einsum('bhij,bhjd->bhid', attn, v)
        out = out.transpose(0, 2, 1, 3).reshape(B, Nq, H * D)
        return out @ Wout + bout

    def _L1_ffn_ref(hidden_states, w_router, fc1_w, fc2_w, gate_w, up_w, down_w):
        import jax, jax.numpy as jnp
        import numpy as np
        E = 8
        TOPK = 2
        H = 128
        I = 128
        ISH = I * 2
        B, S = (2, 128)
        orig_shape = hidden_states.shape
        x = hidden_states.reshape(-1, orig_shape[-1])
        logits = x @ w_router
        top_logits, top_idx = jax.lax.top_k(logits, TOPK)
        scores = jax.nn.softmax(top_logits, axis=-1)
        flat_idx = top_idx.reshape(-1)
        sorted_idx = jnp.argsort(flat_idx)
        permuted = x[sorted_idx // TOPK]
        eid = flat_idx[sorted_idx]
        out_perm = jnp.zeros((permuted.shape[0], orig_shape[-1]), x.dtype)
        for e in range(E):
            m = (eid == e).astype(x.dtype)[:, None]
            h1 = permuted * m @ fc1_w[e]
            proj, gate = jnp.split(h1, 2, axis=-1)
            out_perm = out_perm + jax.nn.silu(proj) * gate @ fc2_w[e]
        unperm = jnp.zeros_like(out_perm).at[sorted_idx].set(out_perm)
        moe_out = (unperm.reshape(-1, TOPK, orig_shape[-1]) * scores[:, :, None]).sum(axis=1)
        moe_out = moe_out.reshape(orig_shape)
        shared = jax.nn.silu(hidden_states @ gate_w) * (hidden_states @ up_w) @ down_w
        return moe_out + shared

    def _L2_xattn_ref(q, k, v, Wq, bq, Wk, bk, Wv, bv, Wo, bo):
        import jax, jax.numpy as jnp
        import numpy as np
        D_MODEL = 128
        NHEAD = 16
        D_K = D_MODEL // NHEAD
        B, S, _ = q.shape

        def proj(x, W, b):
            y = jnp.einsum('bsd,ed->bse', x, W) + b
            return y.reshape(B, -1, NHEAD, D_K).transpose(0, 2, 1, 3)
        qh = proj(q, Wq, bq)
        kh = proj(k, Wk, bk)
        vh = proj(v, Wv, bv)
        scores = jnp.einsum('bhqd,bhkd->bhqk', qh, kh) / jnp.sqrt(jnp.asarray(D_K, qh.dtype))
        attn = jax.nn.softmax(scores, axis=-1)
        out = jnp.einsum('bhqk,bhkd->bhqd', attn, vh)
        out = out.transpose(0, 2, 1, 3).reshape(B, S, D_MODEL)
        return jnp.einsum('bsd,ed->bse', out, Wo) + bo

    def _L2_ffn_ref(x, shared_w1, shared_b1, shared_w2, shared_b2, router_w, router_b, exp_w1, exp_b1, exp_w2, exp_b2):
        import jax, jax.numpy as jnp
        import numpy as np
        D_MODEL = 128
        D_FF = 512
        N_EXP = 8
        TOP_K = 2

        def _gelu(x):
            return jax.nn.gelu(x, approximate=False)
        leading = x.shape[:-1]
        d = x.shape[-1]
        xf = x.reshape(-1, d)
        T = xf.shape[0]
        h_shared = _gelu(xf @ shared_w1 + shared_b1) @ shared_w2 + shared_b2
        logits = xf @ router_w + router_b
        routing = jax.nn.softmax(logits, axis=-1)
        sel_w, sel_idx = jax.lax.top_k(routing, TOP_K)
        sel_w = sel_w / (jnp.sum(sel_w, axis=-1, keepdims=True) + 1e-09)
        combine = jnp.zeros((T, N_EXP), routing.dtype)
        combine = combine.at[jnp.arange(T)[:, None], sel_idx].add(sel_w)
        residual = jnp.zeros_like(xf)
        for e in range(N_EXP):
            h = _gelu(xf @ exp_w1[e] + exp_b1[e])
            y = h @ exp_w2[e] + exp_b2[e]
            residual = residual + combine[:, e:e + 1] * y
        out = h_shared + residual
        return out.reshape(*leading, d)

    def _L3_xattn_ref(x, knowledge_embeddings, Wq, bq, Wk, bk, Wv, bv, Wo, bo):
        import jax, jax.numpy as jnp
        import numpy as np
        import math
        D_MODEL = 128
        N_HEADS = 16
        HEAD_DIM = D_MODEL // N_HEADS
        TOP_K = 32
        SCALE = math.sqrt(HEAD_DIM)

        def _split_heads(t, n):
            B, L, _ = t.shape
            return t.reshape(B, L, N_HEADS, HEAD_DIM).transpose(0, 2, 1, 3)
        B, S, _ = x.shape
        N = knowledge_embeddings.shape[1]
        Q = _split_heads(x @ Wq.T + bq, N_HEADS)
        K = _split_heads(knowledge_embeddings @ Wk.T + bk, N_HEADS)
        V = _split_heads(knowledge_embeddings @ Wv.T + bv, N_HEADS)
        scores = jnp.einsum('bhsd,bhnd->bhsn', Q, K) / SCALE
        k = min(TOP_K, N)
        topk_scores, topk_indices = jax.lax.top_k(scores, k)
        sparse_weights = jax.nn.softmax(topk_scores, axis=-1)
        sel_V = jnp.take_along_axis(V[:, :, None, :, :], topk_indices[..., None], axis=3)
        context = jnp.einsum('bhsk,bhskd->bhsd', sparse_weights, sel_V)
        context = context.transpose(0, 2, 1, 3).reshape(B, S, D_MODEL)
        return context @ Wo.T + bo

    def _L3_ffn_ref(hidden_states, sim_matrix, gates, q_proj, k_proj, v_proj, o_proj):
        import jax, jax.numpy as jnp
        import numpy as np
        B, T, C, H, E, MIN_E = (4, 256, 128, 128, 16, 2)
        IS_CAUSAL = False

        def _forward(hidden_states, sim_matrix, gates, q_proj, k_proj, v_proj, o_proj):
            b, t, c = hidden_states.shape
            n = b * t
            x = hidden_states.reshape(n, c)
            xn = x / jnp.maximum(jnp.linalg.norm(x, axis=-1, keepdims=True), 1e-12)
            sn = sim_matrix / jnp.maximum(jnp.linalg.norm(sim_matrix, axis=0, keepdims=True), 1e-12)
            logits = xn @ sn - jax.nn.sigmoid(gates)
            gated = jax.nn.relu(logits)
            hard = (gated > 0).astype(gated.dtype)
            mask = gated + jax.lax.stop_gradient(hard - gated)
            inactive = jnp.sum(hard, axis=1) == 0
            _, fb_idx = jax.lax.top_k(logits, MIN_E)
            fb = jnp.zeros((n, logits.shape[1]), gated.dtype).at[jnp.arange(n)[:, None], fb_idx].set(1.0)
            put = jax.lax.stop_gradient(inactive[:, None].astype(gated.dtype) * fb)
            mask = mask * (1.0 - put) + put
            masked = jnp.where(mask > 0, gated, -jnp.inf)
            w = jax.nn.softmax(masked, axis=-1)

            def moe_proj(p):
                y = jnp.einsum('nc,ech->neh', x, p)
                return jnp.einsum('ne,neh->nh', w, y)
            q = moe_proj(q_proj).reshape(b, t, -1)
            k = moe_proj(k_proj).reshape(b, t, -1)
            v = moe_proj(v_proj).reshape(b, t, -1)
            h = q.shape[-1]
            scores = jnp.einsum('bth,bsh->bts', q, k) / jnp.sqrt(jnp.asarray(h, q.dtype))
            if IS_CAUSAL and t > 1:
                causal = jnp.tril(jnp.ones((t, t), bool))
                scores = jnp.where(causal[None], scores, -jnp.inf)
            attn = jax.nn.softmax(scores, axis=-1)
            o = jnp.einsum('bts,bsh->bth', attn, v).reshape(n, h)
            z = jnp.einsum('ne,nh->enh', w, o)
            out = jnp.einsum('enh,ehc->nc', z, o_proj)
            return out.reshape(b, t, c)
        return _forward(hidden_states, sim_matrix, gates, q_proj, k_proj, v_proj, o_proj)
    x = x + jnp.tanh(g_xattn[0]) * _L0_xattn_ref(_layernorm(x, axis=-1), ctx_1024, ctx_1024, L0_xattn_random_features)
    x = x + jnp.tanh(g_ffn[0]) * _L0_ffn_ref(_layernorm(x, axis=-1), L0_ffn_W_qkv, L0_ffn_b_qkv, L0_ffn_W_gate, L0_ffn_b_gate, L0_ffn_W_experts, L0_ffn_b_experts)
    x = x + jnp.tanh(g_xattn[1]) * _L1_xattn_ref(_layernorm(x, axis=-1), ctx_1024, L1_xattn_Wq, L1_xattn_Wkv, L1_xattn_Wout, L1_xattn_bout, 64)
    x = x + jnp.tanh(g_ffn[1]) * _L1_ffn_ref(_layernorm(x, axis=-1), L1_ffn_w_router, L1_ffn_fc1_w, L1_ffn_fc2_w, L1_ffn_gate_w, L1_ffn_up_w, L1_ffn_down_w)
    x = x + jnp.tanh(g_xattn[2]) * _L2_xattn_ref(_layernorm(x, axis=-1), ctx_1024, ctx_1024, L2_xattn_Wq, L2_xattn_bq, L2_xattn_Wk, L2_xattn_bk, L2_xattn_Wv, L2_xattn_bv, L2_xattn_Wo, L2_xattn_bo)
    x = x + jnp.tanh(g_ffn[2]) * _L2_ffn_ref(_layernorm(x, axis=-1), L2_ffn_shared_w1, L2_ffn_shared_b1, L2_ffn_shared_w2, L2_ffn_shared_b2, L2_ffn_router_w, L2_ffn_router_b, L2_ffn_exp_w1, L2_ffn_exp_b1, L2_ffn_exp_w2, L2_ffn_exp_b2)
    x = x + jnp.tanh(g_xattn[3]) * _L3_xattn_ref(_layernorm(x, axis=-1), ctx_1024, L3_xattn_Wq, L3_xattn_bq, L3_xattn_Wk, L3_xattn_bk, L3_xattn_Wv, L3_xattn_bv, L3_xattn_Wo, L3_xattn_bo)
    x = x + jnp.tanh(g_ffn[3]) * _L3_ffn_ref(_layernorm(x, axis=-1), L3_ffn_sim_matrix, L3_ffn_gates, L3_ffn_q_proj, L3_ffn_k_proj, L3_ffn_v_proj, L3_ffn_o_proj)
    return x

_drawn_inputs = setup_inputs


def setup_inputs(seed=0):
    import zlib

    import numpy as np

    out = dict(_drawn_inputs(seed))
    spreads = {'L0_ffn_b_qkv': (0.0, 0.1),
     'L0_ffn_b_gate': (0.0, 0.333),
     'L0_ffn_b_experts': (0.0, 0.324),
     'L2_xattn_bq': (0.0, 0.321),
     'L2_xattn_bk': (0.0, 0.8),
     'L2_xattn_bv': (0.0, 0.1),
     'L2_xattn_bo': (0.0, 0.1),
     'L2_ffn_shared_b1': (0.0, 0.325),
     'L2_ffn_shared_b2': (0.0, 0.1),
     'L2_ffn_router_b': (0.0, 0.1),
     'L2_ffn_exp_b1': (0.0, 0.393),
     'L2_ffn_exp_b2': (0.0, 0.1),
     'L3_xattn_bq': (0.0, 0.1),
     'L3_xattn_bk': (0.0, 0.8),
     'L3_xattn_bv': (0.0, 0.1),
     'L3_xattn_bo': (0.0, 0.1),
     'L3_ffn_gates': (0.0, 0.1)}
    factors = {'g_ffn': 8.0,
     'L1_ffn_w_router': 6.492,
     'L1_ffn_fc1_w': 6.278,
     'L1_ffn_fc2_w': 6.398,
     'L1_ffn_gate_w': 4.071,
     'L1_ffn_up_w': 4.175,
     'L1_ffn_down_w': 4.366,
     'L3_ffn_q_proj': 3.349,
     'L3_ffn_k_proj': 3.401}
    for name, (base, spread) in spreads.items():
        noise = np.random.default_rng([zlib.crc32(name.encode()), seed]).standard_normal(out[name].shape)
        drawn = base * np.exp(spread * noise) if base else spread * noise
        out[name] = jnp.asarray(drawn.astype(out[name].dtype))
    for name, factor in factors.items():
        out[name] = (out[name] * factor).astype(out[name].dtype)
    return out
```

```python
from contextlib import ExitStack

import numpy as np
import concourse.bass as bass
from concourse import mybir

F32 = mybir.dt.float32
ACT = mybir.ActivationFunctionType
ALU = mybir.AluOpType
AX = mybir.AxisListType

NB, T, D = 8, 256, 128
P = 128
NT = T // P
H, HD = 16, 8
PAD = 32
HG = P // PAD
NG = H // HG
M_RF = 32
H1, HD1 = 8, 64
E8, E16 = 8, 16
FF2 = 4
SENT, GONE = -1.0e38, -3.0e38
RF_SCALE = float(D) ** -0.25

CONST = [("ident", 128), ("tri", 128), ("ones", 128), ("hsum", NG * 128)]
PACK1 = [("rf", NG * 128), ("wq0", NG * 128), ("wk0", NG * 128), ("wv0", 128), ("gate0", E8), ("exp0", E8 * D),
         ("bq0", NG), ("bk0", NG), ("bias0", D)]
PACK2 = [("wq1", H1 * HD1), ("wk1", H1 * HD1), ("wv1", H1 * HD1), ("wo1", 4 * D)]
PACK3 = [("router1", E8), ("fc1", E8 * 2 * D), ("fc2", E8 * D), ("gate_w", 2 * D), ("up_w", 2 * D), ("down_w", 2 * D),
         ("wq2", NG * 128), ("wk2", NG * 128), ("wv2", 128), ("wo2", 128), ("bq2", NG), ("bk2", NG),
         ("router2", E8), ("b1", (E8 + 1) * FF2), ("bias2", D)]
PACK3W = [("w1", (E8 + 1) * FF2 * 128), ("w2", (E8 + 1) * FF2 * 128)]
PACK4 = [("wq3", NG * 128), ("wk3", NG * 128), ("wv3", 128), ("wo3", 128), ("bq3", NG), ("bk3", NG), ("sim", E16)]
PACK4W = [("qp", E16 * D), ("kp", E16 * D), ("vp", E16 * D), ("op", E16 * D)]
ROWS = [("bgate0", E8), ("br2", E8), ("gates", E16), ("g", 8)]
BELOW = {"bias0": ["bv0", "bout1", "bv2"], "bias2": ["bo2", "bv3", "bo3"]}
PACKS = [("const", CONST), ("pack1", PACK1), ("pack2", PACK2), ("pack3", PACK3), ("pack3w", PACK3W),
         ("pack4", PACK4), ("pack4w", PACK4W)]


def cols(pack):
    return sum(n for _, n in pack)


class Chain:

    def __init__(self, sem):
        self.sem, self.n = sem, 0

    def link(self, eng, ins):
        self.n += 1
        ins.then_inc(self.sem, 1)
        eng.wait_ge(self.sem, self.n)


class Shared:

    def __init__(self, nc, ctx):
        self.nc, self.ctx = nc, ctx
        self.sems, self.bufs, self.w = {}, {}, {}
        self.first = self.last = None
        self.psum = [ctx.enter_context(nc.psum_tensor(f"bank{i}", [P, 512], F32)) for i in range(8)]

    def sb(self, name, shape):
        if name not in self.bufs:
            self.bufs[name] = self.ctx.enter_context(self.nc.sbuf_tensor(name, shape, F32))
        return self.bufs[name]

    def one(self, name):
        r = max((32 * (names.index(name) + 1) for names in BELOW.values() if name in names), default=0)
        return self.w["ones"][r:r + 1, :]

    def lasting_sem(self, name):
        return self.ctx.enter_context(self.nc.semaphore(name))

    def sem(self, name):
        if name not in self.sems:
            s = self.ctx.enter_context(self.nc.semaphore(name))
            self.first = s.num if self.first is None else min(self.first, s.num)
            self.last = s.num if self.last is None else max(self.last, s.num)
            self.sems[name] = s
        return self.sems[name]


class Workspace:

    def __init__(self, k, side):
        self.whole = k.sb(f"work{side}", [P, (4 if side == "Q" else 3) * NG, T])
        self.kT, self.qT, self.oT = (self.whole[:, i * NG:(i + 1) * NG, :] for i in range(3))
        if side == "Q":
            self.work = self.whole[:, 3 * NG:, :].rearrange("p (u j) t -> p u j t", j=NT)
        self.v = k.sb(f"att_v{side}", [P, NT, H, PAD])
        self.p, self.pT = k.sb(f"att_p{side}", [P, 2, NT, T])[:, :, :, :], k.sb(f"att_pT{side}", [P, 2, NT, T])[:, :, :, :]


class Units:

    def units(self, count, rounds, tail):
        self.count, self.rounds = count, rounds
        self.steps = 1 + count * rounds + tail + 1

    def at(self, s, lag, r):
        u, rest = divmod(s - 1 - r, self.rounds)
        return u - lag if s >= 1 and rest == 0 and 0 <= u - lag < self.count else -1

    def final(self, s):
        return s == self.steps - 1


class TopSelect(Units):
    OPS = 4

    def top_buffers(self, k, buf, n):
        self.work, self.rest = buf.work, k.sb("top_rest", [P, NT, T])
        self.lead, self.eight = k.sb("top_lead", [P, 2, NT, 8]), k.sb("top_eight", [P, NT, 8])
        self.top, self.rest_done = k.sem(n + "top"), k.sem(n + "rest")
        self.topn = 0

    def top_count(self, u, r):
        return self.OPS * (u * self.rounds + r + 1)

    def select(self, dve, u, r):
        nc, sc = self.k.nc, self.banks[u % 2]
        if r == 0:
            dve.wait_ge(self.scores, u + 1)
            if u >= 2:
                dve.wait_ge(self.rest_done, u - 1)
        for replace in range(2):
            for j in range(NT):
                if self.topn >= 2:
                    dve.wait_ge(self.top, self.topn - 1)
                src = sc[:, j * T:(j + 1) * T] if r == 0 else self.work[:, u % 2, j, :]
                eight = self.lead[:, u % 2, j, :] if r == 0 else self.eight[:, j, :]
                if replace:
                    ins = nc.vector.match_replace(self.work[:, u % 2, j, :], eight, src, GONE)
                else:
                    ins = nc.vector.max(eight, src)
                ins.then_inc(self.top, 1)
                self.topn += 1

    def negative_max(self, pool, u):
        pool.wait_ge(self.top, self.top_count(u, 0) - NT)
        self.k.nc.gpsimd.tensor_scalar(self.nmax[:, u, :], self.lead[:, u % 2, :, 0], -1.0, 1.0, ALU.mult,
                                       ALU.mult).then_inc(self.max_ready, 1)

    def exp_scores(self, act, u):
        act.wait_ge(self.max_ready, u + 1)
        if self.topk:
            act.wait_ge(self.top, self.top_count(u, 0))
        if u >= 2:
            act.wait_ge(self.pT_ps, u - 1)
        for j in range(NT):
            e = self.k.nc.scalar.activation(self.p[:, u % 2, j, :], self.banks[u % 2][:, j * T:(j + 1) * T], ACT.Exp,
                                            bias=self.nmax[:, u, j:j + 1])
        e.then_inc(self.exp_done, 1)

    def exp_rest(self, act, u):
        act.wait_ge(self.top, self.top_count(u, self.rounds - 1))
        if u >= 1:
            act.wait_ge(self.p_ready, u)
        for j in range(NT):
            e = self.k.nc.scalar.activation(self.rest[:, j, :], self.work[:, u % 2, j, :], ACT.Exp, bias=self.nmax[:, u, j:j + 1])
        e.then_inc(self.rest_done, 1)

    def keep_top(self, pool, u):
        pool.wait_ge(self.rest_done, u + 1)
        v = self.p[:, u % 2, :, :]
        self.k.nc.gpsimd.tensor_tensor(v, v, self.rest[:, :, :], ALU.subtract).then_inc(self.p_ready, 1)

    def turn_p(self, pe, u):
        pe.wait_ge(self.p_ready, u + 1)
        if u >= 1:
            pe.wait_ge(self.pT_copied, u)
        for kt in range(NT):
            for j in range(NT):
                tr = self.k.nc.tensor.transpose(self.banks[2][:, kt * T + j * P:kt * T + (j + 1) * P],
                                                self.p[:, u % 2, j, kt * P:(kt + 1) * P], self.k.w["ident"])
        tr.then_inc(self.pT_ps, 1)

    def copy_pT(self, act, u):
        act.wait_ge(self.pT_ps, u + 1)
        if u >= 2:
            act.wait_ge(self.pv_done, u - 1)
        self.k.nc.scalar.activation(self.pT[:, u % 2, :, :], self.banks[2][:, :], ACT.Copy).then_inc(self.pT_copied, 1)


class LayerNorm:

    def __init__(self, k, side, tag, x, bank):
        self.k, self.x, self.bank = k, x, bank
        self.y, self.yT = k.sb(f"y{side}", [P, NT, D]), k.sb(f"yT{side}", [P, T])
        self.stats, self.mv = k.sb(f"ln_stats{side}", [P, NT, 6]), k.sb(f"ln_mv{side}", [P, NT, 2])
        self.var, self.rstd = k.sb(f"ln_var{side}", [P, NT]), k.sb(f"ln_rstd{side}", [P, NT])
        n = f"ln{side}{tag}_"
        self.chain = Chain(k.sem(n + "dve"))
        self.var_ready, self.rstd_ready = k.sem(n + "var_ready"), k.sem(n + "rstd_ready")
        self.y_ready, self.turned, self.yT_ready = k.sem(n + "y_ready"), k.sem(n + "turned"), k.sem(n + "yT_ready")

    def dve(self, dve):
        nc = self.k.nc
        for j in range(NT):
            self.chain.link(dve, nc.vector.bn_stats(self.stats[:, j, :], self.x[:, j, :]))
            self.chain.link(dve, nc.vector.bn_aggr(self.mv[:, j, :], self.stats[:, j, :]))
        nc.vector.tensor_scalar(self.var[:, :], self.mv[:, :, 1], 1e-5, None, ALU.add).then_inc(self.var_ready, 1)
        dve.wait_ge(self.rstd_ready, 1)
        for j in range(NT):
            nc.vector.tensor_scalar(self.y[:, j, :], self.x[:, j, :], self.mv[:, j, 0:1], self.rstd[:, j:j + 1],
                                    ALU.subtract, ALU.mult).then_inc(self.y_ready, 1)

    def pool(self, pool):
        pool.wait_ge(self.var_ready, 1)
        self.k.nc.gpsimd.tensor_tensor(self.rstd[:, :], self.var[:, :], self.k.half[:, 0:NT],
                                       ALU.pow).then_inc(self.rstd_ready, 1)

    def pe(self, pe):
        for j in range(NT):
            pe.wait_ge(self.y_ready, j + 1)
            self.k.nc.tensor.transpose(self.bank[:, j * P:(j + 1) * P], self.y[:, j, :],
                                       self.k.w["ident"]).then_inc(self.turned, 1)

    def act(self, act):
        act.wait_ge(self.turned, NT)
        self.k.nc.scalar.activation(self.yT[:, :], self.bank[:, 0:T], ACT.Copy).then_inc(self.yT_ready, 1)


class Performer:
    UNITS = H

    def __init__(self, k, side, x, ctxT, ctx_tok, banks, load):
        self.k, self.x, self.ctxT, self.ctx_tok, self.banks, self.load = k, x, ctxT, ctx_tok, banks, load
        self.ln = LayerNorm(k, side, "a", x, banks[0])
        work = Workspace(k, side)
        self.ksq = work.pT[:, 0, 0, :]
        self.qf, self.kf = work.qT, work.kT
        self.v = work.v
        self.a = work.p.rearrange("p u j t -> p u (j t)")[:, :, 0:3 * P]
        self.oT = work.oT
        self.den, self.tiny, self.o = k.sb("perf_den", [P, H]), k.sb("perf_tiny", [P, H]), self.ln.y
        n = "perf_"
        self.chain = Chain(k.sem(n + "dve"))
        self.ksq_ready, self.v_ready = k.sem(n + "ksq_ready"), k.sem(n + "v_ready")
        self.proj_ready, self.exp_ready, self.feat_ready = k.sem(n + "proj"), k.sem(n + "exp"), k.sem(n + "feat")
        self.a_ps, self.a_copied, self.a_masked = k.sem(n + "a_ps"), k.sem(n + "a_copied"), k.sem(n + "a_masked")
        self.pv_done, self.oT_copied, self.back = k.sem(n + "pv"), k.sem(n + "oT"), k.sem(n + "back")
        self.x_ready = k.sem(n + "x_ready")
        self.steps = 1 + self.UNITS + 2 + 1

    def pe(self, pe, s):
        nc, w, b = self.k.nc, self.k.w, self.banks
        if s == 0:
            self.ln.pe(pe)
            pe.wait_ge(self.load, 3 * 16)
            pe.wait_ge(self.ksq_ready, 1)
            for g in range(NG):
                out = b[2 + g // 2][:, (g % 2) * T:(g % 2 + 1) * T]
                nc.tensor.matmul(out, w["rf"][:, g * P:(g + 1) * P], self.ctxT[:, :], start=True, stop=False)
                nc.tensor.matmul(out, w["hsum"][:, g * P:(g + 1) * P], self.ksq, start=False,
                                 stop=True).then_inc(self.proj_ready, 1)
            pe.wait_ge(self.ln.yT_ready, 1)
            for g in range(NG):
                nc.tensor.matmul(b[g // 2][:, (g % 2) * T:(g % 2 + 1) * T], w["rf"][:, g * P:(g + 1) * P], self.ln.yT[:, :],
                                 start=True, stop=True).then_inc(self.proj_ready, 1)
        u = s - 1
        if 0 <= u < H:
            g, a = divmod(u, HG)
            r = slice(PAD * a, PAD * a + M_RF)
            if u == 0:
                pe.wait_ge(self.feat_ready, 4)
            if u >= 2:
                pe.wait_ge(self.a_copied, u - 1)
            out = b[u % 2]
            nc.tensor.matmul(out[:, 0:T], self.kf[r, g, 0:P], self.qf[r, g, :], start=True, stop=True)
            nc.tensor.matmul(out[:, T:T + P], self.kf[r, g, P:T], self.qf[r, g, P:T], start=True,
                             stop=True).then_inc(self.a_ps, 1)
        u = s - 3
        if 0 <= u < H:
            g, a = divmod(u, HG)
            pe.wait_ge(self.a_masked, u + 1)
            if u == 0:
                pe.wait_ge(self.v_ready, 1)
            if a == 0 and g > 0:
                pe.wait_ge(self.oT_copied, g)
            out = b[2][PAD * a:PAD * (a + 1), (g % 2) * T:(g % 2 + 1) * T]
            nc.tensor.matmul(out, self.v[:, 0, u, :], self.a[:, u % 2, 0:T], start=True, stop=False)
            nc.tensor.matmul(out[:, P:T], self.v[:, 1, u, :], self.a[:, u % 2, T:T + P], start=False,
                             stop=True).then_inc(self.pv_done, 1)
        if s == self.steps - 1:
            pe.wait_ge(self.oT_copied, NG)
            for j in range(NT):
                for g in range(NG):
                    nc.tensor.transpose(b[j][:, g * P:(g + 1) * P], self.oT[:, g, j * P:(j + 1) * P],
                                        w["ident"]).then_inc(self.back, 1)

    def act(self, act, s):
        nc, b = self.k.nc, self.banks
        if s == 0:
            self.ln.act(act)
            for i, (dst, bias) in enumerate([(self.kf, self.k.kbias[:, 0:1]), (self.qf, 0.0)]):
                for half in range(2):
                    act.wait_ge(self.proj_ready, 4 * i + 2 * half + 2)
                    nc.scalar.activation(dst[:, 2 * half:2 * half + 2, :], b[2 - 2 * i + half][:, :], ACT.Exp, bias=bias,
                                         scale=RF_SCALE).then_inc(self.exp_ready, 1)
        u = s - 2
        if 0 <= u < H:
            act.wait_ge(self.a_ps, u + 1)
            if u >= 2:
                act.wait_ge(self.pv_done, u - 1)
            nc.scalar.activation(self.a[:, u % 2, :], b[u % 2][:, 0:3 * P], ACT.Copy).then_inc(self.a_copied, 1)
        u = s - 3
        if 0 <= u < H and u % HG == HG - 1:
            g = u // HG
            act.wait_ge(self.pv_done, u + 1)
            nc.scalar.activation(self.oT[:, g, :], b[2][:, (g % 2) * T:(g % 2 + 1) * T], ACT.Copy).then_inc(self.oT_copied, 1)

    def pool(self, pool, s):
        nc = self.k.nc
        if s == 0:
            pool.wait_ge(self.load, 3 * 16)
            nc.gpsimd.tensor_tensor(self.ksq, self.ctxT[:, :], self.ctxT[:, :], ALU.mult).then_inc(self.ksq_ready, 1)
            self.ln.pool(pool)
            nc.gpsimd.tensor_copy(self.v[:, :, :, 0:HD],
                                  self.ctx_tok[:, :, :].rearrange("p j (h d) -> p j h d", d=HD)).then_inc(self.v_ready, 1)
            for i, dst in enumerate([self.kf, self.qf]):
                for half in range(2):
                    pool.wait_ge(self.exp_ready, 2 * i + half + 1)
                    v = dst[:, 2 * half:2 * half + 2, :]
                    nc.gpsimd.tensor_scalar(v, v, 1e-4, 1.0, ALU.add, ALU.mult).then_inc(self.feat_ready, 1)
        u = s - 2
        if 0 <= u < H:
            pool.wait_ge(self.a_copied, u + 1)
            v = self.a[:, u % 2, :].rearrange("p (b t) -> p b t", t=P)[:, 0:3:2, :]
            nc.gpsimd.tensor_tensor(v, v, self.k.w["tri"].unsqueeze(1).broadcast_to([P, 2, P]),
                                    ALU.mult).then_inc(self.a_masked, 1)

    def dve(self, dve, s):
        nc = self.k.nc
        if s == 0:
            dve.wait_ge(self.load, 3 * 16)
            self.ln.dve(dve)
        if s == self.steps - 1:
            link = lambda ins: self.chain.link(dve, ins)
            dve.wait_ge(self.back, NT * NG)
            for j in range(NT):
                t = self.banks[j][:, :].rearrange("p (h c) -> p h c", c=PAD)
                link(nc.vector.tensor_scalar(self.den[:, :], t[:, :, HD], 1.0 / M_RF, None, ALU.mult))
                link(nc.vector.tensor_scalar(self.tiny[:, :], self.den[:, :], 1e-6, 2e-6, ALU.is_le, ALU.mult))
                link(nc.vector.tensor_tensor(self.den[:, :], self.den[:, :], self.tiny[:, :], ALU.add))
                link(nc.vector.reciprocal(self.den[:, :], self.den[:, :]))
                link(nc.vector.scalar_tensor_tensor(out=self.o[:, j, :].rearrange("p (h d) -> p h d", d=HD), in0=t[:, :, 0:HD],
                                                    scalar=1.0 / M_RF, in1=self.den[:, :].unsqueeze(2).broadcast_to([P, H, HD]),
                                                    op0=ALU.mult, op1=ALU.mult))
            link(nc.vector.scalar_tensor_tensor(out=self.x[:, :, :], in0=self.o[:, :, :], scalar=self.k.tg[:, 0:1],
                                                in1=self.x[:, :, :], op0=ALU.mult, op1=ALU.add))


class HeadAttention(TopSelect):

    def __init__(self, k, side, layer, x, ctxT, banks, tag, topk=0, gate=None):
        self.k, self.x, self.banks, self.topk, self.layer, self.gate = k, x, banks, topk, layer, gate
        self.ln = LayerNorm(k, side, tag, x, banks[0])
        self.kvT = self.ln.yT if ctxT is None else ctxT
        buf = Workspace(k, side)
        self.kT, self.qT, self.v, self.p, self.pT, self.oT = buf.kT, buf.qT, buf.v, buf.p, buf.pT, buf.oT
        self.nmax = k.sb(f"att_nmax{side}", [P, H, NT])
        self.rden, self.o = k.sb(f"att_rden{side}", [P, NT, H]), self.ln.y
        self.otT = self.ln.yT
        n = f"att{side}_"
        self.chain = Chain(k.sem(n + "dve"))
        self.proj, self.proj_copied = k.sem(n + "proj"), k.sem(n + "proj_copied")
        self.v_ps, self.v_copied = k.sem(n + "v_ps"), k.sem(n + "v_copied")
        self.scores, self.max_ready, self.exp_done = k.sem(n + "scores"), k.sem(n + "max"), k.sem(n + "exp")
        self.pT_ps, self.pT_copied = k.sem(n + "pT_ps"), k.sem(n + "pT")
        self.pv_done, self.oT_copied, self.back = k.sem(n + "pv"), k.sem(n + "oT"), k.sem(n + "back")
        self.o_ready, self.o_turned, self.otT_ready = k.sem(n + "o"), k.sem(n + "o_turned"), k.sem(n + "otT")
        self.out_ps = k.sem(n + "out")
        if topk:
            self.top_buffers(k, buf, n)
            self.p_ready = k.sem(n + "p")
            self.units(H, topk // 8, 4)
            self.EXP, self.TURN, self.COPY, self.PV = (0, 1), (1, 2), (1, 2), (1, 3)
        else:
            self.p_ready = self.exp_done
            self.units(H, 1, 3)
            self.EXP, self.TURN, self.COPY, self.PV = (1, 0), (2, 0), (2, 0), (3, 0)

    def score(self, pe, u):
        g, a = divmod(u, HG)
        r = slice(PAD * a, PAD * a + HD)
        if u == 0:
            pe.wait_ge(self.proj_copied, 2 * NG)
            pe.wait_ge(self.v_copied, 1)
        if u >= 2:
            pe.wait_ge(self.exp_done, u - 1)
        for j in range(NT):
            mm = self.k.nc.tensor.matmul(self.banks[u % 2][:, j * T:(j + 1) * T], self.qT[r, g, j * P:(j + 1) * P],
                                         self.kT[r, g, :], start=True, stop=True)
        mm.then_inc(self.scores, 1)

    def pe(self, pe, s):
        nc, w, b, L = self.k.nc, self.k.w, self.banks, self.layer
        if s == 0:
            self.ln.pe(pe)
            pe.wait_ge(self.ln.yT_ready, 1)
            for i, (wt, src) in enumerate([(f"wk{L}", self.kvT), (f"wq{L}", self.ln.yT)]):
                for g in range(NG):
                    nc.tensor.matmul(b[2 * i + g // 2][:, (g % 2) * T:(g % 2 + 1) * T], w[wt][:, g * P:(g + 1) * P], src[:, :],
                                     start=True, stop=True).then_inc(self.proj, 1)
            pe.wait_ge(self.proj_copied, 2)
            for j in range(NT):
                out = b[0][:, j * D:(j + 1) * D]
                nc.tensor.matmul(out, self.kvT[:, j * P:(j + 1) * P], w[f"wv{L}"], start=True, stop=False)
                nc.tensor.matmul(out, self.k.one(f"bv{L}"), w[f"bv{L}"], start=False, stop=True).then_inc(self.v_ps, 1)
        if self.topk:
            if s == 0:
                self.score(pe, 0)
            u = self.at(s, 0, 1) + 1
            if 1 <= u < H:
                self.score(pe, u)
        else:
            u = self.at(s, 0, 0)
            if u >= 0:
                self.score(pe, u)
        u = self.at(s, *self.TURN)
        if u >= 0:
            self.turn_p(pe, u)
        u = self.at(s, *self.PV)
        if u >= 0:
            g, a = divmod(u, HG)
            pe.wait_ge(self.pT_copied, u + 1)
            if a == 0 and g > 0:
                pe.wait_ge(self.oT_copied, g)
            for kt in range(NT):
                mm = nc.tensor.matmul(b[3][PAD * a:PAD * (a + 1), (g % 2) * T:(g % 2 + 1) * T], self.v[:, kt, u, :],
                                      self.pT[:, u % 2, kt, :], start=(kt == 0), stop=(kt == NT - 1))
            mm.then_inc(self.pv_done, 1)
        if self.final(s):
            pe.wait_ge(self.oT_copied, NG)
            for j in range(NT):
                for g in range(NG):
                    tr = nc.tensor.transpose(b[j][:, g * P:(g + 1) * P], self.oT[:, g, j * P:(j + 1) * P], w["ident"])
            tr.then_inc(self.back, 1)
            if self.gate is not None:
                pe.wait_ge(self.o_ready, 2)
                for j in range(NT):
                    tr = nc.tensor.transpose(b[2][:, j * P:(j + 1) * P], self.o[:, j, :], w["ident"])
                tr.then_inc(self.o_turned, 1)
                pe.wait_ge(self.otT_ready, 1)
                for j in range(NT):
                    out = b[3][:, j * D:(j + 1) * D]
                    nc.tensor.matmul(out, self.otT[:, j * P:(j + 1) * P], w[f"wo{L}"], start=True, stop=False)
                    mm = nc.tensor.matmul(out, self.k.one(f"bo{L}"), w[f"bo{L}"], start=False, stop=True)
                mm.then_inc(self.out_ps, 1)

    def act(self, act, s):
        nc, b, L = self.k.nc, self.banks, self.layer
        if s == 0:
            self.ln.act(act)
            for i, (dst, bias, scale) in enumerate([(self.kT, self.k.w[f"bk{L}"], 1.0),
                                                    (self.qT, self.k.bq_scaled[f"bq{L}"], HD ** -0.5)]):
                for g in range(NG):
                    act.wait_ge(self.proj, NG * i + 2 * (g // 2) + 2)
                    nc.scalar.activation(dst[:, g, :], b[2 * i + g // 2][:, (g % 2) * T:(g % 2 + 1) * T], ACT.Identity,
                                         bias=bias[:, g:g + 1], scale=scale).then_inc(self.proj_copied, 1)
            act.wait_ge(self.v_ps, NT)
            nc.scalar.activation(self.v[:, :, :, 0:HD], b[0][:, 0:NT * D].rearrange("p (j h d) -> p j h d", j=NT, d=HD),
                                 ACT.Copy).then_inc(self.v_copied, 1)
        if self.topk:
            u = self.at(s, 1, 0)
            if u >= 0:
                self.exp_rest(act, u)
        u = self.at(s, *self.EXP)
        if u >= 0:
            self.exp_scores(act, u)
        u = self.at(s, *self.COPY)
        if u >= 0:
            self.copy_pT(act, u)
        u = self.at(s, *self.PV)
        if u >= 0 and u % HG == HG - 1:
            g = u // HG
            act.wait_ge(self.pv_done, u + 1)
            nc.scalar.activation(self.oT[:, g, :], b[3][:, (g % 2) * T:(g % 2 + 1) * T], ACT.Copy).then_inc(self.oT_copied, 1)
        if self.final(s) and self.gate is not None:
            act.wait_ge(self.o_turned, 1)
            nc.scalar.activation(self.otT[:, :], b[2][:, 0:T], ACT.Copy).then_inc(self.otT_ready, 1)

    def pool(self, pool, s):
        if s == 0:
            self.ln.pool(pool)
        if self.topk:
            u = self.at(s, 0, 0)
            if u >= 0:
                self.negative_max(pool, u)
            u = self.at(s, 1, 1)
            if u >= 0:
                self.keep_top(pool, u)

    def dve(self, dve, s):
        nc = self.k.nc
        if s == 0:
            self.ln.dve(dve)
        for r in range(self.rounds):
            u = self.at(s, 0, r)
            if u >= 0 and self.topk:
                self.select(dve, u, r)
            elif u >= 0:
                dve.wait_ge(self.scores, u + 1)
                nc.vector.tensor_reduce(self.nmax[:, u, :], self.banks[u % 2][:, :].rearrange("p (j t) -> p j t", j=NT),
                                        AX.X, ALU.max, negate=True).then_inc(self.max_ready, 1)
        if self.final(s):
            dve.wait_ge(self.back, 1)
            for j in range(NT):
                t = self.banks[j][:, :].rearrange("p (h c) -> p h c", c=PAD)
                self.chain.link(dve, nc.vector.reciprocal(self.rden[:, j, :], t[:, :, HD]))
                nc.vector.tensor_tensor(self.o[:, j, :].rearrange("p (h d) -> p h d", d=HD), t[:, :, 0:HD],
                                        self.rden[:, j, :].unsqueeze(2).broadcast_to([P, H, HD]),
                                        ALU.mult).then_inc(self.o_ready, 1)
            if self.gate is not None:
                dve.wait_ge(self.out_ps, 1)
                self.chain.link(dve, nc.vector.scalar_tensor_tensor(
                    out=self.x[:, :, :], in0=self.banks[3][:, 0:NT * D].rearrange("p (j d) -> p j d", j=NT),
                    scalar=self.k.tg[:, self.gate:self.gate + 1], in1=self.x[:, :, :], op0=ALU.mult, op1=ALU.add))


class WideAttention(TopSelect):
    topk = 64

    def __init__(self, k, side, x, ctxT, banks, gate):
        self.k, self.x, self.ctxT, self.banks, self.gate = k, x, ctxT, banks, gate
        self.ln = LayerNorm(k, side, "a", x, banks[0])
        buf = Workspace(k, side)
        self.qT, self.kT, self.p, self.pT = buf.qT, buf.kT, buf.p, buf.pT
        self.v = k.sb("wide_v", [P, NT, H1, HD1 + 1])
        self.nmax = k.sb(f"att_nmax{side}", [P, H, NT])
        self.rden, self.o = k.sb("wide_rden", [P, H1, NT]), buf.oT.rearrange("p (j c) t -> p j (c t)", j=NT)
        self.otT = k.sb("mix_wb", [P, E16, T])[:, 0:4, :].rearrange("p (j a) (b t) -> p j (a b) t", j=NT, t=P)
        n = f"att{side}_"
        self.chain = Chain(k.sem(n + "dve"))
        self.proj, self.proj_copied = k.sem(n + "proj"), k.sem(n + "proj_copied")
        self.scores, self.max_ready, self.exp_done = k.sem(n + "scores"), k.sem(n + "max"), k.sem(n + "exp")
        self.p_ready, self.pT_ps, self.pT_copied = k.sem(n + "p"), k.sem(n + "pT_ps"), k.sem(n + "pT")
        self.pv_done, self.rden_ready, self.o_ready = k.sem(n + "pv"), k.sem(n + "rden"), k.sem(n + "o")
        self.back, self.otT_ready, self.out_ps = k.sem(n + "back"), k.sem(n + "otT"), k.sem(n + "out")
        self.top_buffers(k, buf, n)
        self.units(H1, self.topk // 8, 7)

    def score(self, pe, u):
        c, a = divmod(u, 2)
        r = slice(HD1 * a, HD1 * (a + 1))
        if u == 0:
            pe.wait_ge(self.proj_copied, 6)
        if u >= 2:
            pe.wait_ge(self.exp_done, u - 1)
        for j in range(NT):
            mm = self.k.nc.tensor.matmul(self.banks[u % 2][:, j * T:(j + 1) * T], self.qT[r, c, j * P:(j + 1) * P],
                                         self.kT[r, c, :], start=True, stop=True)
        mm.then_inc(self.scores, 1)

    def pe(self, pe, s):
        nc, w, b = self.k.nc, self.k.w, self.banks
        if s == 0:
            self.ln.pe(pe)
            pe.wait_ge(self.ln.yT_ready, 1)
            for i, (wt, src) in enumerate([("wk1", self.ctxT), ("wq1", self.ln.yT)]):
                for c in range(4):
                    nc.tensor.matmul(b[2 * i + c // 2][:, (c % 2) * T:(c % 2 + 1) * T], w[wt][:, c * P:(c + 1) * P], src[:, :],
                                     start=True, stop=True).then_inc(self.proj, 1)
            for j in range(NT):
                pe.wait_ge(self.proj_copied, 1 + j)
                nc.tensor.matmul(b[j][:, :], self.ctxT[:, j * P:(j + 1) * P], w["wv1"], start=True,
                                 stop=True).then_inc(self.proj, 1)
            self.score(pe, 0)
        u = self.at(s, 0, 2) + 1
        if 1 <= u < H1:
            self.score(pe, u)
        u = self.at(s, 1, 3)
        if u >= 0:
            self.turn_p(pe, u)
        u = self.at(s, 1, 5)
        if u >= 0:
            pe.wait_ge(self.pT_copied, u + 1)
            if u >= 1:
                pe.wait_ge(self.o_ready, u)
            for j in range(NT):
                for kt in range(NT):
                    mm = nc.tensor.matmul(b[3][:, j * (HD1 + 1):(j + 1) * (HD1 + 1)], self.pT[:, u % 2, kt, j * P:(j + 1) * P],
                                          self.v[:, kt, u, :], start=(kt == 0), stop=(kt == NT - 1))
            mm.then_inc(self.pv_done, 1)
        if self.final(s):
            pe.wait_ge(self.o_ready, H1)
            for j in range(NT):
                for c in range(4):
                    tr = nc.tensor.transpose(b[j][:, c * P:(c + 1) * P], self.o[:, j, c * P:(c + 1) * P], w["ident"])
                tr.then_inc(self.back, 1)
            for j in range(NT):
                pe.wait_ge(self.otT_ready, j + 1)
                out = b[2][:, j * D:(j + 1) * D]
                nc.tensor.matmul(out, self.k.one("bout1"), w["bout1"], start=True, stop=False)
                for c in range(4):
                    mm = nc.tensor.matmul(out, self.otT[:, j, c, :], w["wo1"][:, c * D:(c + 1) * D], start=False, stop=(c == 3))
            mm.then_inc(self.out_ps, 1)

    def act(self, act, s):
        nc, b = self.k.nc, self.banks
        if s == 0:
            self.ln.act(act)
            for i, (dst, scale) in enumerate([(self.kT, 1.0), (self.qT, HD1 ** -0.5)]):
                for half in range(2):
                    act.wait_ge(self.proj, 4 * i + 2 * half + 2)
                    nc.scalar.activation(dst[:, 2 * half:2 * half + 2, :], b[2 * i + half][:, :], ACT.Copy,
                                         scale=scale).then_inc(self.proj_copied, 1)
            for j in range(NT):
                act.wait_ge(self.proj, 8 + j + 1)
                nc.scalar.activation(self.v[:, j, :, 0:HD1], b[j][:, :].rearrange("p (h d) -> p h d", d=HD1),
                                     ACT.Copy).then_inc(self.proj_copied, 1)
        u = self.at(s, 1, 0)
        if u >= 0:
            self.exp_rest(act, u)
        u = self.at(s, 0, 1)
        if u >= 0:
            self.exp_scores(act, u)
        u = self.at(s, 1, 4)
        if u >= 0:
            self.copy_pT(act, u)
        u = self.at(s, 1, 6)
        if u >= 0:
            act.wait_ge(self.rden_ready, u + 1)
            for j in range(NT):
                e = nc.scalar.activation(self.o[:, j, u * HD1:(u + 1) * HD1], b[3][:, j * (HD1 + 1):j * (HD1 + 1) + HD1],
                                         ACT.Copy, scale=self.rden[:, u, j:j + 1])
            e.then_inc(self.o_ready, 1)
        if self.final(s):
            for j in range(NT):
                act.wait_ge(self.back, j + 1)
                nc.scalar.activation(self.otT[:, j, :, :], b[j][:, :], ACT.Copy).then_inc(self.otT_ready, 1)

    def pool(self, pool, s):
        if s == 0:
            self.ln.pool(pool)
        u = self.at(s, 0, 0)
        if u >= 0:
            self.negative_max(pool, u)
        u = self.at(s, 1, 1)
        if u >= 0:
            self.keep_top(pool, u)

    def dve(self, dve, s):
        nc = self.k.nc
        if s == 0:
            self.ln.dve(dve)
        for r in range(self.rounds):
            u = self.at(s, 0, r)
            if u >= 0:
                self.select(dve, u, r)
        u = self.at(s, 1, 6)
        if u >= 0:
            dve.wait_ge(self.pv_done, u + 1)
            nc.vector.reciprocal(self.rden[:, u, :], self.banks[3][:, 0:NT * (HD1 + 1)].rearrange("p (j c) -> p j c", j=NT)[:, :, HD1]).then_inc(self.rden_ready, 1)
        if self.final(s):
            dve.wait_ge(self.out_ps, 1)
            self.chain.link(dve, nc.vector.scalar_tensor_tensor(
                out=self.x[:, :, :], in0=self.banks[2][:, 0:NT * D].rearrange("p (j d) -> p j d", j=NT),
                scalar=self.k.tg[:, self.gate:self.gate + 1], in1=self.x[:, :, :], op0=ALU.mult, op1=ALU.add))


class Router:

    def __init__(self, k, side, tag, kind, lhsT, weight, bias, bank, t_bank):
        self.k, self.kind, self.lhsT, self.weight, self.bias, self.bank, self.t_bank = k, kind, lhsT, weight, bias, bank, t_bank
        self.nmax, self.sum = k.sb(f"rt_nmax{side}", [P, NT]), k.sb(f"rt_sum{side}", [P, NT])
        self.e = k.sb(f"rt_e{side}", [P, NT, E8])
        self.pr, self.wk = k.sb(f"rt_pr{side}", [P, NT, E8 + 6]), k.sb(f"rt_wk{side}", [P, NT, E8 + 6])
        self.m8 = k.sb(f"rt_m8{side}", [P, NT, 8])
        self.comb, self.combT = k.sb(f"rt_comb{side}", [P, NT, E8 + 1]), k.sb(f"rt_combT{side}", [E8 + 1, T])
        n = f"rt{side}{tag}_"
        self.chain = Chain(k.sem(n + "dve"))
        self.logits, self.nmax_ready, self.e_ready = k.sem(n + "logits"), k.sem(n + "nmax"), k.sem(n + "e")
        self.comb_ready, self.turned, self.combT_ready = k.sem(n + "comb"), k.sem(n + "turned"), k.sem(n + "combT")

    def pe_logits(self, pe):
        nc, w = self.k.nc, self.k.w
        for j in range(NT):
            out = self.bank[:, j * E8:(j + 1) * E8]
            mm = nc.tensor.matmul(out, self.lhsT[:, j * P:(j + 1) * P], w[self.weight], start=True, stop=self.bias is None)
            if self.bias is not None:
                mm = nc.tensor.matmul(out, w["ones"][0:1, :], w[self.bias], start=False, stop=True)
        mm.then_inc(self.logits, 1)

    def pe_turn(self, pe):
        pe.wait_ge(self.comb_ready, 1)
        for j in range(NT):
            tr = self.k.nc.tensor.transpose(self.t_bank[0:E8 + 1, j * P:(j + 1) * P], self.comb[:, j, :], self.k.w["ident"])
        tr.then_inc(self.turned, 1)

    def act_exp(self, act):
        act.wait_ge(self.nmax_ready, 1)
        for j in range(NT):
            e = self.k.nc.scalar.activation(self.e[:, j, :], self.bank[:, j * E8:(j + 1) * E8], ACT.Exp, bias=self.nmax[:, j:j + 1])
        e.then_inc(self.e_ready, 1)

    def act_turn(self, act):
        act.wait_ge(self.turned, 1)
        self.k.nc.scalar.activation(self.combT[:, :], self.t_bank[0:E8 + 1, 0:T], ACT.Copy).then_inc(self.combT_ready, 1)

    def dve(self, dve):
        nc = self.k.nc
        v = nc.vector
        link = lambda ins: self.chain.link(dve, ins)
        lg = self.bank[:, 0:NT * E8].rearrange("p (j e) -> p j e", j=NT)
        pr = self.pr[:, :, 0:E8]
        wide = lambda t: t.unsqueeze(2).broadcast_to([P, NT, E8])
        dve.wait_ge(self.logits, 1)
        if self.kind == "top":
            link(v.tensor_copy(pr, lg))
        v.tensor_reduce(self.nmax[:, :], lg, AX.X, ALU.max, negate=True).then_inc(self.nmax_ready, 1)
        dve.wait_ge(self.e_ready, 1)
        if self.kind != "top":
            link(v.tensor_reduce(self.sum[:, :], self.e[:, :, :], AX.X, ALU.add))
            link(v.reciprocal(self.sum[:, :], self.sum[:, :]))
            link(v.tensor_tensor(pr, self.e[:, :, :], wide(self.sum[:, :]), ALU.mult))
        for j in range(NT):
            link(v.max(self.m8[:, j, :], self.pr[:, j, 0:E8]))
        link(v.memset(self.m8[:, :, 2:8], SENT))
        for j in range(NT):
            link(v.match_replace(self.wk[:, j, :], self.m8[:, j, :], self.pr[:, j, :], GONE))
        link(v.tensor_scalar(self.wk[:, :, 0:E8], self.wk[:, :, 0:E8], 0.5 * (SENT + GONE), None, ALU.is_le))
        comb, chosen = self.comb[:, :, 0:E8], self.wk[:, :, 0:E8]
        if self.kind == "prob":
            v.tensor_tensor(comb, chosen, pr, ALU.mult).then_inc(self.comb_ready, 1)
        else:
            src = self.e[:, :, :] if self.kind == "top" else pr
            link(v.tensor_tensor(comb, chosen, src, ALU.mult))
            link(v.tensor_reduce(self.sum[:, :], comb, AX.X, ALU.add))
            if self.kind == "renorm":
                link(v.tensor_scalar(self.sum[:, :], self.sum[:, :], 1e-9, None, ALU.add))
            link(v.reciprocal(self.sum[:, :], self.sum[:, :]))
            v.tensor_tensor(comb, comb, wide(self.sum[:, :]), ALU.mult).then_inc(self.comb_ready, 1)
        dve.wait_ge(self.comb_ready, 1)


class LinearExperts:

    def __init__(self, k, side, x, att, banks, gate):
        self.k, self.x, self.att, self.banks, self.gate = k, x, att, banks, gate
        self.yT = att.ln.yT
        self.rt = Router(k, side, "a", "prob", self.yT, "gate0", "bgate0", banks[2], banks[3])
        self.acc = k.sb(f"moe_acc{side}", [P, NT, D])
        n = f"moe{side}_"
        self.chain = Chain(k.sem(n + "dve"))
        self.y_ps, self.y_used, self.bias_ps = k.sem(n + "y_ps"), k.sem(n + "y_used"), k.sem(n + "bias_ps")
        self.steps = 3

    def pe(self, pe, s):
        nc, w, b = self.k.nc, self.k.w, self.banks
        if s == 0:
            pe.wait_ge(self.att.oT_copied, NG)
            self.rt.pe_logits(pe)
        if s == 1:
            self.rt.pe_turn(pe)
            pe.wait_ge(self.rt.combT_ready, 1)
            for j in range(NT):
                mm = nc.tensor.matmul(b[2][:, j * D:(j + 1) * D], self.rt.combT[:, j * P:(j + 1) * P], w["bias0"][0:E8 + 1, :],
                                      start=True, stop=True)
            mm.then_inc(self.bias_ps, 1)
            pe.wait_ge(self.att.o_ready, 2)
        if s in (1, 2):
            j = s - 1
            for half in range(2):
                if j == 1:
                    pe.wait_ge(self.y_used, 4 * half + 4)
                nc.tensor.matmul(b[half][:, :], self.yT[:, j * P:(j + 1) * P], w["exp0"][:, half * 512:(half + 1) * 512],
                                 start=True, stop=True).then_inc(self.y_ps, 1)

    def act(self, act, s):
        if s == 0:
            self.rt.act_exp(act)
        if s == 1:
            self.rt.act_turn(act)

    def pool(self, pool, s):
        pass

    def dve(self, dve, s):
        nc = self.k.nc
        if s == 0:
            self.rt.dve(dve)
        if s == 1:
            dve.wait_ge(self.bias_ps, 1)
            self.chain.link(dve, nc.vector.tensor_tensor(
                self.acc[:, :, :], self.banks[2][:, 0:NT * D].rearrange("p (j d) -> p j d", j=NT), self.att.o[:, :, :], ALU.add))
        if s in (1, 2):
            j = s - 1
            for e in range(E8):
                dve.wait_ge(self.y_ps, 2 * j + e // 4 + 1)
                if j == 1 or e > 0:
                    dve.wait_ge(self.y_used, E8 * j + e)
                nc.vector.scalar_tensor_tensor(out=self.acc[:, j, :], in0=self.banks[e // 4][:, (e % 4) * D:(e % 4 + 1) * D],
                                               scalar=self.rt.comb[:, j, e:e + 1], in1=self.acc[:, j, :], op0=ALU.mult,
                                               op1=ALU.add).then_inc(self.y_used, 1)
        if s == 2:
            dve.wait_ge(self.y_used, NT * E8)
            self.chain.link(dve, nc.vector.scalar_tensor_tensor(out=self.x[:, :, :], in0=self.acc[:, :, :],
                                                                scalar=self.k.tg[:, self.gate:self.gate + 1], in1=self.x[:, :, :],
                                                                op0=ALU.mult, op1=ALU.add))


class GatedExperts:

    def __init__(self, k, side, x, banks, gate):
        self.k, self.x, self.banks, self.gate = k, x, banks, gate
        self.ln = LayerNorm(k, side, "a", x, banks[0])
        self.rt = Router(k, side, "a", "top", self.ln.yT, "router1", None, banks[2], banks[3])
        buf = Workspace(k, side)
        self.th, self.hT = buf.p[:, 0, :, :], buf.p[:, 1, :, :]
        self.acc = k.sb(f"moe_acc{side}", [P, NT, D])
        n = f"moe{side}_"
        self.chain = Chain(k.sem(n + "dve"))
        self.h_ps, self.th_ready, self.u_ready = k.sem(n + "h_ps"), k.sem(n + "th"), k.sem(n + "u")
        self.hT_ready, self.y_ps, self.y_used = k.sem(n + "hT"), k.sem(n + "y_ps"), k.sem(n + "y_used")
        self.N = 2 + E8
        self.steps = 1 + self.N + 1

    def pe(self, pe, s):
        nc, w, b = self.k.nc, self.k.w, self.banks
        if s == 0:
            self.ln.pe(pe)
            pe.wait_ge(self.ln.yT_ready, 1)
            self.rt.pe_logits(pe)
        u = s - 1
        if 0 <= u < self.N:
            if u == 0:
                pe.wait_ge(self.ln.yT_ready, 1)
            if u >= 2:
                pe.wait_ge(self.hT_ready, u - 1)
            if u < 2:
                pw, gw = w["gate_w"][:, u * D:(u + 1) * D], w["up_w"][:, u * D:(u + 1) * D]
            else:
                pw, gw = (w["fc1"][:, (2 * (u - 2) + i) * D:(2 * (u - 2) + i + 1) * D] for i in range(2))
            nc.tensor.matmul(b[u % 2][:, 0:T], pw, self.ln.yT[:, :], start=True, stop=True)
            nc.tensor.matmul(b[u % 2][:, T:2 * T], gw, self.ln.yT[:, :], start=True, stop=True).then_inc(self.h_ps, 1)
        u = s - 2
        if u == 1:
            pe.wait_ge(self.rt.combT_ready, 1)
            pe.wait_ge(self.hT_ready, 2)
            for j in range(NT):
                for c in range(2):
                    mm = nc.tensor.matmul(b[2][:, j * D:(j + 1) * D], self.hT[:, c, j * P:(j + 1) * P],
                                          w["down_w"][:, c * D:(c + 1) * D], start=(c == 0), stop=(c == 1))
            mm.then_inc(self.y_ps, 1)
        if 2 <= u < self.N:
            pe.wait_ge(self.hT_ready, u + 1)
            if u >= 3:
                pe.wait_ge(self.y_used, u - 2)
            for j in range(NT):
                mm = nc.tensor.matmul(b[3 - u % 2][:, j * D:(j + 1) * D], self.hT[:, u % 2, j * P:(j + 1) * P],
                                      w["fc2"][:, (u - 2) * D:(u - 1) * D], start=True, stop=True)
            mm.then_inc(self.y_ps, 1)
        if s == 1:
            self.rt.pe_turn(pe)

    def act(self, act, s):
        nc = self.k.nc
        if s == 0:
            self.ln.act(act)
            self.rt.act_exp(act)
        u = s - 1
        if 0 <= u < self.N:
            act.wait_ge(self.h_ps, u + 1)
            if u >= 2:
                act.wait_ge(self.hT_ready, u - 1)
            nc.scalar.activation(self.th[:, u % 2, :], self.banks[u % 2][:, 0:T], ACT.Tanh, scale=0.5).then_inc(self.th_ready, 1)
        if s == 1:
            self.rt.act_turn(act)

    def pool(self, pool, s):
        if s == 0:
            self.ln.pool(pool)

    def dve(self, dve, s):
        nc, b = self.k.nc, self.banks
        if s == 0:
            self.ln.dve(dve)
            self.rt.dve(dve)
        u = s - 1
        if 0 <= u < self.N:
            dve.wait_ge(self.th_ready, u + 1)
            th = self.th[:, u % 2, :]
            nc.vector.scalar_tensor_tensor(out=th, in0=th, scalar=1.0, in1=b[u % 2][:, 0:T], op0=ALU.add,
                                           op1=ALU.mult).then_inc(self.u_ready, 1)
            dve.wait_ge(self.u_ready, u + 1)
            if u >= 2:
                dve.wait_ge(self.y_ps, u - 2 if u > 3 else 1)
            nc.vector.scalar_tensor_tensor(out=self.hT[:, u % 2, :], in0=th, scalar=0.5, in1=b[u % 2][:, T:2 * T],
                                           op0=ALU.mult, op1=ALU.mult).then_inc(self.hT_ready, 1)
        u = s - 2
        if u == 1:
            dve.wait_ge(self.y_ps, 1)
            nc.vector.tensor_copy(self.acc[:, :, :], b[2][:, 0:NT * D].rearrange("p (j d) -> p j d", j=NT)).then_inc(self.y_used, 1)
        if 2 <= u < self.N:
            dve.wait_ge(self.y_ps, u)
            dve.wait_ge(self.y_used, u - 1)
            for j in range(NT):
                ins = nc.vector.scalar_tensor_tensor(out=self.acc[:, j, :], in0=b[3 - u % 2][:, j * D:(j + 1) * D],
                                                     scalar=self.rt.comb[:, j, u - 2:u - 1], in1=self.acc[:, j, :], op0=ALU.mult,
                                                     op1=ALU.add)
            ins.then_inc(self.y_used, 1)
        if s == self.steps - 1:
            dve.wait_ge(self.y_used, self.N - 1)
            self.chain.link(dve, nc.vector.scalar_tensor_tensor(out=self.x[:, :, :], in0=self.acc[:, :, :],
                                                                scalar=self.k.tg[:, self.gate:self.gate + 1], in1=self.x[:, :, :],
                                                                op0=ALU.mult, op1=ALU.add))


class GeluExperts:

    def __init__(self, k, side, x, banks, gate):
        self.k, self.x, self.banks, self.gate = k, x, banks, gate
        self.ln = LayerNorm(k, side, "c", x, banks[0])
        self.rt = Router(k, side, "b", "renorm", self.ln.yT, "router2", "br2", banks[2], banks[3])
        buf = Workspace(k, side)
        self.hT = [buf.kT, buf.qT]
        self.acc = k.sb(f"moe_acc{side}", [P, NT, D])
        n = f"gelu{side}_"
        self.chain = Chain(k.sem(n + "dve"))
        self.h_ps, self.hT_ready, self.y_ps, self.y_used = k.sem(n + "h_ps"), k.sem(n + "hT"), k.sem(n + "y_ps"), k.sem(n + "y_used")
        self.N = 1 + E8
        self.steps = 1 + self.N + 1

    def pe(self, pe, s):
        nc, w, b = self.k.nc, self.k.w, self.banks
        if s == 0:
            self.ln.pe(pe)
            pe.wait_ge(self.ln.yT_ready, 1)
            self.rt.pe_logits(pe)
        u = s - 1
        if 0 <= u < self.N:
            for c in range(FF2):
                if u >= 1 and c % 2 == 0:
                    pe.wait_ge(self.hT_ready, FF2 * (u - 1) + c + 2)
                mm = nc.tensor.matmul(b[c // 2][:, (c % 2) * T:(c % 2 + 1) * T], w["w1"][:, (u * FF2 + c) * 128:(u * FF2 + c + 1) * 128],
                                      self.ln.yT[:, :], start=True, stop=True)
                if c % 2 == 1:
                    mm.then_inc(self.h_ps, 1)
        if s == 1:
            self.rt.pe_turn(pe)
        u = s - 2
        if 0 <= u < self.N:
            if u == 0:
                pe.wait_ge(self.rt.combT_ready, 1)
            if u >= 2:
                pe.wait_ge(self.y_used, u - 1)
            pe.wait_ge(self.hT_ready, FF2 * (u + 1))
            for j in range(NT):
                out = b[2 + u % 2][:, j * D:(j + 1) * D]
                if u == 0:
                    nc.tensor.matmul(out, self.rt.combT[:, j * P:(j + 1) * P], w["bias2"][0:E8 + 1, :], start=True, stop=False)
                for c in range(FF2):
                    mm = nc.tensor.matmul(out, self.hT[u % 2][:, c, j * P:(j + 1) * P],
                                          w["w2"][:, (u * FF2 + c) * 128:(u * FF2 + c + 1) * 128],
                                          start=(u > 0 and c == 0), stop=(c == FF2 - 1))
            mm.then_inc(self.y_ps, 1)

    def act(self, act, s):
        nc = self.k.nc
        if s == 0:
            self.ln.act(act)
            self.rt.act_exp(act)
        if s == 1:
            self.rt.act_turn(act)
        u = s - 1
        if 0 <= u < self.N:
            for c in range(FF2):
                act.wait_ge(self.h_ps, 2 * u + c // 2 + 1)
                if u >= 2 and c == 0:
                    act.wait_ge(self.y_ps, u - 1)
                nc.scalar.activation(self.hT[u % 2][:, c, :], self.banks[c // 2][:, (c % 2) * T:(c % 2 + 1) * T], ACT.Gelu,
                                     bias=self.k.w["b1"][:, u * FF2 + c:u * FF2 + c + 1]).then_inc(self.hT_ready, 1)

    def pool(self, pool, s):
        if s == 0:
            self.ln.pool(pool)

    def dve(self, dve, s):
        nc, b = self.k.nc, self.banks
        if s == 0:
            self.ln.dve(dve)
            self.rt.dve(dve)
        u = s - 2
        if u == 0:
            dve.wait_ge(self.y_ps, 1)
            nc.vector.tensor_copy(self.acc[:, :, :], b[2][:, 0:NT * D].rearrange("p (j d) -> p j d", j=NT)).then_inc(self.y_used, 1)
        if 1 <= u < self.N:
            dve.wait_ge(self.y_ps, u + 1)
            dve.wait_ge(self.y_used, u)
            for j in range(NT):
                ins = nc.vector.scalar_tensor_tensor(out=self.acc[:, j, :], in0=b[2 + u % 2][:, j * D:(j + 1) * D],
                                                     scalar=self.rt.comb[:, j, u - 1:u], in1=self.acc[:, j, :], op0=ALU.mult,
                                                     op1=ALU.add)
            ins.then_inc(self.y_used, 1)
        if s == self.steps - 1:
            dve.wait_ge(self.y_used, self.N)
            self.chain.link(dve, nc.vector.scalar_tensor_tensor(out=self.x[:, :, :], in0=self.acc[:, :, :],
                                                                scalar=self.k.tg[:, self.gate:self.gate + 1], in1=self.x[:, :, :],
                                                                op0=ALU.mult, op1=ALU.add))


class MixedAttention:

    def __init__(self, k, side, x, banks, gate):
        self.k, self.x, self.banks, self.gate = k, x, banks, gate
        self.ln = LayerNorm(k, side, "b", x, banks[0])
        self.ssq, self.rn = k.sb("mix_ssq", [P, NT]), k.sb("mix_rn", [P, NT])
        self.lg, self.wk = k.sb("mix_lg", [P, NT, E16 + 6]), k.sb("mix_wk", [P, NT, E16 + 6])
        self.m8, self.none, self.ngm = k.sb("mix_m8", [P, NT, 8]), k.sb("mix_none", [P, NT]), k.sb("mix_ngm", [P, NT])
        self.gt, self.act_mask, self.wt = k.sb("mix_gt", [P, NT, E16]), k.sb("mix_mask", [P, NT, E16]), k.sb("mix_wt", [P, NT, E16])
        self.sum = k.sb("mix_sum", [P, NT])
        buf = Workspace(k, side)
        self.sq = buf.p[:, 0, 0, :].rearrange("p (j d) -> p j d", j=NT)
        self.wT, self.wb, self.zT = buf.p[0:E16, 0, 1, :], k.sb("mix_wb", [P, E16, T]), buf.whole
        self.qT, self.kT = buf.p[:, 1, 0, :], buf.p[:, 1, 1, :]
        self.v = buf.pT[:, 1, 0, :].rearrange("p (j d) -> p j d", j=NT)
        self.nmax, self.den, self.rden = k.sb("mix_nmax", [P, NT]), k.sb("mix_den", [P, NT]), k.sb("mix_rden", [P, NT])
        self.p, self.pT, self.oT = buf.p[:, 0, :, :], buf.pT[:, 0, :, :], buf.pT[:, 1, 1, :]
        n = "mix_"
        self.chain = Chain(k.sem(n + "dve"))
        self.ssq_ready, self.rn_in, self.rn_ready, self.logits = k.sem(n + "ssq"), k.sem(n + "rn_in"), k.sem(n + "rn"), k.sem(n + "logits")
        self.gt_ready, self.e_ready, self.wt_ready = k.sem(n + "gt"), k.sem(n + "e"), k.sem(n + "wt")
        self.turned, self.wT_ready = k.sem(n + "turned"), k.sem(n + "wT")
        self.wb_ps, self.wb_ready, self.z_ready = k.sem(n + "wb_ps"), k.sem(n + "wb"), k.sem(n + "z")
        self.qk_ps, self.qk_copied, self.v_ps, self.v_copied = k.sem(n + "qk_ps"), k.sem(n + "qk"), k.sem(n + "v_ps"), k.sem(n + "v")
        self.scores, self.max_ready, self.exp_done, self.p_ready = k.sem(n + "scores"), k.sem(n + "max"), k.sem(n + "exp"), k.sem(n + "p")
        self.pT_ps, self.pT_copied, self.o_ps, self.o_copied = k.sem(n + "pT_ps"), k.sem(n + "pT"), k.sem(n + "o_ps"), k.sem(n + "o")
        self.zo_ready, self.out_ps, self.x_done = k.sem(n + "zo"), k.sem(n + "out"), k.sem(n + "x_done")
        self.PAIRS = E16 // 2
        self.steps = 2 + self.PAIRS + 1 + 2

    def pe(self, pe, s):
        nc, w, b = self.k.nc, self.k.w, self.banks
        if s == 0:
            self.ln.pe(pe)
            pe.wait_ge(self.ln.yT_ready, 1)
            for j in range(NT):
                mm = nc.tensor.matmul(b[1][:, j * E16:(j + 1) * E16], self.ln.yT[:, j * P:(j + 1) * P], self.k.sn[:, :],
                                      start=True, stop=True)
            mm.then_inc(self.logits, 1)
        if s == 1:
            pe.wait_ge(self.wt_ready, 1)
            for j in range(NT):
                tr = nc.tensor.transpose(b[0][0:E16, j * P:(j + 1) * P], self.wt[:, j, :], w["ident"])
            tr.then_inc(self.turned, 1)
            pe.wait_ge(self.wT_ready, 1)
        i = s - 2
        if 0 <= i < self.PAIRS:
            if i >= 2:
                pe.wait_ge(self.wb_ready, i - 1)
            for e in (2 * i, 2 * i + 1):
                mm = nc.tensor.matmul(b[i % 2][:, (e % 2) * T:(e % 2 + 1) * T], w["ident"][0:E16, e:e + 1].broadcast_to([E16, P]), self.wT,
                                      start=True, stop=True)
            mm.then_inc(self.wb_ps, 1)
        i = s - 3
        if 0 <= i < self.PAIRS:
            pe.wait_ge(self.z_ready, i + 1)
            for e in (2 * i, 2 * i + 1):
                first, last = e == 0, e == E16 - 1
                nc.tensor.matmul(b[2][:, 0:T], w["qp"][:, e * D:(e + 1) * D], self.zT[:, e, :], start=first, stop=last)
                mm = nc.tensor.matmul(b[3][:, 0:T], w["kp"][:, e * D:(e + 1) * D], self.zT[:, e, :], start=first, stop=last)
            if i == self.PAIRS - 1:
                mm.then_inc(self.qk_ps, 1)
        if s == self.steps - 2:
            pe.wait_ge(self.wb_ready, self.PAIRS)
            for j in range(NT):
                for e in range(E16):
                    mm = nc.tensor.matmul(b[0][:, j * D:(j + 1) * D], self.zT[:, e, j * P:(j + 1) * P], w["vp"][:, e * D:(e + 1) * D],
                                          start=(e == 0), stop=(e == E16 - 1))
            mm.then_inc(self.v_ps, 1)
            pe.wait_ge(self.qk_copied, 2)
            for j in range(NT):
                mm = nc.tensor.matmul(b[1][:, j * T:(j + 1) * T], self.qT[:, j * P:(j + 1) * P], self.kT[:, :], start=True, stop=True)
            mm.then_inc(self.scores, 1)
            pe.wait_ge(self.p_ready, NT)
            for kt in range(NT):
                for j in range(NT):
                    tr = nc.tensor.transpose(b[2][:, kt * T + j * P:kt * T + (j + 1) * P], self.p[:, j, kt * P:(kt + 1) * P], w["ident"])
            tr.then_inc(self.pT_ps, 1)
            pe.wait_ge(self.pT_copied, 1)
            pe.wait_ge(self.v_copied, 1)
            for kt in range(NT):
                mm = nc.tensor.matmul(b[3][:, 0:T], self.v[:, kt, :], self.pT[:, kt, :], start=(kt == 0), stop=(kt == NT - 1))
            mm.then_inc(self.o_ps, 1)
        if s == self.steps - 1:
            for j in range(NT):
                for e in range(E16):
                    if e % 2 == 0:
                        pe.wait_ge(self.zo_ready, e // 2 + 1)
                    mm = nc.tensor.matmul(b[j][:, 0:D], self.zT[:, e, j * P:(j + 1) * P], w["op"][:, e * D:(e + 1) * D],
                                          start=(e == 0), stop=(e == E16 - 1))
                mm.then_inc(self.out_ps, 1)

    def act(self, act, s):
        nc, b = self.k.nc, self.banks
        if s == 0:
            self.ln.act(act)
            for j in range(NT):
                act.wait_ge(self.ln.y_ready, j + 1)
                nc.scalar.activation(self.sq[:, j, :], self.ln.y[:, j, :], ACT.Square,
                                     accum_out=self.ssq[:, j:j + 1]).then_inc(self.ssq_ready, 1)
            act.wait_ge(self.gt_ready, 1)
            for j in range(NT):
                e = nc.scalar.activation(self.wt[:, j, :], self.gt[:, j, :], ACT.Exp, bias=self.ngm[:, j:j + 1])
            e.then_inc(self.e_ready, 1)
        if s == 1:
            act.wait_ge(self.turned, 1)
            nc.scalar.activation(self.wT, b[0][0:E16, 0:T], ACT.Copy).then_inc(self.wT_ready, 1)
        i = s - 2
        if 0 <= i < self.PAIRS:
            act.wait_ge(self.wb_ps, i + 1)
            nc.scalar.activation(self.wb[:, 2 * i:2 * i + 2, :], b[i % 2][:, :], ACT.Copy).then_inc(self.wb_ready, 1)
        if s == self.steps - 2:
            act.wait_ge(self.qk_ps, 1)
            nc.scalar.activation(self.qT, b[2][:, 0:T], ACT.Copy, scale=D ** -0.5).then_inc(self.qk_copied, 1)
            nc.scalar.activation(self.kT, b[3][:, 0:T], ACT.Copy).then_inc(self.qk_copied, 1)
            act.wait_ge(self.v_ps, 1)
            nc.scalar.activation(self.v[:, :, :], b[0][:, 0:NT * D], ACT.Copy).then_inc(self.v_copied, 1)
            act.wait_ge(self.max_ready, 1)
            for j in range(NT):
                nc.scalar.activation(self.p[:, j, :], b[1][:, j * T:(j + 1) * T], ACT.Exp, bias=self.nmax[:, j:j + 1],
                                     accum_out=self.den[:, j:j + 1]).then_inc(self.exp_done, 1)
            act.wait_ge(self.pT_ps, 1)
            nc.scalar.activation(self.pT[:, :, :], b[2][:, :], ACT.Copy).then_inc(self.pT_copied, 1)
            act.wait_ge(self.o_ps, 1)
            nc.scalar.activation(self.oT[:, :], b[3][:, 0:T], ACT.Copy).then_inc(self.o_copied, 1)

    def pool(self, pool, s):
        nc = self.k.nc
        if s == 0:
            self.ln.pool(pool)
            pool.wait_ge(self.rn_in, 1)
            nc.gpsimd.tensor_tensor(self.rn[:, :], self.ssq[:, :], self.k.half[:, 0:NT], ALU.pow).then_inc(self.rn_ready, 1)
        i = s - 2
        if 0 <= i < self.PAIRS:
            pool.wait_ge(self.wb_ready, i + 1)
            nc.gpsimd.tensor_tensor(self.zT[:, 2 * i:2 * i + 2, :], self.wb[:, 2 * i:2 * i + 2, :],
                                    self.ln.yT[:, :].unsqueeze(1).broadcast_to([P, 2, T]), ALU.mult).then_inc(self.z_ready, 1)

    def dve(self, dve, s):
        nc, b = self.k.nc, self.banks
        v = nc.vector
        link = lambda ins: self.chain.link(dve, ins)
        if s == 0:
            self.ln.dve(dve)
            dve.wait_ge(self.ssq_ready, NT)
            v.tensor_scalar(self.ssq[:, :], self.ssq[:, :], 1e-24, None, ALU.max).then_inc(self.rn_in, 1)
            dve.wait_ge(self.rn_ready, 1)
            dve.wait_ge(self.logits, 1)
            for j in range(NT):
                link(v.scalar_tensor_tensor(out=self.lg[:, j, 0:E16], in0=b[1][:, j * E16:(j + 1) * E16], scalar=self.rn[:, j:j + 1],
                                            in1=self.k.sig[:, :], op0=ALU.mult, op1=ALU.subtract))
            for j in range(NT):
                link(v.max(self.m8[:, j, :], self.lg[:, j, 0:E16]))
            link(v.tensor_scalar(self.none[:, :], self.m8[:, :, 0], 0.0, None, ALU.is_le))
            link(v.tensor_scalar(self.ngm[:, :], self.m8[:, :, 0], 0.0, -1.0, ALU.max, ALU.mult))
            v.tensor_scalar(self.gt[:, :, :], self.lg[:, :, 0:E16], 0.0, None, ALU.max).then_inc(self.gt_ready, 1)
            link(v.memset(self.m8[:, :, 2:8], SENT))
            for j in range(NT):
                link(v.match_replace(self.wk[:, j, :], self.m8[:, j, :], self.lg[:, j, :], GONE))
            link(v.tensor_scalar(self.wk[:, :, 0:E16], self.wk[:, :, 0:E16], 0.5 * (SENT + GONE), None, ALU.is_le))
            for j in range(NT):
                link(v.tensor_scalar(self.act_mask[:, j, :], self.wk[:, j, 0:E16], self.none[:, j:j + 1], None, ALU.mult))
            link(v.tensor_scalar(self.wk[:, :, 0:E16], self.lg[:, :, 0:E16], 0.0, None, ALU.is_gt))
            link(v.tensor_tensor(self.act_mask[:, :, :], self.act_mask[:, :, :], self.wk[:, :, 0:E16], ALU.max))
            dve.wait_ge(self.e_ready, 1)
            link(v.tensor_tensor(self.wt[:, :, :], self.wt[:, :, :], self.act_mask[:, :, :], ALU.mult))
            link(v.tensor_reduce(self.sum[:, :], self.wt[:, :, :], AX.X, ALU.add))
            link(v.reciprocal(self.sum[:, :], self.sum[:, :]))
            v.tensor_tensor(self.wt[:, :, :], self.wt[:, :, :], self.sum[:, :].unsqueeze(2).broadcast_to([P, NT, E16]),
                            ALU.mult).then_inc(self.wt_ready, 1)
        if s == self.steps - 2:
            dve.wait_ge(self.scores, 1)
            v.tensor_reduce(self.nmax[:, :], b[1][:, :].rearrange("p (j t) -> p j t", j=NT), AX.X, ALU.max,
                            negate=True).then_inc(self.max_ready, 1)
            dve.wait_ge(self.exp_done, NT)
            link(v.reciprocal(self.rden[:, :], self.den[:, :]))
            for j in range(NT):
                v.tensor_scalar(self.p[:, j, :], self.p[:, j, :], self.rden[:, j:j + 1], None, ALU.mult).then_inc(self.p_ready, 1)
        if s == self.steps - 1:
            dve.wait_ge(self.o_copied, 1)
            dve.wait_ge(self.v_ps, 1)
            for i in range(self.PAIRS):
                v.tensor_tensor(self.zT[:, 2 * i:2 * i + 2, :], self.wb[:, 2 * i:2 * i + 2, :],
                                self.oT[:, :].unsqueeze(1).broadcast_to([P, 2, T]), ALU.mult).then_inc(self.zo_ready, 1)
            for j in range(NT):
                dve.wait_ge(self.out_ps, j + 1)
                v.scalar_tensor_tensor(out=self.x[:, j, :], in0=b[j][:, 0:D], scalar=self.k.tg[:, self.gate:self.gate + 1],
                                       in1=self.x[:, j, :], op0=ALU.mult, op1=ALU.add).then_inc(self.x_done, 1)


class Chunk1:
    def __init__(self, k, lane, batch):
        self.k, self.batch = k, batch
        self.x, self.ctxT, self.ctx_tok = k.x[lane], k.ctxT[lane], k.ctx_tok
        self.load = k.sem("load_c1")
        b = k.psum[0:4]
        perf = Performer(k, "P", self.x, self.ctxT, self.ctx_tok, b, self.load)
        att = HeadAttention(k, "P", 0, self.x, None, b, "b")
        self.stages = [perf, att, LinearExperts(k, "P", self.x, att, b, 4)]

    def sync(self, sp):
        k, i = self.k, self.batch
        sp.dma_start(self.x[:, :, :], k.x_dram[bass.ds(i * T, T), :].rearrange("(j p) d -> p j d", p=P)).then_inc(self.load, 16)
        sp.dma_start(self.ctx_tok[:, :, :], k.ctx_dram[bass.ds(i * T, T), :].rearrange("(j p) d -> p j d", p=P)).then_inc(self.load, 16)
        sp.dma_start(self.ctxT[:, :], k.ctxT_dram[:, bass.ds(i * T, T)]).then_inc(self.load, 16)


class Chunk2:
    def __init__(self, k, lane, batch):
        self.stages = [WideAttention(k, "Q", k.x[lane], k.ctxT[lane], k.psum[4:8], 1)]

    def sync(self, sp):
        pass


class Chunk3:
    def __init__(self, k, lane, batch):
        x, b = k.x[lane], k.psum[0:4]
        self.stages = [GatedExperts(k, "P", x, b, 5), HeadAttention(k, "P", 2, x, k.ctxT[lane], b, "b", gate=2),
                       GeluExperts(k, "P", x, b, 6)]

    def sync(self, sp):
        pass


class Chunk4:
    def __init__(self, k, lane, batch):
        self.k, self.x, self.batch = k, k.x[lane], batch
        b = k.psum[4:8]
        self.mix = MixedAttention(k, "Q", self.x, b, 7)
        self.stages = [HeadAttention(k, "Q", 3, self.x, k.ctxT[lane], b, "a", topk=32, gate=3), self.mix]
        self.stored = k.sem("stored")

    def sync(self, sp):
        sp.wait_ge(self.mix.x_done, NT)
        sp.dma_start(self.k.out_dram[bass.ds(self.batch * T, T), :].rearrange("(j p) d -> p j d", p=P),
                     self.x[:, :, :]).then_inc(self.stored, 16)
        sp.wait_ge(self.stored, 16)


def steps_of(chunk):
    return [(stage, s) for stage in chunk.stages for s in range(stage.steps)]


def interleaved(chunks):
    order = []
    for n, c in enumerate(chunks):
        steps = steps_of(c)
        order += [((i + 0.5) / len(steps), n, stage, s) for i, (stage, s) in enumerate(steps)]
    return [(stage, s) for _, _, stage, s in sorted(order, key=lambda o: o[:2])]


def run_block(k, chunks):
    nc = k.nc
    steps = interleaved(chunks)
    with nc.Block() as block:
        @block.sync
        def _(sp):
            for c in chunks:
                c.sync(sp)

        @block.tensor
        def _(pe):
            for stage, s in steps:
                stage.pe(pe, s)

        @block.scalar
        def _(act):
            for stage, s in steps:
                stage.act(act, s)

        @block.vector
        def _(dve):
            for stage, s in steps:
                stage.dve(dve, s)

        @block.gpsimd
        def _(pool):
            for stage, s in steps:
                stage.pool(pool, s)
    nc.all_engine_barrier(sems_to_clear=range(k.first, k.last + 1))


def pair(k, i):
    run_block(k, [Chunk2(k, 0, i), Chunk1(k, 1, i + 1)])
    run_block(k, [Chunk2(k, 1, i + 1), Chunk3(k, 0, i)])
    run_block(k, [Chunk4(k, 0, i), Chunk3(k, 1, i + 1)])


def flamingo(nc, dram):
    with ExitStack() as ctx:
        k = Shared(nc, ctx)
        weights_in = {name: k.lasting_sem(f"{name}_in") for name, _ in PACKS}
        rows_in, all_ctx_in = k.lasting_sem("rows_in"), k.lasting_sem("all_ctx_in")
        for name, pack in PACKS:
            tile = k.sb(name, [P, cols(pack)])
            at = 0
            for what, n in pack:
                k.w[what] = tile[:, at:at + n]
                at += n
        row = k.sb("rows", [1, cols(ROWS)])
        at = 0
        for what, n in ROWS:
            k.w[what] = row[:, at:at + n]
            at += n
        for what, names in BELOW.items():
            for i, name in enumerate(names):
                k.w[name] = k.w[what][32 * (i + 1):32 * (i + 1) + 1, :]
        k.x_dram, k.ctx_dram, k.ctxT_dram, k.out_dram = dram["x"], dram["ctx"], dram["ctxT"], dram["out"]
        k.x = [k.sb(f"x{i}", [P, NT, D]) for i in range(2)]
        k.ctxT = [k.sb(f"ctxT{i}", [P, T]) for i in range(2)]
        k.ctx_tok = k.sb("ctx_tok", [P, NT, D])
        k.half, k.tg, k.kbias = k.sb("minus_half", [P, E16]), k.sb("tanh_g", [P, 8]), k.sb("k_stab", [P, 1])
        k.sn, k.sig = k.sb("sim_unit", [P, E16]), k.sb("sigmoid_gates", [P, E16])
        k.bq_scaled = {f"bq{L}": k.sb(f"bq{L}_scaled", [P, NG]) for L in (0, 2, 3)}

        all_ctx, sq = k.sb("mix_wb", [P, E16, T]), Workspace(k, "Q").whole
        ctx16, sq16 = all_ctx[:, 0:8, :].rearrange("p a b -> p (a b)"), sq[:, 0:8, :].rearrange("p a b -> p (a b)")
        head_sq, least = Workspace(k, "P").p[:, 0, 0, :], k.sb("setup_least", [P, 1])
        least1, simsq, simn = k.sb("setup_least1", [1, 1]), k.sb("setup_simsq", [P, E16]), k.sb("setup_simn", [P, E16])
        th = k.sb("setup_tanh", [P, E16])
        setup = ctx.enter_context(ExitStack())
        setup_sems = {n: setup.enter_context(nc.semaphore(f"setup_{n}")) for n in (
            "preset", "dve", "least", "least_row", "least1", "least_bc", "g_ps", "gates_ps", "gates_th", "simsq", "sim_ps",
            "simn_in", "simn")}
        preset, chain = setup_sems["preset"], Chain(setup_sems["dve"])
        least_ready, least_row, least1_ready, least_bc = (setup_sems[n] for n in ("least", "least_row", "least1", "least_bc"))
        g_ps, gates_ps, gates_th, simsq_ready, sim_ps, simn_in, simn_ready = (
            setup_sems[n] for n in ("g_ps", "gates_ps", "gates_th", "simsq", "sim_ps", "simn_in", "simn"))
        lg, prP = k.sb("mix_lg", [P, NT, E16 + 6]), k.sb("rt_prP", [P, NT, E8 + 6])
        combP = k.sb("rt_combP", [P, NT, E8 + 1])
        heads_v = [k.sb(n, [P, NT, H, PAD]) for n in ("att_vP", "att_vQ")]
        wide_v = k.sb("wide_v", [P, NT, H1, HD1 + 1])
        with nc.Block() as block:
            @block.sync
            def _(sp):
                sp.dma_start(ctx16, dram["ctx"].rearrange("(p n) d -> p (n d)", p=P)).then_inc(all_ctx_in, 16)
                sp.dma_start(row[:, :], dram["rows"]).then_inc(rows_in, 16)
                for name, pack in PACKS:
                    sp.dma_start(k.bufs[name][:, :], dram[name]).then_inc(weights_in[name], 16)
                for name, pack in PACKS:
                    sp.wait_ge(weights_in[name], 16)

            @block.gpsimd
            def _(pool):
                nc.gpsimd.memset(k.half[:, :], -0.5).then_inc(preset, 1)
                nc.gpsimd.memset(lg[:, :, E16:], SENT).then_inc(preset, 1)
                nc.gpsimd.memset(prP[:, :, E8:], SENT).then_inc(preset, 1)
                nc.gpsimd.memset(combP[:, :, E8:], 1.0).then_inc(preset, 1)
                for n, v in enumerate(heads_v):
                    nc.gpsimd.memset(v[:, :, :, HD:HD + 1], 1.0).then_inc(preset, 1)
                    nc.gpsimd.memset(v[:, :, :, HD + 1:], 0.0).then_inc(preset, 1)
                nc.gpsimd.memset(wide_v[:, :, :, HD1:], 1.0).then_inc(preset, 1)
                pool.wait_ge(preset, 1)
                pool.wait_ge(simn_in, 1)
                nc.gpsimd.tensor_tensor(simn[:, :], simsq[:, :], k.half[:, :], ALU.pow).then_inc(simn_ready, 1)

            @block.vector
            def _(dve):
                v = nc.vector
                dve.wait_ge(all_ctx_in, 16)
                chain.link(dve, v.tensor_tensor(sq16, ctx16, ctx16, ALU.mult))
                chain.link(dve, v.tensor_reduce(head_sq, sq16.rearrange("p (n d) -> p n d", d=HD), AX.X, ALU.add))
                v.tensor_reduce(least[:, :], head_sq, AX.X, ALU.min).then_inc(least_ready, 1)
                dve.wait_ge(least_row, 1)
                v.tensor_reduce(least1[:, :], k.psum[0][0:1, 0:P], AX.X, ALU.min).then_inc(least1_ready, 1)
                dve.wait_ge(least_bc, 1)
                v.tensor_scalar(k.kbias[:, :], k.psum[1][:, 0:1], 0.5 * RF_SCALE ** 2, None, ALU.mult)
                dve.wait_ge(weights_in["pack4"], 16)
                v.tensor_tensor(simsq[:, :], k.w["sim"], k.w["sim"], ALU.mult).then_inc(simsq_ready, 1)
                dve.wait_ge(sim_ps, 1)
                v.tensor_scalar(simsq[:, :], k.psum[4][:, 0:E16], 1e-24, None, ALU.max).then_inc(simn_in, 1)
                dve.wait_ge(simn_ready, 1)
                v.tensor_tensor(k.sn[:, :], k.w["sim"], simn[:, :], ALU.mult)
                dve.wait_ge(gates_th, 1)
                v.tensor_scalar(k.sig[:, :], th[:, :], 0.5, 0.5, ALU.mult, ALU.add)
                for L, name in ((0, "pack1"), (2, "pack3"), (3, "pack4")):
                    dve.wait_ge(weights_in[name], 16)
                    v.tensor_scalar(k.bq_scaled[f"bq{L}"][:, :], k.w[f"bq{L}"], HD ** -0.5, None, ALU.mult)

            @block.tensor
            def _(pe):
                pe.wait_ge(weights_in["const"], 16)
                pe.wait_ge(least_ready, 1)
                nc.tensor.transpose(k.psum[0][0:1, 0:P], least[:, :], k.w["ident"]).then_inc(least_row, 1)
                pe.wait_ge(least1_ready, 1)
                nc.tensor.matmul(k.psum[1][:, 0:1], k.w["ones"][0:1, :], least1[:, :], start=True, stop=True).then_inc(least_bc, 1)
                pe.wait_ge(rows_in, 16)
                nc.tensor.matmul(k.psum[2][:, 0:8], k.w["ones"][0:1, :], k.w["g"], start=True, stop=True).then_inc(g_ps, 1)
                nc.tensor.matmul(k.psum[3][:, 0:E16], k.w["ones"][0:1, :], k.w["gates"], start=True, stop=True).then_inc(gates_ps, 1)
                pe.wait_ge(simsq_ready, 1)
                nc.tensor.matmul(k.psum[4][:, 0:E16], k.w["ones"], simsq[:, :], start=True, stop=True).then_inc(sim_ps, 1)

            @block.scalar
            def _(act):
                act.wait_ge(g_ps, 1)
                nc.scalar.activation(k.tg[:, :], k.psum[2][:, 0:8], ACT.Tanh)
                act.wait_ge(gates_ps, 1)
                nc.scalar.activation(th[:, :], k.psum[3][:, 0:E16], ACT.Tanh, scale=0.5).then_inc(gates_th, 1)
        numbers = [q.num for q in setup_sems.values()]
        nc.all_engine_barrier(sems_to_clear=range(min(numbers), max(numbers) + 1))
        setup.close()
        for make in (Chunk1, Chunk2, Chunk3, Chunk4):
            make(k, 0, 0)

        run_block(k, [Chunk1(k, 0, 0)])
        with nc.Fori(0, NB - 2, 2) as i:
            pair(k, i)
            run_block(k, [Chunk1(k, 0, i + 2), Chunk4(k, 1, i + 1)])
        pair(k, NB - 2)
        run_block(k, [Chunk4(k, 1, NB - 1)])


def kernel(**inputs):
    import concourse.bacc as bacc
    from concourse.bass_utils import run_bass_kernel_spmd

    a = {n: np.asarray(v) for n, v in inputs.items()}
    f = np.float32

    def heads_apart(w):
        out = np.zeros((D, NG, HG, PAD), f)
        out[..., :HD] = w.reshape(D, NG, HG, HD)
        return out.reshape(D, NG * P)

    def bias_apart(b):
        out = np.zeros((HG, PAD, NG), f)
        out[:, :HD] = b.reshape(NG, HG, HD).transpose(1, 2, 0)
        return out.reshape(P, NG)

    def with_rows_below(b, rows):
        out = np.zeros((P, D), f)
        out[:b.shape[0]] = b
        for i, row in enumerate(rows):
            out[32 * (i + 1)] = row
        return out

    def side_by_side(w):
        return w.transpose(1, 0, 2).reshape(w.shape[1], -1)

    rf = np.zeros((NG, HG, HD, NG, HG, PAD), f)
    hsum = np.zeros((NG, HG, HD, NG, HG, PAD), f)
    for g in range(NG):
        for h in range(HG):
            rf[g, h, :, g, h, :] = a["L0_xattn_random_features"]
            hsum[g, h, :, g, h, :] = -0.5 * RF_SCALE
    w_qkv, b_qkv = a["L0_ffn_W_qkv"], a["L0_ffn_b_qkv"]
    parts = {
        "ident": np.eye(P, dtype=f), "tri": np.triu(np.ones((P, P), f)), "ones": np.ones((P, P), f),
        "hsum": hsum.reshape(D, -1),
        "rf": rf.reshape(D, -1), "wq0": heads_apart(w_qkv[:, 0:D]), "wk0": heads_apart(w_qkv[:, D:2 * D]),
        "wv0": w_qkv[:, 2 * D:], "gate0": a["L0_ffn_W_gate"], "exp0": side_by_side(a["L0_ffn_W_experts"]),
        "bq0": bias_apart(b_qkv[0:D]), "bk0": bias_apart(b_qkv[D:2 * D]), 
        "wq1": a["L1_xattn_Wq"], "wk1": a["L1_xattn_Wkv"][:, :H1 * HD1], "wv1": a["L1_xattn_Wkv"][:, H1 * HD1:],
        "wo1": side_by_side(a["L1_xattn_Wout"].reshape(4, P, D)),
        "router1": a["L1_ffn_w_router"], "fc1": side_by_side(a["L1_ffn_fc1_w"]), "fc2": side_by_side(a["L1_ffn_fc2_w"]),
        "gate_w": a["L1_ffn_gate_w"], "up_w": a["L1_ffn_up_w"], "down_w": side_by_side(a["L1_ffn_down_w"].reshape(2, P, D)),
        "router2": a["L2_ffn_router_w"],
        "b1": np.concatenate([a["L2_ffn_shared_b1"].reshape(1, FF2, P), a["L2_ffn_exp_b1"].reshape(E8, FF2, P)]).transpose(2, 0, 1).reshape(P, -1),
        "w1": side_by_side(np.concatenate([a["L2_ffn_shared_w1"].reshape(1, D, -1), a["L2_ffn_exp_w1"]])),
        "w2": side_by_side(np.concatenate([a["L2_ffn_shared_w2"].reshape(FF2, P, D), a["L2_ffn_exp_w2"].reshape(E8 * FF2, P, D)])),
        "sim": a["L3_ffn_sim_matrix"],
        "qp": side_by_side(a["L3_ffn_q_proj"]), "kp": side_by_side(a["L3_ffn_k_proj"]),
        "vp": side_by_side(a["L3_ffn_v_proj"]), "op": side_by_side(a["L3_ffn_o_proj"]),
        "bv0": b_qkv[2 * D:], "bgate0": a["L0_ffn_b_gate"], "bout1": a["L1_xattn_bout"], "br2": a["L2_ffn_router_b"],
        "gates": a["L3_ffn_gates"], "g": np.concatenate([a["g_xattn"], a["g_ffn"]]),
    }
    for L in (2, 3):
        parts[f"wq{L}"], parts[f"wk{L}"] = (heads_apart(a[f"L{L}_xattn_W{c}"].T) for c in "qk")
        parts[f"wv{L}"], parts[f"wo{L}"] = (a[f"L{L}_xattn_W{c}"].T for c in "vo")
        parts[f"bq{L}"], parts[f"bk{L}"] = (bias_apart(a[f"L{L}_xattn_b{c}"]) for c in "qk")
        parts[f"bv{L}"], parts[f"bo{L}"] = (a[f"L{L}_xattn_b{c}"] for c in "vo")
    parts["bias0"] = with_rows_below(a["L0_ffn_b_experts"], [parts[n] for n in BELOW["bias0"]])
    parts["bias2"] = with_rows_below(np.concatenate([a["L2_ffn_exp_b2"], a["L2_ffn_shared_b2"].reshape(1, D)]),
                                     [parts[n] for n in BELOW["bias2"]])
    ctx2d = a["ctx_1024"].reshape(NB * T, D)
    arrays = {name: np.concatenate([parts[n] for n, _ in pack], axis=1) for name, pack in PACKS}
    arrays["rows"] = np.concatenate([parts[n] for n, _ in ROWS]).reshape(1, -1)
    arrays["x"], arrays["ctx"], arrays["ctxT"] = a["x"].reshape(NB * T, D), ctx2d, ctx2d.T
    arrays = {f"in_{n}": np.ascontiguousarray(v) for n, v in arrays.items()}

    nc = bacc.Bacc("TRN2", target_bir_lowering=False, num_devices=1)
    dram = {n[3:]: nc.dram_tensor(n, v.shape, F32, kind="ExternalInput").ap() for n, v in arrays.items()}
    dram["out"] = nc.dram_tensor("out_x", (NB * T, D), F32, kind="ExternalOutput").ap()
    flamingo(nc, dram)
    r = run_bass_kernel_spmd(nc, [arrays], core_ids=[0])
    return r.results[0]["out_x"].reshape(NB, T, D)
```

```python
from contextlib import ExitStack

import numpy as np
import concourse.bass as bass
from concourse import mybir

F32 = mybir.dt.float32
ACT = mybir.ActivationFunctionType
ALU = mybir.AluOpType
AX = mybir.AxisListType

NB, T, D = 8, 256, 128
P = 128
NT = T // P
H, HD = 16, 8
PAD = 32
HG = P // PAD
NG = H // HG
M_RF = 32
H1, HD1 = 8, 64
E8, E16 = 8, 16
FF2 = 4
SENT, GONE = -1.0e38, -3.0e38
RF_SCALE = float(D) ** -0.25

CONST = [("ident", 128), ("tri", 128), ("ones", 128), ("hsum", NG * 128), ("head_rows", H), ("group_rows", HG)]
PACK1 = [("rf", NG * 128), ("wq0", D), ("wk0", D), ("wv0", 128), ("gate0", E8), ("exp0", E8 * D),
         ("bq0", 1), ("bk0", 1), ("bias0", D)]
PACK2 = [("wq1", H1 * HD1), ("wk1", H1 * HD1), ("wv1", H1 * HD1), ("wo1", 4 * D)]
PACK3 = [("router1", E8), ("fc1", E8 * 2 * D), ("fc2", E8 * D), ("gate_w", 2 * D), ("up_w", 2 * D), ("down_w", 2 * D),
         ("wq2", D), ("wk2", D), ("wv2", 128), ("wo2", 128), ("bq2", 1), ("bk2", 1),
         ("router2", E8), ("b1", (E8 + 1) * FF2), ("bias2", D)]
PACK3W = [("w1", (E8 + 1) * FF2 * 128), ("w2", (E8 + 1) * FF2 * 128)]
PACK4 = [("wq3", D), ("wk3", D), ("wv3", 128), ("wo3", 128), ("bq3", 1), ("bk3", 1), ("sim", E16)]
PACK4W = [("qp", E16 * D), ("kp", E16 * D), ("vp", E16 * D), ("op", E16 * D)]
ROWS = [("bgate0", E8), ("br2", E8), ("gates", E16), ("g", 8)]
BELOW = {"bias0": ["bv0", "bout1", "bv2"], "bias2": ["bo2", "bv3", "bo3"]}
PACKS = [("const", CONST), ("pack1", PACK1), ("pack2", PACK2), ("pack3", PACK3), ("pack3w", PACK3W),
         ("pack4", PACK4), ("pack4w", PACK4W)]


def cols(pack):
    return sum(n for _, n in pack)


class Chain:

    def __init__(self, sem):
        self.sem, self.n = sem, 0

    def link(self, eng, ins):
        self.n += 1
        ins.then_inc(self.sem, 1)
        eng.wait_ge(self.sem, self.n)


class Shared:

    def __init__(self, nc, ctx):
        self.nc, self.ctx = nc, ctx
        self.sems, self.bufs, self.w = {}, {}, {}
        self.first = self.last = None
        self.psum = [ctx.enter_context(nc.psum_tensor(f"bank{i}", [P, 512], F32)) for i in range(8)]

    def sb(self, name, shape):
        if name not in self.bufs:
            self.bufs[name] = self.ctx.enter_context(self.nc.sbuf_tensor(name, shape, F32))
        return self.bufs[name]

    def one(self, name):
        r = max((32 * (names.index(name) + 1) for names in BELOW.values() if name in names), default=0)
        return self.w["ones"][r:r + 1, :]

    def lasting_sem(self, name):
        return self.ctx.enter_context(self.nc.semaphore(name))

    def sem(self, name):
        if name not in self.sems:
            s = self.ctx.enter_context(self.nc.semaphore(name))
            self.first = s.num if self.first is None else min(self.first, s.num)
            self.last = s.num if self.last is None else max(self.last, s.num)
            self.sems[name] = s
        return self.sems[name]


class Workspace:

    def __init__(self, k, side):
        self.whole = k.sb(f"work{side}", [P, 4 * NG, T])
        self.kT, self.qT, self.oT, self.extra = (self.whole[:, i * NG:(i + 1) * NG, :] for i in range(4))
        self.work = self.extra.rearrange("p (u j) t -> p u j t", j=NT)
        self.v = k.sb(f"att_v{side}", [P, NT, H, PAD])
        self.p, self.pT = k.sb(f"att_p{side}", [P, 2, NT, T])[:, :, :, :], k.sb(f"att_pT{side}", [P, 2, NT, T])[:, :, :, :]


class Units:

    def units(self, first, count, rounds, tail, closing, weights):
        self.first, self.count, self.rounds, self.weights = first, count, rounds, weights
        self.closing_from = first + count * rounds + tail
        self.steps = self.closing_from + closing

    def at(self, s, lag, r):
        u, rest = divmod(s - self.first - r, self.rounds)
        return u - lag if s >= self.first and rest == 0 and 0 <= u - lag < self.count else -1

    def close(self, s):
        return s - self.closing_from if s >= self.closing_from else -1

    def weight(self, s):
        return self.weights[0 if s < self.first else 2 if s >= self.closing_from else 1]


class TopSelect(Units):
    OPS = 4

    def top_buffers(self, k, buf, n):
        self.work, self.rest = buf.work, k.sb("top_rest", [P, NT, T])
        self.lead, self.eight = k.sb("top_lead", [P, 2, NT, 8]), k.sb("top_eight", [P, NT, 8])
        self.top, self.rest_done = k.sem(n + "top"), k.sem(n + "rest")
        self.topn = 0

    def top_count(self, u, r):
        return self.OPS * (u * self.rounds + r + 1)

    def select(self, dve, u, r):
        nc, sc = self.k.nc, self.banks[u % 2]
        if r == 0:
            dve.wait_ge(self.scores, u + 1)
            if u >= 2:
                dve.wait_ge(self.rest_done, u - 1)
        for replace in range(2):
            for j in range(NT):
                if self.topn >= 2:
                    dve.wait_ge(self.top, self.topn - 1)
                src = sc[:, j * T:(j + 1) * T] if r == 0 else self.work[:, u % 2, j, :]
                eight = self.lead[:, u % 2, j, :] if r == 0 else self.eight[:, j, :]
                if replace:
                    ins = nc.vector.match_replace(self.work[:, u % 2, j, :], eight, src, GONE)
                else:
                    ins = nc.vector.max(eight, src)
                ins.then_inc(self.top, 1)
                self.topn += 1

    def negative_max(self, pool, u):
        pool.wait_ge(self.top, self.top_count(u, 0) - NT)
        self.k.nc.gpsimd.tensor_scalar(self.nmax[:, u, :], self.lead[:, u % 2, :, 0], -1.0, 1.0, ALU.mult,
                                       ALU.mult).then_inc(self.max_ready, 1)

    def exp_scores(self, act, u):
        act.wait_ge(self.max_ready, u + 1)
        if self.topk:
            act.wait_ge(self.top, self.top_count(u, 0))
        if u >= 2:
            act.wait_ge(self.pT_ps, u - 1)
        for j in range(NT):
            e = self.k.nc.scalar.activation(self.p[:, u % 2, j, :], self.banks[u % 2][:, j * T:(j + 1) * T], ACT.Exp,
                                            bias=self.nmax[:, u, j:j + 1])
        e.then_inc(self.exp_done, 1)

    def exp_rest(self, act, u):
        act.wait_ge(self.top, self.top_count(u, self.rounds - 1))
        if u >= 1:
            act.wait_ge(self.p_ready, u)
        for j in range(NT):
            e = self.k.nc.scalar.activation(self.rest[:, j, :], self.work[:, u % 2, j, :], ACT.Exp, bias=self.nmax[:, u, j:j + 1])
        e.then_inc(self.rest_done, 1)

    def keep_top(self, pool, u):
        pool.wait_ge(self.rest_done, u + 1)
        v = self.p[:, u % 2, :, :]
        self.k.nc.gpsimd.tensor_tensor(v, v, self.rest[:, :, :], ALU.subtract).then_inc(self.p_ready, 1)

    def turn_p(self, pe, u):
        pe.wait_ge(self.p_ready, u + 1)
        if u >= 1:
            pe.wait_ge(self.pT_copied, u)
        for kt in range(NT):
            for j in range(NT):
                tr = self.k.nc.tensor.transpose(self.banks[2][:, kt * T + j * P:kt * T + (j + 1) * P],
                                                self.p[:, u % 2, j, kt * P:(kt + 1) * P], self.k.w["ident"])
        tr.then_inc(self.pT_ps, 1)

    def copy_pT(self, act, u):
        act.wait_ge(self.pT_ps, u + 1)
        if u >= 2:
            act.wait_ge(self.pv_done, u - 1)
        self.k.nc.scalar.activation(self.pT[:, u % 2, :, :], self.banks[2][:, :], ACT.Copy).then_inc(self.pT_copied, 1)


class LayerNorm:

    def __init__(self, k, side, tag, x, bank):
        self.k, self.x, self.bank = k, x, bank
        self.y, self.yT = k.sb(f"y{side}", [P, NT, D]), k.sb(f"yT{side}", [P, T])
        self.stats, self.mv = k.sb(f"ln_stats{side}", [P, NT, 6]), k.sb(f"ln_mv{side}", [P, NT, 2])
        self.var, self.rstd = k.sb(f"ln_var{side}", [P, NT]), k.sb(f"ln_rstd{side}", [P, NT])
        n = f"ln{side}{tag}_"
        self.chain = Chain(k.sem(n + "dve"))
        self.var_ready, self.rstd_ready = k.sem(n + "var_ready"), k.sem(n + "rstd_ready")
        self.y_ready, self.turned, self.yT_ready = k.sem(n + "y_ready"), k.sem(n + "turned"), k.sem(n + "yT_ready")

    def dve_stats(self, dve):
        nc = self.k.nc
        for j in range(NT):
            self.chain.link(dve, nc.vector.bn_stats(self.stats[:, j, :], self.x[:, j, :]))
            self.chain.link(dve, nc.vector.bn_aggr(self.mv[:, j, :], self.stats[:, j, :]))
        nc.vector.tensor_scalar(self.var[:, :], self.mv[:, :, 1], 1e-5, None, ALU.add).then_inc(self.var_ready, 1)

    def dve_scale(self, dve):
        dve.wait_ge(self.rstd_ready, 1)
        for j in range(NT):
            self.k.nc.vector.tensor_scalar(self.y[:, j, :], self.x[:, j, :], self.mv[:, j, 0:1], self.rstd[:, j:j + 1],
                                           ALU.subtract, ALU.mult).then_inc(self.y_ready, 1)

    def pool(self, pool):
        pool.wait_ge(self.var_ready, 1)
        self.k.nc.gpsimd.tensor_tensor(self.rstd[:, :], self.var[:, :], self.k.half[:, 0:NT],
                                       ALU.pow).then_inc(self.rstd_ready, 1)

    def pe(self, pe):
        for j in range(NT):
            pe.wait_ge(self.y_ready, j + 1)
            self.k.nc.tensor.transpose(self.bank[:, j * P:(j + 1) * P], self.y[:, j, :],
                                       self.k.w["ident"]).then_inc(self.turned, 1)

    def act(self, act):
        act.wait_ge(self.turned, NT)
        self.k.nc.scalar.activation(self.yT[:, :], self.bank[:, 0:T], ACT.Copy).then_inc(self.yT_ready, 1)


class Performer(Units):
    RING = 4

    def __init__(self, k, side, x, ctxT, ctx_tok, banks, load, before):
        self.k, self.x, self.ctxT, self.ctx_tok, self.banks, self.load = k, x, ctxT, ctx_tok, banks, load
        self.before = before
        self.ln = LayerNorm(k, side, "a", x, banks[0])
        work = Workspace(k, side)
        self.ksq = work.pT[:, 0, 0, :]
        self.qf, self.kf, self.q1 = work.qT, work.kT, work.extra
        self.v = work.v
        self.a = work.p.rearrange("p u j t -> p u (j t)")[:, :, 0:3 * P]
        self.oT = work.oT
        self.den, self.tiny, self.o = k.sb("perf_den", [P, H]), k.sb("perf_tiny", [P, H]), self.ln.y
        n = "perf_"
        self.chain = Chain(k.sem(n + "dve"))
        self.ksq_ready, self.v_ready = k.sem(n + "ksq_ready"), k.sem(n + "v_ready")
        self.proj_ready, self.exp_ready, self.kf_ready = k.sem(n + "proj"), k.sem(n + "exp"), k.sem(n + "kf")
        self.q1_ready = k.sem(n + "q1")
        self.a_ps, self.a_copied, self.a_masked = k.sem(n + "a_ps"), k.sem(n + "a_copied"), k.sem(n + "a_masked")
        self.pv_done, self.oT_copied, self.back = k.sem(n + "pv"), k.sem(n + "oT"), k.sem(n + "back")
        self.units(3, H, 1, 3, 3, (2.0, 1.2, 1.5))

    def pe(self, pe, s):
        nc, w, b = self.k.nc, self.k.w, self.banks
        if s == 0:
            pe.wait_ge(self.load, 3 * 16)
            pe.wait_ge(self.ksq_ready, 1)
            for g in range(NG):
                out = b[2 + g // 2][:, (g % 2) * T:(g % 2 + 1) * T]
                nc.tensor.matmul(out, w["rf"][:, g * P:(g + 1) * P], self.ctxT[:, :], start=True, stop=False)
                nc.tensor.matmul(out, w["hsum"][:, g * P:(g + 1) * P], self.ksq, start=False,
                                 stop=True).then_inc(self.proj_ready, 1)
        if s == 1:
            self.ln.pe(pe)
        if s == 2:
            pe.wait_ge(self.ln.yT_ready, 1)
            for g in range(NG):
                nc.tensor.matmul(b[g // 2][:, (g % 2) * T:(g % 2 + 1) * T], w["rf"][:, g * P:(g + 1) * P], self.ln.yT[:, :],
                                 start=True, stop=True).then_inc(self.proj_ready, 1)
        u = self.at(s, 0, 0)
        if u >= 0:
            if u == 0:
                pe.wait_ge(self.kf_ready, 2)
                pe.wait_ge(self.exp_ready, 4)
            pe.wait_ge(self.q1_ready, u + 1)
            if u >= 2:
                pe.wait_ge(self.a_copied, u - 1)
            out, kf, q1 = b[u % 2], self.kf[:, u // HG, :], self.q1[:, u % self.RING, :]
            nc.tensor.matmul(out[:, 0:T], kf[:, 0:P], q1, start=True, stop=True)
            nc.tensor.matmul(out[:, T:T + P], kf[:, P:T], q1[:, P:T], start=True, stop=True).then_inc(self.a_ps, 1)
        u = self.at(s, 3, 0)
        if u >= 0:
            g, a = divmod(u, HG)
            pe.wait_ge(self.a_masked, u + 1)
            if u == 0:
                pe.wait_ge(self.v_ready, 1)
            if a == 0 and g > 0:
                pe.wait_ge(self.oT_copied, g)
            out = b[2][PAD * a:PAD * (a + 1), (g % 2) * T:(g % 2 + 1) * T]
            nc.tensor.matmul(out, self.v[:, 0, u, :], self.a[:, u % 2, 0:T], start=True, stop=False)
            nc.tensor.matmul(out[:, P:T], self.v[:, 1, u, :], self.a[:, u % 2, T:T + P], start=False,
                             stop=True).then_inc(self.pv_done, 1)
        if self.close(s) == 0:
            pe.wait_ge(self.oT_copied, NG)
            for j in range(NT):
                for g in range(NG):
                    nc.tensor.transpose(b[j][:, g * P:(g + 1) * P], self.oT[:, g, j * P:(j + 1) * P],
                                        w["ident"]).then_inc(self.back, 1)

    def act(self, act, s):
        nc, b = self.k.nc, self.banks
        if s == 1:
            self.ln.act(act)
            for half in range(2):
                act.wait_ge(self.proj_ready, 2 * half + 2)
                nc.scalar.activation(self.kf[:, 2 * half:2 * half + 2, :], b[2 + half][:, :], ACT.Exp, bias=self.k.kbias[:, 0:1],
                                     scale=RF_SCALE).then_inc(self.exp_ready, 1)
        if s == 2:
            for half in range(2):
                act.wait_ge(self.proj_ready, NG + 2 * half + 2)
                nc.scalar.activation(self.qf[:, 2 * half:2 * half + 2, :], b[half][:, :], ACT.Exp,
                                     scale=RF_SCALE).then_inc(self.exp_ready, 1)
        u = self.at(s, 1, 0)
        if u >= 0:
            act.wait_ge(self.a_ps, u + 1)
            if u >= 2:
                act.wait_ge(self.pv_done, u - 1)
            nc.scalar.activation(self.a[:, u % 2, :], b[u % 2][:, 0:3 * P], ACT.Copy).then_inc(self.a_copied, 1)
        u = self.at(s, 3, 0)
        if u >= 0 and u % HG == HG - 1:
            g = u // HG
            act.wait_ge(self.pv_done, u + 1)
            nc.scalar.activation(self.oT[:, g, :], b[2][:, (g % 2) * T:(g % 2 + 1) * T], ACT.Copy).then_inc(self.oT_copied, 1)

    def pool_q1(self, pool, u):
        if u >= self.RING:
            pool.wait_ge(self.a_ps, u - self.RING + 1)
        g, a = divmod(u, HG)
        self.k.nc.gpsimd.tensor_scalar(self.q1[:, u % self.RING, :], self.qf[:, g, :], 1e-4,
                                       self.k.w["group_rows"][:, a:a + 1], ALU.add, ALU.mult).then_inc(self.q1_ready, 1)

    def pool(self, pool, s):
        nc = self.k.nc
        if s == 0:
            if self.before is not None:
                pool.wait_ge(self.before.x_done, NT)
            self.ln.pool(pool)
            pool.wait_ge(self.load, 3 * 16)
            nc.gpsimd.tensor_tensor(self.ksq, self.ctxT[:, :], self.ctxT[:, :], ALU.mult).then_inc(self.ksq_ready, 1)
            nc.gpsimd.tensor_copy(self.v[:, :, :, 0:HD],
                                  self.ctx_tok[:, :, :].rearrange("p j (h d) -> p j h d", d=HD)).then_inc(self.v_ready, 1)
        if s == 2:
            for half in range(2):
                pool.wait_ge(self.exp_ready, half + 1)
                v = self.kf[:, 2 * half:2 * half + 2, :]
                nc.gpsimd.tensor_scalar(v, v, 1e-4, 1.0, ALU.add, ALU.mult).then_inc(self.kf_ready, 1)
            pool.wait_ge(self.exp_ready, 4)
            for u in range(2):
                self.pool_q1(pool, u)
        u = self.at(s, 0, 0) + 2
        if 2 <= u < H:
            self.pool_q1(pool, u)
        u = self.at(s, 2, 0)
        if u >= 0:
            pool.wait_ge(self.a_copied, u + 1)
            v = self.a[:, u % 2, :].rearrange("p (b t) -> p b t", t=P)[:, 0:3:2, :]
            nc.gpsimd.tensor_tensor(v, v, self.k.w["tri"].unsqueeze(1).broadcast_to([P, 2, P]),
                                    ALU.mult).then_inc(self.a_masked, 1)

    def dve(self, dve, s):
        nc = self.k.nc
        if s == 0:
            dve.wait_ge(self.load, 3 * 16)
            self.ln.dve_stats(dve)
        if s == 1:
            self.ln.dve_scale(dve)
        j = self.close(s) - 1
        if j >= 0:
            link = lambda ins: self.chain.link(dve, ins)
            dve.wait_ge(self.back, (j + 1) * NG)
            t = self.banks[j][:, :].rearrange("p (h c) -> p h c", c=PAD)
            link(nc.vector.tensor_scalar(self.den[:, :], t[:, :, HD], 1.0 / M_RF, None, ALU.mult))
            link(nc.vector.tensor_scalar(self.tiny[:, :], self.den[:, :], 1e-6, 2e-6, ALU.is_le, ALU.mult))
            link(nc.vector.tensor_tensor(self.den[:, :], self.den[:, :], self.tiny[:, :], ALU.add))
            link(nc.vector.reciprocal(self.den[:, :], self.den[:, :]))
            link(nc.vector.scalar_tensor_tensor(out=self.o[:, j, :].rearrange("p (h d) -> p h d", d=HD), in0=t[:, :, 0:HD],
                                                scalar=1.0 / M_RF, in1=self.den[:, :].unsqueeze(2).broadcast_to([P, H, HD]),
                                                op0=ALU.mult, op1=ALU.mult))
            if j == NT - 1:
                link(nc.vector.scalar_tensor_tensor(out=self.x[:, :, :], in0=self.o[:, :, :], scalar=self.k.tg[:, 0:1],
                                                    in1=self.x[:, :, :], op0=ALU.mult, op1=ALU.add))


class HeadAttention(TopSelect):

    RING = 4

    def __init__(self, k, side, layer, x, ctxT, banks, tag, topk=0, gate=None):
        self.k, self.x, self.banks, self.topk, self.layer, self.gate = k, x, banks, topk, layer, gate
        self.ln = LayerNorm(k, side, tag, x, banks[0])
        self.kvT = self.ln.yT if ctxT is None else ctxT
        buf = Workspace(k, side)
        self.kT, self.qT, self.q1 = buf.kT[:, 0, :], buf.kT[:, 1, :], buf.qT
        self.v, self.p, self.pT, self.oT = buf.v, buf.p, buf.pT, buf.oT
        self.nmax = k.sb(f"att_nmax{side}", [P, H, NT])
        self.rden, self.o = k.sb(f"att_rden{side}", [P, NT, H]), self.ln.y
        self.otT = self.ln.yT
        n = f"att{side}_"
        self.chain = Chain(k.sem(n + "dve"))
        self.proj, self.proj_copied = k.sem(n + "proj"), k.sem(n + "proj_copied")
        self.scores, self.max_ready, self.exp_done = k.sem(n + "scores"), k.sem(n + "max"), k.sem(n + "exp")
        self.pT_ps, self.pT_copied = k.sem(n + "pT_ps"), k.sem(n + "pT")
        self.pv_done, self.oT_copied, self.back = k.sem(n + "pv"), k.sem(n + "oT"), k.sem(n + "back")
        self.o_ready, self.o_turned, self.otT_ready = k.sem(n + "o"), k.sem(n + "o_turned"), k.sem(n + "otT")
        self.out_ps, self.q1_ready = k.sem(n + "out"), k.sem(n + "q1")
        closing = 2 if gate is None else 4
        if topk:
            self.top_buffers(k, buf, n)
            self.p_ready = k.sem(n + "p")
            self.units(3, H, topk // 8, 4, closing, (2.0, 1.4, 1.4))
            self.EXP, self.TURN, self.COPY, self.PV = (0, 1), (1, 2), (1, 2), (1, 3)
        else:
            self.p_ready = self.exp_done
            self.units(3, H, 1, 3, closing, (2.0, 2.2, 1.4))
            self.EXP, self.TURN, self.COPY, self.PV = (1, 0), (2, 0), (2, 0), (3, 0)

    def score(self, pe, u):
        if u == 0:
            pe.wait_ge(self.proj_copied, 3)
        pe.wait_ge(self.q1_ready, u + 1)
        if u >= 2:
            pe.wait_ge(self.exp_done, u - 1)
        for j in range(NT):
            mm = self.k.nc.tensor.matmul(self.banks[u % 2][:, j * T:(j + 1) * T], self.q1[:, u % self.RING, j * P:(j + 1) * P],
                                         self.kT, start=True, stop=True)
        mm.then_inc(self.scores, 1)

    def pe(self, pe, s):
        nc, w, b, L = self.k.nc, self.k.w, self.banks, self.layer
        if s == 1:
            self.ln.pe(pe)
        if s == 2:
            pe.wait_ge(self.ln.yT_ready, 1)
            nc.tensor.matmul(b[2][:, 0:T], w[f"wk{L}"], self.kvT[:, :], start=True, stop=True).then_inc(self.proj, 1)
            nc.tensor.matmul(b[3][:, 0:T], w[f"wq{L}"], self.ln.yT[:, :], start=True, stop=True).then_inc(self.proj, 1)
            for j in range(NT):
                out = b[1][:, j * D:(j + 1) * D]
                nc.tensor.matmul(out, self.kvT[:, j * P:(j + 1) * P], w[f"wv{L}"], start=True, stop=False)
                mm = nc.tensor.matmul(out, self.k.one(f"bv{L}"), w[f"bv{L}"], start=False, stop=True)
            mm.then_inc(self.proj, 1)
        if self.topk:
            if s == 2:
                self.score(pe, 0)
            u = self.at(s, 0, 1) + 1
            if 1 <= u < H:
                self.score(pe, u)
        else:
            u = self.at(s, 0, 0)
            if u >= 0:
                self.score(pe, u)
        u = self.at(s, *self.TURN)
        if u >= 0:
            self.turn_p(pe, u)
        u = self.at(s, *self.PV)
        if u >= 0:
            g, a = divmod(u, HG)
            pe.wait_ge(self.pT_copied, u + 1)
            if a == 0 and g > 0:
                pe.wait_ge(self.oT_copied, g)
            for kt in range(NT):
                mm = nc.tensor.matmul(b[3][PAD * a:PAD * (a + 1), (g % 2) * T:(g % 2 + 1) * T], self.v[:, kt, u, :],
                                      self.pT[:, u % 2, kt, :], start=(kt == 0), stop=(kt == NT - 1))
            mm.then_inc(self.pv_done, 1)
        c = self.close(s)
        if c == 0:
            pe.wait_ge(self.oT_copied, NG)
            for j in range(NT):
                for g in range(NG):
                    tr = nc.tensor.transpose(b[j][:, g * P:(g + 1) * P], self.oT[:, g, j * P:(j + 1) * P], w["ident"])
            tr.then_inc(self.back, 1)
        if c == 2:
            pe.wait_ge(self.o_ready, 2)
            for j in range(NT):
                tr = nc.tensor.transpose(b[2][:, j * P:(j + 1) * P], self.o[:, j, :], w["ident"])
            tr.then_inc(self.o_turned, 1)
        if c == 3:
            pe.wait_ge(self.otT_ready, 1)
            for j in range(NT):
                out = b[3][:, j * D:(j + 1) * D]
                nc.tensor.matmul(out, self.otT[:, j * P:(j + 1) * P], w[f"wo{L}"], start=True, stop=False)
                mm = nc.tensor.matmul(out, self.k.one(f"bo{L}"), w[f"bo{L}"], start=False, stop=True)
            mm.then_inc(self.out_ps, 1)

    def act(self, act, s):
        nc, b, L = self.k.nc, self.banks, self.layer
        if s == 1:
            self.ln.act(act)
        if s == 2:
            for i, (dst, bias, scale) in enumerate([(self.kT, self.k.w[f"bk{L}"], 1.0),
                                                    (self.qT, self.k.bq_scaled[f"bq{L}"], HD ** -0.5)]):
                act.wait_ge(self.proj, i + 1)
                nc.scalar.activation(dst, b[2 + i][:, 0:T], ACT.Identity, bias=bias[:, 0:1],
                                     scale=scale).then_inc(self.proj_copied, 1)
            act.wait_ge(self.proj, 3)
            nc.scalar.activation(self.v[:, :, :, 0:HD], b[1][:, 0:NT * D].rearrange("p (j h d) -> p j h d", j=NT, d=HD),
                                 ACT.Copy).then_inc(self.proj_copied, 1)
        if self.topk:
            u = self.at(s, 1, 0)
            if u >= 0:
                self.exp_rest(act, u)
        u = self.at(s, *self.EXP)
        if u >= 0:
            self.exp_scores(act, u)
        u = self.at(s, *self.COPY)
        if u >= 0:
            self.copy_pT(act, u)
        u = self.at(s, *self.PV)
        if u >= 0 and u % HG == HG - 1:
            g = u // HG
            act.wait_ge(self.pv_done, u + 1)
            nc.scalar.activation(self.oT[:, g, :], b[3][:, (g % 2) * T:(g % 2 + 1) * T], ACT.Copy).then_inc(self.oT_copied, 1)
        if self.close(s) == 2:
            act.wait_ge(self.o_turned, 1)
            nc.scalar.activation(self.otT[:, :], b[2][:, 0:T], ACT.Copy).then_inc(self.otT_ready, 1)

    def pool_q1(self, pool, u):
        if u >= self.RING:
            pool.wait_ge(self.scores, u - self.RING + 1)
        self.k.nc.gpsimd.tensor_scalar(self.q1[:, u % self.RING, :], self.qT, self.k.w["head_rows"][:, u:u + 1], 1.0,
                                       ALU.mult, ALU.mult).then_inc(self.q1_ready, 1)

    def pool(self, pool, s):
        if s == 0:
            self.ln.pool(pool)
        if s == 2:
            pool.wait_ge(self.proj_copied, 2)
            for u in range(3):
                self.pool_q1(pool, u)
        if self.topk:
            u = self.at(s, 0, 0)
            if u >= 0:
                self.negative_max(pool, u)
            u = self.at(s, 1, 1)
            if u >= 0:
                self.keep_top(pool, u)
        u = self.at(s, 0, 0) + 3
        if 3 <= u < H:
            self.pool_q1(pool, u)

    def dve(self, dve, s):
        nc = self.k.nc
        if s == 0:
            self.ln.dve_stats(dve)
        if s == 1:
            self.ln.dve_scale(dve)
        for r in range(self.rounds):
            u = self.at(s, 0, r)
            if u >= 0 and self.topk:
                self.select(dve, u, r)
            elif u >= 0:
                dve.wait_ge(self.scores, u + 1)
                nc.vector.tensor_reduce(self.nmax[:, u, :], self.banks[u % 2][:, :].rearrange("p (j t) -> p j t", j=NT),
                                        AX.X, ALU.max, negate=True).then_inc(self.max_ready, 1)
        c = self.close(s)
        if c == 1:
            dve.wait_ge(self.back, 1)
            for j in range(NT):
                t = self.banks[j][:, :].rearrange("p (h c) -> p h c", c=PAD)
                self.chain.link(dve, nc.vector.reciprocal(self.rden[:, j, :], t[:, :, HD]))
                nc.vector.tensor_tensor(self.o[:, j, :].rearrange("p (h d) -> p h d", d=HD), t[:, :, 0:HD],
                                        self.rden[:, j, :].unsqueeze(2).broadcast_to([P, H, HD]),
                                        ALU.mult).then_inc(self.o_ready, 1)
        if c == 3:
            dve.wait_ge(self.out_ps, 1)
            self.chain.link(dve, nc.vector.scalar_tensor_tensor(
                out=self.x[:, :, :], in0=self.banks[3][:, 0:NT * D].rearrange("p (j d) -> p j d", j=NT),
                scalar=self.k.tg[:, self.gate:self.gate + 1], in1=self.x[:, :, :], op0=ALU.mult, op1=ALU.add))


class WideAttention(TopSelect):
    topk = 64

    def __init__(self, k, side, x, ctxT, banks, gate):
        self.k, self.x, self.ctxT, self.banks, self.gate = k, x, ctxT, banks, gate
        self.ln = LayerNorm(k, side, "a", x, banks[0])
        buf = Workspace(k, side)
        self.qT, self.kT, self.p, self.pT = buf.qT, buf.kT, buf.p, buf.pT
        self.v = k.sb("wide_v", [P, NT, H1, HD1 + 1])
        self.nmax = k.sb(f"att_nmax{side}", [P, H, NT])
        self.rden, self.o = k.sb("wide_rden", [P, H1, NT]), buf.oT.rearrange("p (j c) t -> p j (c t)", j=NT)
        self.otT = buf.kT.rearrange("p (j a) (b t) -> p j (a b) t", j=NT, t=P)
        n = f"att{side}_"
        self.chain = Chain(k.sem(n + "dve"))
        self.proj, self.proj_copied = k.sem(n + "proj"), k.sem(n + "proj_copied")
        self.scores, self.max_ready, self.exp_done = k.sem(n + "scores"), k.sem(n + "max"), k.sem(n + "exp")
        self.p_ready, self.pT_ps, self.pT_copied = k.sem(n + "p"), k.sem(n + "pT_ps"), k.sem(n + "pT")
        self.pv_done, self.rden_ready, self.o_ready = k.sem(n + "pv"), k.sem(n + "rden"), k.sem(n + "o")
        self.back, self.otT_ready, self.out_ps = k.sem(n + "back"), k.sem(n + "otT"), k.sem(n + "out")
        self.top_buffers(k, buf, n)
        self.units(3, H1, self.topk // 8, 7, 3, (2.0, 1.4, 1.4))

    def score(self, pe, u):
        c, a = divmod(u, 2)
        r = slice(HD1 * a, HD1 * (a + 1))
        if u == 0:
            pe.wait_ge(self.proj_copied, 6)
        if u >= 2:
            pe.wait_ge(self.exp_done, u - 1)
        for j in range(NT):
            mm = self.k.nc.tensor.matmul(self.banks[u % 2][:, j * T:(j + 1) * T], self.qT[r, c, j * P:(j + 1) * P],
                                         self.kT[r, c, :], start=True, stop=True)
        mm.then_inc(self.scores, 1)

    def pe(self, pe, s):
        nc, w, b = self.k.nc, self.k.w, self.banks
        if s == 0:
            for c in range(4):
                nc.tensor.matmul(b[2 + c // 2][:, (c % 2) * T:(c % 2 + 1) * T], w["wk1"][:, c * P:(c + 1) * P], self.ctxT[:, :],
                                 start=True, stop=True).then_inc(self.proj, 1)
        if s == 1:
            self.ln.pe(pe)
            for j in range(NT):
                pe.wait_ge(self.proj_copied, j + 1)
                nc.tensor.matmul(b[2 + j][:, :], self.ctxT[:, j * P:(j + 1) * P], w["wv1"], start=True,
                                 stop=True).then_inc(self.proj, 1)
        if s == 2:
            pe.wait_ge(self.ln.yT_ready, 1)
            for c in range(4):
                nc.tensor.matmul(b[c // 2][:, (c % 2) * T:(c % 2 + 1) * T], w["wq1"][:, c * P:(c + 1) * P], self.ln.yT[:, :],
                                 start=True, stop=True).then_inc(self.proj, 1)
            self.score(pe, 0)
        u = self.at(s, 0, 2) + 1
        if 1 <= u < H1:
            self.score(pe, u)
        u = self.at(s, 1, 3)
        if u >= 0:
            self.turn_p(pe, u)
        u = self.at(s, 1, 5)
        if u >= 0:
            pe.wait_ge(self.pT_copied, u + 1)
            if u >= 1:
                pe.wait_ge(self.o_ready, u)
            for j in range(NT):
                for kt in range(NT):
                    mm = nc.tensor.matmul(b[3][:, j * (HD1 + 1):(j + 1) * (HD1 + 1)], self.pT[:, u % 2, kt, j * P:(j + 1) * P],
                                          self.v[:, kt, u, :], start=(kt == 0), stop=(kt == NT - 1))
            mm.then_inc(self.pv_done, 1)
        c = self.close(s)
        if c == 0:
            pe.wait_ge(self.o_ready, H1)
            for j in range(NT):
                for i in range(4):
                    tr = nc.tensor.transpose(b[j][:, i * P:(i + 1) * P], self.o[:, j, i * P:(i + 1) * P], w["ident"])
                tr.then_inc(self.back, 1)
        if c == 1:
            for j in range(NT):
                pe.wait_ge(self.otT_ready, j + 1)
                out = b[2][:, j * D:(j + 1) * D]
                nc.tensor.matmul(out, self.k.one("bout1"), w["bout1"], start=True, stop=False)
                for i in range(4):
                    mm = nc.tensor.matmul(out, self.otT[:, j, i, :], w["wo1"][:, i * D:(i + 1) * D], start=False, stop=(i == 3))
            mm.then_inc(self.out_ps, 1)

    def act(self, act, s):
        nc, b = self.k.nc, self.banks
        if s == 0:
            for half in range(2):
                act.wait_ge(self.proj, 2 * half + 2)
                nc.scalar.activation(self.kT[:, 2 * half:2 * half + 2, :], b[2 + half][:, :], ACT.Copy).then_inc(self.proj_copied, 1)
        if s == 1:
            self.ln.act(act)
            for j in range(NT):
                act.wait_ge(self.proj, 4 + j + 1)
                nc.scalar.activation(self.v[:, j, :, 0:HD1], b[2 + j][:, :].rearrange("p (h d) -> p h d", d=HD1),
                                     ACT.Copy).then_inc(self.proj_copied, 1)
        if s == 2:
            for half in range(2):
                act.wait_ge(self.proj, 6 + 2 * half + 2)
                nc.scalar.activation(self.qT[:, 2 * half:2 * half + 2, :], b[half][:, :], ACT.Copy,
                                     scale=HD1 ** -0.5).then_inc(self.proj_copied, 1)
        u = self.at(s, 1, 0)
        if u >= 0:
            self.exp_rest(act, u)
        u = self.at(s, 0, 1)
        if u >= 0:
            self.exp_scores(act, u)
        u = self.at(s, 1, 4)
        if u >= 0:
            self.copy_pT(act, u)
        u = self.at(s, 1, 6)
        if u >= 0:
            act.wait_ge(self.rden_ready, u + 1)
            for j in range(NT):
                e = nc.scalar.activation(self.o[:, j, u * HD1:(u + 1) * HD1], b[3][:, j * (HD1 + 1):j * (HD1 + 1) + HD1],
                                         ACT.Copy, scale=self.rden[:, u, j:j + 1])
            e.then_inc(self.o_ready, 1)
        if self.close(s) == 0:
            for j in range(NT):
                act.wait_ge(self.back, j + 1)
                nc.scalar.activation(self.otT[:, j, :, :], b[j][:, :], ACT.Copy).then_inc(self.otT_ready, 1)

    def pool(self, pool, s):
        if s == 0:
            self.ln.pool(pool)
        u = self.at(s, 0, 0)
        if u >= 0:
            self.negative_max(pool, u)
        u = self.at(s, 1, 1)
        if u >= 0:
            self.keep_top(pool, u)

    def dve(self, dve, s):
        nc = self.k.nc
        if s == 0:
            self.ln.dve_stats(dve)
        if s == 1:
            self.ln.dve_scale(dve)
        for r in range(self.rounds):
            u = self.at(s, 0, r)
            if u >= 0:
                self.select(dve, u, r)
        u = self.at(s, 1, 6)
        if u >= 0:
            dve.wait_ge(self.pv_done, u + 1)
            nc.vector.reciprocal(self.rden[:, u, :], self.banks[3][:, 0:NT * (HD1 + 1)].rearrange("p (j c) -> p j c", j=NT)[:, :, HD1]).then_inc(self.rden_ready, 1)
        if self.close(s) == 2:
            dve.wait_ge(self.out_ps, 1)
            self.chain.link(dve, nc.vector.scalar_tensor_tensor(
                out=self.x[:, :, :], in0=self.banks[2][:, 0:NT * D].rearrange("p (j d) -> p j d", j=NT),
                scalar=self.k.tg[:, self.gate:self.gate + 1], in1=self.x[:, :, :], op0=ALU.mult, op1=ALU.add))


class Router:

    def __init__(self, k, side, tag, kind, lhsT, weight, bias, bank, t_bank):
        self.k, self.kind, self.lhsT, self.weight, self.bias, self.bank, self.t_bank = k, kind, lhsT, weight, bias, bank, t_bank
        self.nmax, self.sum = k.sb(f"rt_nmax{side}", [P, NT]), k.sb(f"rt_sum{side}", [P, NT])
        self.e = k.sb(f"rt_e{side}", [P, NT, E8])
        self.pr, self.wk = k.sb(f"rt_pr{side}", [P, NT, E8 + 6]), k.sb(f"rt_wk{side}", [P, NT, E8 + 6])
        self.m8 = k.sb(f"rt_m8{side}", [P, NT, 8])
        self.comb, self.combT = k.sb(f"rt_comb{side}", [P, NT, E8 + 1]), k.sb(f"rt_combT{side}", [E8 + 1, T])
        n = f"rt{side}{tag}_"
        self.chain = Chain(k.sem(n + "dve"))
        self.logits, self.nmax_ready, self.e_ready = k.sem(n + "logits"), k.sem(n + "nmax"), k.sem(n + "e")
        self.pr_ready = k.sem(n + "pr")
        self.comb_ready, self.turned, self.combT_ready = k.sem(n + "comb"), k.sem(n + "turned"), k.sem(n + "combT")

    def pe_logits(self, pe):
        nc, w = self.k.nc, self.k.w
        for j in range(NT):
            out = self.bank[:, j * E8:(j + 1) * E8]
            mm = nc.tensor.matmul(out, self.lhsT[:, j * P:(j + 1) * P], w[self.weight], start=True, stop=self.bias is None)
            if self.bias is not None:
                mm = nc.tensor.matmul(out, w["ones"][0:1, :], w[self.bias], start=False, stop=True)
        mm.then_inc(self.logits, 1)

    def pe_turn(self, pe):
        pe.wait_ge(self.comb_ready, 1)
        for j in range(NT):
            tr = self.k.nc.tensor.transpose(self.t_bank[0:E8 + 1, j * P:(j + 1) * P], self.comb[:, j, :], self.k.w["ident"])
        tr.then_inc(self.turned, 1)

    def act_exp(self, act):
        act.wait_ge(self.nmax_ready, 1)
        for j in range(NT):
            e = self.k.nc.scalar.activation(self.e[:, j, :], self.bank[:, j * E8:(j + 1) * E8], ACT.Exp, bias=self.nmax[:, j:j + 1])
        e.then_inc(self.e_ready, 1)

    def act_turn(self, act):
        act.wait_ge(self.turned, 1)
        self.k.nc.scalar.activation(self.combT[:, :], self.t_bank[0:E8 + 1, 0:T], ACT.Copy).then_inc(self.combT_ready, 1)

    def dve_max(self, dve):
        v = self.k.nc.vector
        lg = self.bank[:, 0:NT * E8].rearrange("p (j e) -> p j e", j=NT)
        dve.wait_ge(self.logits, 1)
        if self.kind == "top":
            v.tensor_copy(self.pr[:, :, 0:E8], lg).then_inc(self.pr_ready, 1)
        v.tensor_reduce(self.nmax[:, :], lg, AX.X, ALU.max, negate=True).then_inc(self.nmax_ready, 1)

    def dve_choose(self, dve):
        nc = self.k.nc
        v = nc.vector
        link = lambda ins: self.chain.link(dve, ins)
        pr = self.pr[:, :, 0:E8]
        wide = lambda t: t.unsqueeze(2).broadcast_to([P, NT, E8])
        if self.kind == "top":
            dve.wait_ge(self.pr_ready, 1)
        dve.wait_ge(self.e_ready, 1)
        if self.kind != "top":
            link(v.tensor_reduce(self.sum[:, :], self.e[:, :, :], AX.X, ALU.add))
            link(v.reciprocal(self.sum[:, :], self.sum[:, :]))
            link(v.tensor_tensor(pr, self.e[:, :, :], wide(self.sum[:, :]), ALU.mult))
        for j in range(NT):
            link(v.max(self.m8[:, j, :], self.pr[:, j, 0:E8]))
        link(v.memset(self.m8[:, :, 2:8], SENT))
        for j in range(NT):
            link(v.match_replace(self.wk[:, j, :], self.m8[:, j, :], self.pr[:, j, :], GONE))
        link(v.tensor_scalar(self.wk[:, :, 0:E8], self.wk[:, :, 0:E8], 0.5 * (SENT + GONE), None, ALU.is_le))
        comb, chosen = self.comb[:, :, 0:E8], self.wk[:, :, 0:E8]
        if self.kind == "prob":
            v.tensor_tensor(comb, chosen, pr, ALU.mult).then_inc(self.comb_ready, 1)
        else:
            src = self.e[:, :, :] if self.kind == "top" else pr
            link(v.tensor_tensor(comb, chosen, src, ALU.mult))
            link(v.tensor_reduce(self.sum[:, :], comb, AX.X, ALU.add))
            if self.kind == "renorm":
                link(v.tensor_scalar(self.sum[:, :], self.sum[:, :], 1e-9, None, ALU.add))
            link(v.reciprocal(self.sum[:, :], self.sum[:, :]))
            v.tensor_tensor(comb, comb, wide(self.sum[:, :]), ALU.mult).then_inc(self.comb_ready, 1)
        dve.wait_ge(self.comb_ready, 1)


class LinearExperts(Units):
    PART = 4

    def __init__(self, k, side, x, out, att, banks, gate, before):
        self.k, self.x, self.out, self.att, self.banks, self.gate, self.before = k, x, out, att, banks, gate, before
        self.yT = att.ln.yT
        self.rt = Router(k, side, "a", "prob", self.yT, "gate0", "bgate0", banks[2], banks[3])
        self.acc = k.sb(f"moe_acc{side}", [P, NT, D])
        n = f"moe{side}_"
        self.chain = Chain(k.sem(n + "dve"))
        self.y_ps, self.bias_ps = k.sem(n + "y_ps"), k.sem(n + "bias_ps")
        self.acc_ready = k.sem(n + "acc")
        self.parts = E8 // self.PART
        self.units(2, NT * self.parts, 1, 1, 1, (1.4, 1.4, 1.0))

    def pe(self, pe, s):
        nc, w, b = self.k.nc, self.k.w, self.banks
        if s == 0:
            pe.wait_ge(self.att.oT_copied, NG)
            self.rt.pe_logits(pe)
            pe.wait_ge(self.att.o_ready, 2)
        if s == 2:
            pe.wait_ge(self.rt.combT_ready, 1)
            for j in range(NT):
                mm = nc.tensor.matmul(b[2][:, j * D:(j + 1) * D], self.rt.combT[:, j * P:(j + 1) * P], w["bias0"][0:E8 + 1, :],
                                      start=True, stop=True)
            mm.then_inc(self.bias_ps, 1)
        u = self.at(s + 1, 0, 0)
        if u >= 0:
            j, part = divmod(u, self.parts)
            if j == 1:
                pe.wait_ge(self.acc_ready, 1 + self.PART * (u - self.parts + 1))
            nc.tensor.matmul(b[part][:, :], self.yT[:, j * P:(j + 1) * P], w["exp0"][:, part * 512:(part + 1) * 512],
                             start=True, stop=True).then_inc(self.y_ps, 1)
        if s == 1:
            self.rt.pe_turn(pe)

    def act(self, act, s):
        if s == 0:
            self.rt.act_exp(act)
        if s == 1:
            self.rt.act_turn(act)

    def pool(self, pool, s):
        pass

    def dve(self, dve, s):
        nc = self.k.nc
        if s == 0:
            self.rt.dve_max(dve)
        if s == 1:
            self.rt.dve_choose(dve)
        if s == 2:
            dve.wait_ge(self.bias_ps, 1)
            nc.vector.tensor_tensor(self.acc[:, :, :], self.banks[2][:, 0:NT * D].rearrange("p (j d) -> p j d", j=NT),
                                    self.att.o[:, :, :], ALU.add).then_inc(self.acc_ready, 1)
        u = self.at(s, 0, 0)
        if u >= 0:
            j, part = divmod(u, self.parts)
            dve.wait_ge(self.y_ps, u + 1)
            for i in range(self.PART):
                dve.wait_ge(self.acc_ready, 1 + self.PART * u + i)
                e = self.PART * part + i
                ins = nc.vector.scalar_tensor_tensor(out=self.acc[:, j, :], in0=self.banks[part][:, i * D:(i + 1) * D],
                                                     scalar=self.rt.comb[:, j, e:e + 1], in1=self.acc[:, j, :], op0=ALU.mult,
                                                     op1=ALU.add)
                ins.then_inc(self.acc_ready, 1)
        if self.close(s) == 0:
            dve.wait_ge(self.acc_ready, 1 + E8 * NT)
            if self.before is not None:
                dve.wait_ge(self.before.stored, 16)
            self.chain.link(dve, nc.vector.scalar_tensor_tensor(out=self.out[:, :, :], in0=self.acc[:, :, :],
                                                                scalar=self.k.tg[:, self.gate:self.gate + 1], in1=self.x[:, :, :],
                                                                op0=ALU.mult, op1=ALU.add))


class GatedExperts(Units):

    def __init__(self, k, side, x, banks, gate):
        self.k, self.x, self.banks, self.gate = k, x, banks, gate
        self.ln = LayerNorm(k, side, "a", x, banks[0])
        self.rt = Router(k, side, "a", "top", self.ln.yT, "router1", None, banks[2], banks[3])
        buf = Workspace(k, side)
        self.th, self.hT = buf.p[:, 0, :, :], buf.p[:, 1, :, :]
        self.acc = k.sb(f"moe_acc{side}", [P, NT, D])
        n = f"moe{side}_"
        self.chain = Chain(k.sem(n + "dve"))
        self.h_ps, self.th_ready, self.u_ready = k.sem(n + "h_ps"), k.sem(n + "th"), k.sem(n + "u")
        self.hT_ready, self.y_ps, self.y_used = k.sem(n + "hT"), k.sem(n + "y_ps"), k.sem(n + "y_used")
        self.N = 2 + E8
        self.units(3, self.N, 1, 2, 1, (1.4, 1.8, 1.0))

    def pe(self, pe, s):
        nc, w, b = self.k.nc, self.k.w, self.banks
        if s == 1:
            self.ln.pe(pe)
        if s == 2:
            pe.wait_ge(self.ln.yT_ready, 1)
            self.rt.pe_logits(pe)
        u = self.at(s, 0, 0)
        if u >= 0:
            if u >= 2:
                pe.wait_ge(self.hT_ready, u - 1)
            if u < 2:
                pw, gw = w["gate_w"][:, u * D:(u + 1) * D], w["up_w"][:, u * D:(u + 1) * D]
            else:
                pw, gw = (w["fc1"][:, (2 * (u - 2) + i) * D:(2 * (u - 2) + i + 1) * D] for i in range(2))
            nc.tensor.matmul(b[u % 2][:, 0:T], pw, self.ln.yT[:, :], start=True, stop=True)
            nc.tensor.matmul(b[u % 2][:, T:2 * T], gw, self.ln.yT[:, :], start=True, stop=True).then_inc(self.h_ps, 1)
        if s == 4:
            self.rt.pe_turn(pe)
        u = self.at(s, 2, 0)
        if u == 1:
            pe.wait_ge(self.rt.combT_ready, 1)
            pe.wait_ge(self.hT_ready, 2)
            for j in range(NT):
                for c in range(2):
                    mm = nc.tensor.matmul(b[2][:, j * D:(j + 1) * D], self.hT[:, c, j * P:(j + 1) * P],
                                          w["down_w"][:, c * D:(c + 1) * D], start=(c == 0), stop=(c == 1))
            mm.then_inc(self.y_ps, 1)
        if u >= 2:
            pe.wait_ge(self.hT_ready, u + 1)
            if u >= 3:
                pe.wait_ge(self.y_used, u - 2)
            for j in range(NT):
                mm = nc.tensor.matmul(b[3 - u % 2][:, j * D:(j + 1) * D], self.hT[:, u % 2, j * P:(j + 1) * P],
                                      w["fc2"][:, (u - 2) * D:(u - 1) * D], start=True, stop=True)
            mm.then_inc(self.y_ps, 1)

    def act(self, act, s):
        nc = self.k.nc
        if s == 1:
            self.ln.act(act)
        if s == 2:
            self.rt.act_exp(act)
        if s == 4:
            self.rt.act_turn(act)
        u = self.at(s, 0, 0)
        if u >= 0:
            act.wait_ge(self.h_ps, u + 1)
            if u >= 2:
                act.wait_ge(self.hT_ready, u - 1)
            nc.scalar.activation(self.th[:, u % 2, :], self.banks[u % 2][:, 0:T], ACT.Tanh, scale=0.5).then_inc(self.th_ready, 1)

    def pool(self, pool, s):
        if s == 0:
            self.ln.pool(pool)

    def dve(self, dve, s):
        nc, b = self.k.nc, self.banks
        if s == 0:
            self.ln.dve_stats(dve)
        if s == 1:
            self.ln.dve_scale(dve)
        if s == 2:
            self.rt.dve_max(dve)
        if s == 3:
            self.rt.dve_choose(dve)
        u = self.at(s, 1, 0)
        if u >= 0:
            dve.wait_ge(self.th_ready, u + 1)
            th = self.th[:, u % 2, :]
            nc.vector.scalar_tensor_tensor(out=th, in0=th, scalar=1.0, in1=b[u % 2][:, 0:T], op0=ALU.add,
                                           op1=ALU.mult).then_inc(self.u_ready, 1)
            dve.wait_ge(self.u_ready, u + 1)
            if u >= 2:
                dve.wait_ge(self.y_ps, u - 2 if u > 3 else 1)
            nc.vector.scalar_tensor_tensor(out=self.hT[:, u % 2, :], in0=th, scalar=0.5, in1=b[u % 2][:, T:2 * T],
                                           op0=ALU.mult, op1=ALU.mult).then_inc(self.hT_ready, 1)
        u = self.at(s, 2, 0)
        if u == 1:
            dve.wait_ge(self.y_ps, 1)
            nc.vector.tensor_copy(self.acc[:, :, :], b[2][:, 0:NT * D].rearrange("p (j d) -> p j d", j=NT)).then_inc(self.y_used, 1)
        if u >= 2:
            dve.wait_ge(self.y_ps, u)
            dve.wait_ge(self.y_used, u - 1)
            for j in range(NT):
                ins = nc.vector.scalar_tensor_tensor(out=self.acc[:, j, :], in0=b[3 - u % 2][:, j * D:(j + 1) * D],
                                                     scalar=self.rt.comb[:, j, u - 2:u - 1], in1=self.acc[:, j, :], op0=ALU.mult,
                                                     op1=ALU.add)
            ins.then_inc(self.y_used, 1)
        if self.close(s) == 0:
            dve.wait_ge(self.y_used, self.N - 1)
            self.chain.link(dve, nc.vector.scalar_tensor_tensor(out=self.x[:, :, :], in0=self.acc[:, :, :],
                                                                scalar=self.k.tg[:, self.gate:self.gate + 1], in1=self.x[:, :, :],
                                                                op0=ALU.mult, op1=ALU.add))


class GeluExperts(Units):

    def __init__(self, k, side, x, banks, gate):
        self.k, self.x, self.banks, self.gate = k, x, banks, gate
        self.ln = LayerNorm(k, side, "c", x, banks[0])
        self.rt = Router(k, side, "b", "renorm", self.ln.yT, "router2", "br2", banks[2], banks[3])
        buf = Workspace(k, side)
        self.hT = [buf.kT, buf.qT]
        self.acc = k.sb(f"moe_acc{side}", [P, NT, D])
        n = f"gelu{side}_"
        self.chain = Chain(k.sem(n + "dve"))
        self.h_ps, self.hT_ready, self.y_ps, self.y_used = k.sem(n + "h_ps"), k.sem(n + "hT"), k.sem(n + "y_ps"), k.sem(n + "y_used")
        self.N = 1 + E8
        self.units(3, self.N, 2, 2, 1, (1.4, 1.8, 1.0))

    def pe(self, pe, s):
        nc, w, b = self.k.nc, self.k.w, self.banks
        if s == 1:
            self.ln.pe(pe)
        if s == 2:
            pe.wait_ge(self.ln.yT_ready, 1)
            self.rt.pe_logits(pe)
        u = self.at(s, 0, 0)
        if u >= 0:
            for c in range(FF2):
                if u >= 1 and c % 2 == 0:
                    pe.wait_ge(self.hT_ready, FF2 * (u - 1) + c + 2)
                mm = nc.tensor.matmul(b[c // 2][:, (c % 2) * T:(c % 2 + 1) * T], w["w1"][:, (u * FF2 + c) * 128:(u * FF2 + c + 1) * 128],
                                      self.ln.yT[:, :], start=True, stop=True)
                if c % 2 == 1:
                    mm.then_inc(self.h_ps, 1)
        if s == 4:
            self.rt.pe_turn(pe)
        u = self.at(s, 1, 1)
        if u >= 0:
            if u == 0:
                pe.wait_ge(self.rt.combT_ready, 1)
            if u >= 2:
                pe.wait_ge(self.y_used, u - 1)
            pe.wait_ge(self.hT_ready, FF2 * (u + 1))
            for j in range(NT):
                out = b[2 + u % 2][:, j * D:(j + 1) * D]
                if u == 0:
                    nc.tensor.matmul(out, self.rt.combT[:, j * P:(j + 1) * P], w["bias2"][0:E8 + 1, :], start=True, stop=False)
                for c in range(FF2):
                    mm = nc.tensor.matmul(out, self.hT[u % 2][:, c, j * P:(j + 1) * P],
                                          w["w2"][:, (u * FF2 + c) * 128:(u * FF2 + c + 1) * 128],
                                          start=(u > 0 and c == 0), stop=(c == FF2 - 1))
            mm.then_inc(self.y_ps, 1)

    def act(self, act, s):
        nc = self.k.nc
        if s == 1:
            self.ln.act(act)
        if s == 2:
            self.rt.act_exp(act)
        if s == 4:
            self.rt.act_turn(act)
        u = self.at(s, 0, 0)
        if u >= 0:
            for c in range(FF2):
                act.wait_ge(self.h_ps, 2 * u + c // 2 + 1)
                if u >= 2 and c == 0:
                    act.wait_ge(self.y_ps, u - 1)
                nc.scalar.activation(self.hT[u % 2][:, c, :], self.banks[c // 2][:, (c % 2) * T:(c % 2 + 1) * T], ACT.Gelu,
                                     bias=self.k.w["b1"][:, u * FF2 + c:u * FF2 + c + 1]).then_inc(self.hT_ready, 1)

    def pool(self, pool, s):
        if s == 0:
            self.ln.pool(pool)

    def dve(self, dve, s):
        nc, b = self.k.nc, self.banks
        if s == 0:
            self.ln.dve_stats(dve)
        if s == 1:
            self.ln.dve_scale(dve)
        if s == 2:
            self.rt.dve_max(dve)
        if s == 3:
            self.rt.dve_choose(dve)
        u = self.at(s, 2, 0)
        if u == 0:
            dve.wait_ge(self.y_ps, 1)
            nc.vector.tensor_copy(self.acc[:, :, :], b[2][:, 0:NT * D].rearrange("p (j d) -> p j d", j=NT)).then_inc(self.y_used, 1)
        if u >= 1:
            dve.wait_ge(self.y_ps, u + 1)
            dve.wait_ge(self.y_used, u)
            for j in range(NT):
                ins = nc.vector.scalar_tensor_tensor(out=self.acc[:, j, :], in0=b[2 + u % 2][:, j * D:(j + 1) * D],
                                                     scalar=self.rt.comb[:, j, u - 1:u], in1=self.acc[:, j, :], op0=ALU.mult,
                                                     op1=ALU.add)
            ins.then_inc(self.y_used, 1)
        if self.close(s) == 0:
            dve.wait_ge(self.y_used, self.N)
            self.chain.link(dve, nc.vector.scalar_tensor_tensor(out=self.x[:, :, :], in0=self.acc[:, :, :],
                                                                scalar=self.k.tg[:, self.gate:self.gate + 1], in1=self.x[:, :, :],
                                                                op0=ALU.mult, op1=ALU.add))


class MixedAttention(Units):

    def __init__(self, k, side, x, batch, banks, gate):
        self.k, self.x, self.batch, self.banks, self.gate = k, x, batch, banks, gate
        self.ln = LayerNorm(k, side, "m", x, banks[0])
        self.ssq, self.rn = k.sb("mix_ssq", [P, NT]), k.sb("mix_rn", [P, NT])
        self.lg, self.wk = k.sb("mix_lg", [P, NT, E16 + 6]), k.sb("mix_wk", [P, NT, E16 + 6])
        self.m8, self.none, self.ngm = k.sb("mix_m8", [P, NT, 8]), k.sb("mix_none", [P, NT]), k.sb("mix_ngm", [P, NT])
        self.gt, self.act_mask, self.wt = k.sb("mix_gt", [P, NT, E16]), k.sb("mix_mask", [P, NT, E16]), k.sb("mix_wt", [P, NT, E16])
        self.sum = k.sb("mix_sum", [P, NT])
        buf = Workspace(k, side)
        self.sq = buf.p[:, 0, 0, :].rearrange("p (j d) -> p j d", j=NT)
        self.wT, self.wb, self.zT = buf.p[0:E16, 0, 1, :], k.sb("mix_wb", [P, E16, T]), buf.whole
        self.qT, self.kT = buf.p[:, 1, 0, :], buf.p[:, 1, 1, :]
        self.v = buf.pT[:, 1, 0, :].rearrange("p (j d) -> p j d", j=NT)
        self.nmax, self.den, self.rden = k.sb("mix_nmax", [P, NT]), k.sb("mix_den", [P, NT]), k.sb("mix_rden", [P, NT])
        self.p, self.pT, self.oT = buf.p[:, 0, :, :], buf.pT[:, 0, :, :], buf.pT[:, 1, 1, :]
        n = "mix_"
        self.chain = Chain(k.sem(n + "dve"))
        self.ssq_ready, self.rn_in, self.rn_ready, self.logits = k.sem(n + "ssq"), k.sem(n + "rn_in"), k.sem(n + "rn"), k.sem(n + "logits")
        self.gt_ready, self.e_ready, self.wt_ready = k.sem(n + "gt"), k.sem(n + "e"), k.sem(n + "wt")
        self.turned, self.wT_ready = k.sem(n + "turned"), k.sem(n + "wT")
        self.wb_ps, self.wb_ready, self.z_ready = k.sem(n + "wb_ps"), k.sem(n + "wb"), k.sem(n + "z")
        self.qkv_ps, self.qkv_copied = k.sem(n + "qkv_ps"), k.sem(n + "qkv")
        self.scores, self.max_ready, self.exp_done, self.p_ready = k.sem(n + "scores"), k.sem(n + "max"), k.sem(n + "exp"), k.sem(n + "p")
        self.pT_ps, self.pT_copied, self.o_ps, self.o_copied = k.sem(n + "pT_ps"), k.sem(n + "pT"), k.sem(n + "o_ps"), k.sem(n + "o")
        self.zo_ready, self.zo2_ready, self.out_ps, self.x_done = k.sem(n + "zo"), k.sem(n + "zo2"), k.sem(n + "out"), k.sem(n + "x_done")
        self.stored = k.sem("stored")
        self.PAIRS = E16 // 2
        self.units(5, self.PAIRS, 1, 1, 4 + self.PAIRS + 1, (1.6, 3.0, 1.6))

    def pe(self, pe, s):
        nc, w, b = self.k.nc, self.k.w, self.banks
        if s == 1:
            self.ln.pe(pe)
        if s == 2:
            pe.wait_ge(self.ln.yT_ready, 1)
            for j in range(NT):
                mm = nc.tensor.matmul(b[1][:, j * E16:(j + 1) * E16], self.ln.yT[:, j * P:(j + 1) * P], self.k.sn[:, :],
                                      start=True, stop=True)
            mm.then_inc(self.logits, 1)
        if s == 4:
            pe.wait_ge(self.wt_ready, 1)
            for j in range(NT):
                tr = nc.tensor.transpose(b[0][0:E16, j * P:(j + 1) * P], self.wt[:, j, :], w["ident"])
            tr.then_inc(self.turned, 1)
            pe.wait_ge(self.wT_ready, 1)
        i = self.at(s, 0, 0)
        if i >= 0:
            if i >= 2:
                pe.wait_ge(self.wb_ready, i - 1)
            for e in (2 * i, 2 * i + 1):
                mm = nc.tensor.matmul(b[i % 2][:, (e % 2) * T:(e % 2 + 1) * T], w["ident"][0:E16, e:e + 1].broadcast_to([E16, P]), self.wT,
                                      start=True, stop=True)
            mm.then_inc(self.wb_ps, 1)
        i = self.at(s, 1, 0)
        if i >= 0:
            pe.wait_ge(self.z_ready, i + 1)
            for e in (2 * i, 2 * i + 1):
                first, last = e == 0, e == E16 - 1
                nc.tensor.matmul(b[2][:, 0:T], w["qp"][:, e * D:(e + 1) * D], self.zT[:, e, :], start=first, stop=last)
                mm = nc.tensor.matmul(b[3][:, 0:T], w["kp"][:, e * D:(e + 1) * D], self.zT[:, e, :], start=first, stop=last)
            if i == self.PAIRS - 1:
                mm.then_inc(self.qkv_ps, 1)
        c = self.close(s)
        if c == 0:
            pe.wait_ge(self.wb_ready, self.PAIRS)
            for j in range(NT):
                for e in range(E16):
                    mm = nc.tensor.matmul(b[0][:, j * D:(j + 1) * D], self.zT[:, e, j * P:(j + 1) * P], w["vp"][:, e * D:(e + 1) * D],
                                          start=(e == 0), stop=(e == E16 - 1))
                if j == 0:
                    pe.wait_ge(self.qkv_copied, 2)
                    for i in range(NT):
                        sc = nc.tensor.matmul(b[1][:, i * T:(i + 1) * T], self.qT[:, i * P:(i + 1) * P], self.kT[:, :],
                                              start=True, stop=True)
                    sc.then_inc(self.scores, 1)
            mm.then_inc(self.qkv_ps, 1)
        if c == 2:
            pe.wait_ge(self.p_ready, NT)
            for kt in range(NT):
                for j in range(NT):
                    tr = nc.tensor.transpose(b[2][:, kt * T + j * P:kt * T + (j + 1) * P], self.p[:, j, kt * P:(kt + 1) * P], w["ident"])
            tr.then_inc(self.pT_ps, 1)
        if c == 3:
            pe.wait_ge(self.pT_copied, 1)
            pe.wait_ge(self.qkv_copied, 3)
            for kt in range(NT):
                mm = nc.tensor.matmul(b[3][:, 0:T], self.v[:, kt, :], self.pT[:, kt, :], start=(kt == 0), stop=(kt == NT - 1))
            mm.then_inc(self.o_ps, 1)
        i = c - 5
        if 0 <= i < self.PAIRS:
            pe.wait_ge(self.zo2_ready if i % 2 else self.zo_ready, i // 2 + 1)
            for e in (2 * i, 2 * i + 1):
                for j in range(NT):
                    mm = nc.tensor.matmul(b[j][:, 0:D], self.zT[:, e, j * P:(j + 1) * P], w["op"][:, e * D:(e + 1) * D],
                                          start=(e == 0), stop=(e == E16 - 1))
            if i == self.PAIRS - 1:
                mm.then_inc(self.out_ps, 1)

    def act(self, act, s):
        nc, b = self.k.nc, self.banks
        if s == 1:
            self.ln.act(act)
            for j in range(NT):
                act.wait_ge(self.ln.y_ready, j + 1)
                nc.scalar.activation(self.sq[:, j, :], self.ln.y[:, j, :], ACT.Square,
                                     accum_out=self.ssq[:, j:j + 1]).then_inc(self.ssq_ready, 1)
        if s == 3:
            act.wait_ge(self.gt_ready, 1)
            for j in range(NT):
                e = nc.scalar.activation(self.wt[:, j, :], self.gt[:, j, :], ACT.Exp, bias=self.ngm[:, j:j + 1])
            e.then_inc(self.e_ready, 1)
        if s == 4:
            act.wait_ge(self.turned, 1)
            nc.scalar.activation(self.wT, b[0][0:E16, 0:T], ACT.Copy).then_inc(self.wT_ready, 1)
        i = self.at(s, 0, 0)
        if i >= 0:
            act.wait_ge(self.wb_ps, i + 1)
            nc.scalar.activation(self.wb[:, 2 * i:2 * i + 2, :], b[i % 2][:, :], ACT.Copy).then_inc(self.wb_ready, 1)
        c = self.close(s)
        if c == 0:
            act.wait_ge(self.qkv_ps, 1)
            nc.scalar.activation(self.qT, b[2][:, 0:T], ACT.Copy, scale=D ** -0.5).then_inc(self.qkv_copied, 1)
            nc.scalar.activation(self.kT, b[3][:, 0:T], ACT.Copy).then_inc(self.qkv_copied, 1)
        if c == 1:
            act.wait_ge(self.max_ready, 1)
            for j in range(NT):
                nc.scalar.activation(self.p[:, j, :], b[1][:, j * T:(j + 1) * T], ACT.Exp, bias=self.nmax[:, j:j + 1],
                                     accum_out=self.den[:, j:j + 1]).then_inc(self.exp_done, 1)
            act.wait_ge(self.qkv_ps, 2)
            nc.scalar.activation(self.v[:, :, :], b[0][:, 0:NT * D], ACT.Copy).then_inc(self.qkv_copied, 1)
        if c == 2:
            act.wait_ge(self.pT_ps, 1)
            nc.scalar.activation(self.pT[:, :, :], b[2][:, :], ACT.Copy).then_inc(self.pT_copied, 1)
        if c == 3:
            act.wait_ge(self.o_ps, 1)
            nc.scalar.activation(self.oT[:, :], b[3][:, 0:T], ACT.Copy).then_inc(self.o_copied, 1)

    def attended(self, eng, i):
        return eng.tensor_tensor(self.zT[:, 2 * i:2 * i + 2, :], self.wb[:, 2 * i:2 * i + 2, :],
                                 self.oT[:, :].unsqueeze(1).broadcast_to([P, 2, T]), ALU.mult)

    def pool(self, pool, s):
        nc = self.k.nc
        if s == 0:
            self.ln.pool(pool)
        if s == 2:
            pool.wait_ge(self.rn_in, 1)
            nc.gpsimd.tensor_tensor(self.rn[:, :], self.ssq[:, :], self.k.half[:, 0:NT], ALU.pow).then_inc(self.rn_ready, 1)
        i = self.at(s, 0, 0)
        if i >= 0:
            pool.wait_ge(self.wb_ready, i + 1)
            nc.gpsimd.tensor_tensor(self.zT[:, 2 * i:2 * i + 2, :], self.wb[:, 2 * i:2 * i + 2, :],
                                    self.ln.yT[:, :].unsqueeze(1).broadcast_to([P, 2, T]), ALU.mult).then_inc(self.z_ready, 1)
        i = self.close(s) - 4
        if 0 <= i < self.PAIRS and i % 2 == 1:
            pool.wait_ge(self.o_copied, 1)
            self.attended(nc.gpsimd, i).then_inc(self.zo2_ready, 1)

    def dve(self, dve, s):
        nc, b = self.k.nc, self.banks
        v = nc.vector
        link = lambda ins: self.chain.link(dve, ins)
        if s == 0:
            self.ln.dve_stats(dve)
        if s == 1:
            self.ln.dve_scale(dve)
            dve.wait_ge(self.ssq_ready, NT)
            v.tensor_scalar(self.ssq[:, :], self.ssq[:, :], 1e-24, None, ALU.max).then_inc(self.rn_in, 1)
        if s == 3:
            dve.wait_ge(self.rn_ready, 1)
            dve.wait_ge(self.logits, 1)
            for j in range(NT):
                link(v.scalar_tensor_tensor(out=self.lg[:, j, 0:E16], in0=b[1][:, j * E16:(j + 1) * E16], scalar=self.rn[:, j:j + 1],
                                            in1=self.k.sig[:, :], op0=ALU.mult, op1=ALU.subtract))
            for j in range(NT):
                link(v.max(self.m8[:, j, :], self.lg[:, j, 0:E16]))
            link(v.tensor_scalar(self.none[:, :], self.m8[:, :, 0], 0.0, None, ALU.is_le))
            link(v.tensor_scalar(self.ngm[:, :], self.m8[:, :, 0], 0.0, -1.0, ALU.max, ALU.mult))
            v.tensor_scalar(self.gt[:, :, :], self.lg[:, :, 0:E16], 0.0, None, ALU.max).then_inc(self.gt_ready, 1)
        if s == 4:
            link(v.memset(self.m8[:, :, 2:8], SENT))
            for j in range(NT):
                link(v.match_replace(self.wk[:, j, :], self.m8[:, j, :], self.lg[:, j, :], GONE))
            link(v.tensor_scalar(self.wk[:, :, 0:E16], self.wk[:, :, 0:E16], 0.5 * (SENT + GONE), None, ALU.is_le))
            for j in range(NT):
                link(v.tensor_scalar(self.act_mask[:, j, :], self.wk[:, j, 0:E16], self.none[:, j:j + 1], None, ALU.mult))
            link(v.tensor_scalar(self.wk[:, :, 0:E16], self.lg[:, :, 0:E16], 0.0, None, ALU.is_gt))
            link(v.tensor_tensor(self.act_mask[:, :, :], self.act_mask[:, :, :], self.wk[:, :, 0:E16], ALU.max))
            dve.wait_ge(self.e_ready, 1)
            link(v.tensor_tensor(self.wt[:, :, :], self.wt[:, :, :], self.act_mask[:, :, :], ALU.mult))
            link(v.tensor_reduce(self.sum[:, :], self.wt[:, :, :], AX.X, ALU.add))
            link(v.reciprocal(self.sum[:, :], self.sum[:, :]))
            v.tensor_tensor(self.wt[:, :, :], self.wt[:, :, :], self.sum[:, :].unsqueeze(2).broadcast_to([P, NT, E16]),
                            ALU.mult).then_inc(self.wt_ready, 1)
        c = self.close(s)
        if c == 0:
            dve.wait_ge(self.scores, 1)
            v.tensor_reduce(self.nmax[:, :], b[1][:, :].rearrange("p (j t) -> p j t", j=NT), AX.X, ALU.max,
                            negate=True).then_inc(self.max_ready, 1)
        if c == 1:
            dve.wait_ge(self.exp_done, NT)
            link(v.reciprocal(self.rden[:, :], self.den[:, :]))
            for j in range(NT):
                v.tensor_scalar(self.p[:, j, :], self.p[:, j, :], self.rden[:, j:j + 1], None, ALU.mult).then_inc(self.p_ready, 1)
        i = c - 4
        if 0 <= i < self.PAIRS and i % 2 == 0:
            dve.wait_ge(self.o_copied, 1)
            self.attended(v, i).then_inc(self.zo_ready, 1)
        if i == self.PAIRS:
            dve.wait_ge(self.out_ps, 1)
            for j in range(NT):
                v.scalar_tensor_tensor(out=self.x[:, j, :], in0=b[j][:, 0:D], scalar=self.k.tg[:, self.gate:self.gate + 1],
                                       in1=self.x[:, j, :], op0=ALU.mult, op1=ALU.add).then_inc(self.x_done, 1)

    def sync(self, sp):
        sp.wait_ge(self.x_done, NT)
        sp.dma_start(self.k.out_dram[bass.ds(self.batch * T, T), :].rearrange("(j p) d -> p j d", p=P),
                     self.x[:, :, :]).then_inc(self.stored, 16)
        sp.wait_ge(self.stored, 16)


class Chunk0:

    def __init__(self, k, lane, old, batch):
        self.k, self.batch, b = k, batch, k.psum[0:4]
        self.mix = None if old is None else MixedAttention(k, "P", k.x[lane], old, b, 7)
        self.stages = [] if old is None else [self.mix]
        if batch is not None:
            self.ctxT, self.load = k.ctxT[lane], k.sem("load")
            att = HeadAttention(k, "P", 0, k.x_in, None, b, "b")
            self.stages += [Performer(k, "P", k.x_in, self.ctxT, k.ctx_tok, b, self.load, self.mix), att,
                            LinearExperts(k, "P", k.x_in, k.x[lane], att, b, 4, self.mix)]

    def sync(self, sp):
        k, i = self.k, self.batch
        if i is not None:
            sp.dma_start(k.x_in[:, :, :], k.x_dram[bass.ds(i * T, T), :].rearrange("(j p) d -> p j d", p=P)).then_inc(self.load, 16)
            sp.dma_start(k.ctx_tok[:, :, :], k.ctx_dram[bass.ds(i * T, T), :].rearrange("(j p) d -> p j d", p=P)).then_inc(self.load, 16)
            sp.dma_start(self.ctxT[:, :], k.ctxT_dram[:, bass.ds(i * T, T)]).then_inc(self.load, 16)
        if self.mix is not None:
            self.mix.sync(sp)


class Chunk1:
    def __init__(self, k, lane):
        self.stages = [WideAttention(k, "Q", k.x[lane], k.ctxT[lane], k.psum[4:8], 1)]

    def sync(self, sp):
        pass


class Chunk2:
    def __init__(self, k, lane):
        x, b = k.x[lane], k.psum[0:4]
        self.stages = [GatedExperts(k, "P", x, b, 5), HeadAttention(k, "P", 2, x, k.ctxT[lane], b, "b", gate=2),
                       GeluExperts(k, "P", x, b, 6)]

    def sync(self, sp):
        pass


class Chunk3:
    def __init__(self, k, lane):
        self.stages = [HeadAttention(k, "Q", 3, k.x[lane], k.ctxT[lane], k.psum[4:8], "a", topk=32, gate=3)]

    def sync(self, sp):
        pass


def interleaved(chunks):
    order = []
    for n, c in enumerate(chunks):
        steps = [(stage, s) for stage in c.stages for s in range(stage.steps)]
        total, at = sum(stage.weight(s) for stage, s in steps), 0.0
        for i, (stage, s) in enumerate(steps):
            order.append((at / total, n, i, stage, s))
            at += stage.weight(s)
    return [o[3:] for o in sorted(order, key=lambda o: o[:3])]


def run_block(k, chunks):
    nc = k.nc
    steps = interleaved(chunks)
    with nc.Block() as block:
        @block.sync
        def _(sp):
            for c in chunks:
                c.sync(sp)

        @block.tensor
        def _(pe):
            for stage, s in steps:
                stage.pe(pe, s)

        @block.scalar
        def _(act):
            for stage, s in steps:
                stage.act(act, s)

        @block.vector
        def _(dve):
            for stage, s in steps:
                stage.dve(dve, s)

        @block.gpsimd
        def _(pool):
            for stage, s in steps:
                stage.pool(pool, s)
    nc.all_engine_barrier(sems_to_clear=range(k.first, k.last + 1))


def flamingo(nc, dram):
    with ExitStack() as ctx:
        k = Shared(nc, ctx)
        weights_in = {name: k.lasting_sem(f"{name}_in") for name, _ in PACKS}
        rows_in, all_ctx_in = k.lasting_sem("rows_in"), k.lasting_sem("all_ctx_in")
        for name, pack in PACKS:
            tile = k.sb(name, [P, cols(pack)])
            at = 0
            for what, n in pack:
                k.w[what] = tile[:, at:at + n]
                at += n
        row = k.sb("rows", [1, cols(ROWS)])
        at = 0
        for what, n in ROWS:
            k.w[what] = row[:, at:at + n]
            at += n
        for what, names in BELOW.items():
            for i, name in enumerate(names):
                k.w[name] = k.w[what][32 * (i + 1):32 * (i + 1) + 1, :]
        k.x_dram, k.ctx_dram, k.ctxT_dram, k.out_dram = dram["x"], dram["ctx"], dram["ctxT"], dram["out"]
        k.x = [k.sb(f"x{i}", [P, NT, D]) for i in range(2)]
        k.ctxT = [k.sb(f"ctxT{i}", [P, T]) for i in range(2)]
        k.x_in = k.sb("x_in", [P, NT, D])
        k.ctx_tok = k.sb("ctx_tok", [P, NT, D])
        k.half, k.tg, k.kbias = k.sb("minus_half", [P, E16]), k.sb("tanh_g", [P, 8]), k.sb("k_stab", [P, 1])
        k.sn, k.sig = k.sb("sim_unit", [P, E16]), k.sb("sigmoid_gates", [P, E16])
        k.bq_scaled = {f"bq{L}": k.sb(f"bq{L}_scaled", [P, 1]) for L in (0, 2, 3)}

        all_ctx, sq = k.sb("mix_wb", [P, E16, T]), Workspace(k, "Q").whole
        ctx16, sq16 = all_ctx[:, 0:8, :].rearrange("p a b -> p (a b)"), sq[:, 0:8, :].rearrange("p a b -> p (a b)")
        head_sq, least = Workspace(k, "P").p[:, 0, 0, :], k.sb("setup_least", [P, 1])
        least1, simsq, simn = k.sb("setup_least1", [1, 1]), k.sb("setup_simsq", [P, E16]), k.sb("setup_simn", [P, E16])
        th = k.sb("setup_tanh", [P, E16])
        setup = ctx.enter_context(ExitStack())
        setup_sems = {n: setup.enter_context(nc.semaphore(f"setup_{n}")) for n in (
            "preset", "dve", "least", "least_row", "least1", "least_bc", "g_ps", "gates_ps", "gates_th", "simsq", "sim_ps",
            "simn_in", "simn")}
        preset, chain = setup_sems["preset"], Chain(setup_sems["dve"])
        least_ready, least_row, least1_ready, least_bc = (setup_sems[n] for n in ("least", "least_row", "least1", "least_bc"))
        g_ps, gates_ps, gates_th, simsq_ready, sim_ps, simn_in, simn_ready = (
            setup_sems[n] for n in ("g_ps", "gates_ps", "gates_th", "simsq", "sim_ps", "simn_in", "simn"))
        lg, prP = k.sb("mix_lg", [P, NT, E16 + 6]), k.sb("rt_prP", [P, NT, E8 + 6])
        combP = k.sb("rt_combP", [P, NT, E8 + 1])
        heads_v = [k.sb(n, [P, NT, H, PAD]) for n in ("att_vP", "att_vQ")]
        wide_v = k.sb("wide_v", [P, NT, H1, HD1 + 1])
        with nc.Block() as block:
            @block.sync
            def _(sp):
                sp.dma_start(ctx16, dram["ctx"].rearrange("(p n) d -> p (n d)", p=P)).then_inc(all_ctx_in, 16)
                sp.dma_start(row[:, :], dram["rows"]).then_inc(rows_in, 16)
                for name, pack in PACKS:
                    sp.dma_start(k.bufs[name][:, :], dram[name]).then_inc(weights_in[name], 16)
                for name, pack in PACKS:
                    sp.wait_ge(weights_in[name], 16)

            @block.gpsimd
            def _(pool):
                nc.gpsimd.memset(k.half[:, :], -0.5).then_inc(preset, 1)
                nc.gpsimd.memset(lg[:, :, E16:], SENT).then_inc(preset, 1)
                nc.gpsimd.memset(prP[:, :, E8:], SENT).then_inc(preset, 1)
                nc.gpsimd.memset(combP[:, :, E8:], 1.0).then_inc(preset, 1)
                for n, v in enumerate(heads_v):
                    nc.gpsimd.memset(v[:, :, :, HD:HD + 1], 1.0).then_inc(preset, 1)
                    nc.gpsimd.memset(v[:, :, :, HD + 1:], 0.0).then_inc(preset, 1)
                nc.gpsimd.memset(wide_v[:, :, :, HD1:], 1.0).then_inc(preset, 1)
                pool.wait_ge(preset, 1)
                pool.wait_ge(simn_in, 1)
                nc.gpsimd.tensor_tensor(simn[:, :], simsq[:, :], k.half[:, :], ALU.pow).then_inc(simn_ready, 1)

            @block.vector
            def _(dve):
                v = nc.vector
                dve.wait_ge(all_ctx_in, 16)
                chain.link(dve, v.tensor_tensor(sq16, ctx16, ctx16, ALU.mult))
                chain.link(dve, v.tensor_reduce(head_sq, sq16.rearrange("p (n d) -> p n d", d=HD), AX.X, ALU.add))
                v.tensor_reduce(least[:, :], head_sq, AX.X, ALU.min).then_inc(least_ready, 1)
                dve.wait_ge(least_row, 1)
                v.tensor_reduce(least1[:, :], k.psum[0][0:1, 0:P], AX.X, ALU.min).then_inc(least1_ready, 1)
                dve.wait_ge(least_bc, 1)
                v.tensor_scalar(k.kbias[:, :], k.psum[1][:, 0:1], 0.5 * RF_SCALE ** 2, None, ALU.mult)
                dve.wait_ge(weights_in["pack4"], 16)
                v.tensor_tensor(simsq[:, :], k.w["sim"], k.w["sim"], ALU.mult).then_inc(simsq_ready, 1)
                dve.wait_ge(sim_ps, 1)
                v.tensor_scalar(simsq[:, :], k.psum[4][:, 0:E16], 1e-24, None, ALU.max).then_inc(simn_in, 1)
                dve.wait_ge(simn_ready, 1)
                v.tensor_tensor(k.sn[:, :], k.w["sim"], simn[:, :], ALU.mult)
                dve.wait_ge(gates_th, 1)
                v.tensor_scalar(k.sig[:, :], th[:, :], 0.5, 0.5, ALU.mult, ALU.add)
                for L, name in ((0, "pack1"), (2, "pack3"), (3, "pack4")):
                    dve.wait_ge(weights_in[name], 16)
                    v.tensor_scalar(k.bq_scaled[f"bq{L}"][:, :], k.w[f"bq{L}"], HD ** -0.5, None, ALU.mult)

            @block.tensor
            def _(pe):
                pe.wait_ge(weights_in["const"], 16)
                pe.wait_ge(least_ready, 1)
                nc.tensor.transpose(k.psum[0][0:1, 0:P], least[:, :], k.w["ident"]).then_inc(least_row, 1)
                pe.wait_ge(least1_ready, 1)
                nc.tensor.matmul(k.psum[1][:, 0:1], k.w["ones"][0:1, :], least1[:, :], start=True, stop=True).then_inc(least_bc, 1)
                pe.wait_ge(rows_in, 16)
                nc.tensor.matmul(k.psum[2][:, 0:8], k.w["ones"][0:1, :], k.w["g"], start=True, stop=True).then_inc(g_ps, 1)
                nc.tensor.matmul(k.psum[3][:, 0:E16], k.w["ones"][0:1, :], k.w["gates"], start=True, stop=True).then_inc(gates_ps, 1)
                pe.wait_ge(simsq_ready, 1)
                nc.tensor.matmul(k.psum[4][:, 0:E16], k.w["ones"], simsq[:, :], start=True, stop=True).then_inc(sim_ps, 1)

            @block.scalar
            def _(act):
                act.wait_ge(g_ps, 1)
                nc.scalar.activation(k.tg[:, :], k.psum[2][:, 0:8], ACT.Tanh)
                act.wait_ge(gates_ps, 1)
                nc.scalar.activation(th[:, :], k.psum[3][:, 0:E16], ACT.Tanh, scale=0.5).then_inc(gates_th, 1)
        numbers = [q.num for q in setup_sems.values()]
        nc.all_engine_barrier(sems_to_clear=range(min(numbers), max(numbers) + 1))
        setup.close()
        Chunk0(k, 0, 0, 0)
        for make in (Chunk1, Chunk2, Chunk3):
            make(k, 0)

        run_block(k, [Chunk0(k, 0, None, 0)])
        run_block(k, [Chunk1(k, 0), Chunk0(k, 1, None, 1)])
        with nc.Fori(0, NB // 2 - 1) as n:
            i = n * 2
            run_block(k, [Chunk1(k, 1), Chunk2(k, 0)])
            run_block(k, [Chunk3(k, 0), Chunk2(k, 1)])
            run_block(k, [Chunk3(k, 1), Chunk0(k, 0, i, i + 2)])
            run_block(k, [Chunk1(k, 0), Chunk0(k, 1, i + 1, i + 3)])
        run_block(k, [Chunk1(k, 1), Chunk2(k, 0)])
        run_block(k, [Chunk3(k, 0), Chunk2(k, 1)])
        run_block(k, [Chunk3(k, 1), Chunk0(k, 0, NB - 2, None)])
        run_block(k, [Chunk0(k, 1, NB - 1, None)])


def kernel(**inputs):
    import concourse.bacc as bacc
    from concourse.bass_utils import run_bass_kernel_spmd

    a = {n: np.asarray(v) for n, v in inputs.items()}
    f = np.float32

    def with_rows_below(b, rows):
        out = np.zeros((P, D), f)
        out[:b.shape[0]] = b
        for i, row in enumerate(rows):
            out[32 * (i + 1)] = row
        return out

    def side_by_side(w):
        return w.transpose(1, 0, 2).reshape(w.shape[1], -1)

    rf = np.zeros((NG, HG, HD, NG, HG, PAD), f)
    hsum = np.zeros((NG, HG, HD, NG, HG, PAD), f)
    for g in range(NG):
        for h in range(HG):
            rf[g, h, :, g, h, :] = a["L0_xattn_random_features"]
            hsum[g, h, :, g, h, :] = -0.5 * RF_SCALE
    w_qkv, b_qkv = a["L0_ffn_W_qkv"], a["L0_ffn_b_qkv"]
    parts = {
        "ident": np.eye(P, dtype=f), "tri": np.triu(np.ones((P, P), f)), "ones": np.ones((P, P), f),
        "hsum": hsum.reshape(D, -1), "head_rows": np.kron(np.eye(H, dtype=f), np.ones((HD, 1), f)),
        "group_rows": np.kron(np.eye(HG, dtype=f), np.ones((PAD, 1), f)),
        "rf": rf.reshape(D, -1), "wq0": w_qkv[:, 0:D], "wk0": w_qkv[:, D:2 * D],
        "wv0": w_qkv[:, 2 * D:], "gate0": a["L0_ffn_W_gate"], "exp0": side_by_side(a["L0_ffn_W_experts"]),
        "bq0": b_qkv[0:D].reshape(D, 1), "bk0": b_qkv[D:2 * D].reshape(D, 1),
        "wq1": a["L1_xattn_Wq"], "wk1": a["L1_xattn_Wkv"][:, :H1 * HD1], "wv1": a["L1_xattn_Wkv"][:, H1 * HD1:],
        "wo1": side_by_side(a["L1_xattn_Wout"].reshape(4, P, D)),
        "router1": a["L1_ffn_w_router"], "fc1": side_by_side(a["L1_ffn_fc1_w"]), "fc2": side_by_side(a["L1_ffn_fc2_w"]),
        "gate_w": a["L1_ffn_gate_w"], "up_w": a["L1_ffn_up_w"], "down_w": side_by_side(a["L1_ffn_down_w"].reshape(2, P, D)),
        "router2": a["L2_ffn_router_w"],
        "b1": np.concatenate([a["L2_ffn_shared_b1"].reshape(1, FF2, P), a["L2_ffn_exp_b1"].reshape(E8, FF2, P)]).transpose(2, 0, 1).reshape(P, -1),
        "w1": side_by_side(np.concatenate([a["L2_ffn_shared_w1"].reshape(1, D, -1), a["L2_ffn_exp_w1"]])),
        "w2": side_by_side(np.concatenate([a["L2_ffn_shared_w2"].reshape(FF2, P, D), a["L2_ffn_exp_w2"].reshape(E8 * FF2, P, D)])),
        "sim": a["L3_ffn_sim_matrix"],
        "qp": side_by_side(a["L3_ffn_q_proj"]), "kp": side_by_side(a["L3_ffn_k_proj"]),
        "vp": side_by_side(a["L3_ffn_v_proj"]), "op": side_by_side(a["L3_ffn_o_proj"]),
        "bv0": b_qkv[2 * D:], "bgate0": a["L0_ffn_b_gate"], "bout1": a["L1_xattn_bout"], "br2": a["L2_ffn_router_b"],
        "gates": a["L3_ffn_gates"], "g": np.concatenate([a["g_xattn"], a["g_ffn"]]),
    }
    for L in (2, 3):
        for c in "qkvo":
            parts[f"w{c}{L}"] = a[f"L{L}_xattn_W{c}"].T
        parts[f"bq{L}"], parts[f"bk{L}"] = (a[f"L{L}_xattn_b{c}"].reshape(D, 1) for c in "qk")
        parts[f"bv{L}"], parts[f"bo{L}"] = (a[f"L{L}_xattn_b{c}"] for c in "vo")
    parts["bias0"] = with_rows_below(a["L0_ffn_b_experts"], [parts[n] for n in BELOW["bias0"]])
    parts["bias2"] = with_rows_below(np.concatenate([a["L2_ffn_exp_b2"], a["L2_ffn_shared_b2"].reshape(1, D)]),
                                     [parts[n] for n in BELOW["bias2"]])
    ctx2d = a["ctx_1024"].reshape(NB * T, D)
    arrays = {name: np.concatenate([parts[n] for n, _ in pack], axis=1) for name, pack in PACKS}
    arrays["rows"] = np.concatenate([parts[n] for n, _ in ROWS]).reshape(1, -1)
    arrays["x"], arrays["ctx"], arrays["ctxT"] = a["x"].reshape(NB * T, D), ctx2d, ctx2d.T
    arrays = {f"in_{n}": np.ascontiguousarray(v) for n, v in arrays.items()}

    nc = bacc.Bacc("TRN2", target_bir_lowering=False, num_devices=1)
    dram = {n[3:]: nc.dram_tensor(n, v.shape, F32, kind="ExternalInput").ap() for n, v in arrays.items()}
    dram["out"] = nc.dram_tensor("out_x", (NB * T, D), F32, kind="ExternalOutput").ap()
    flamingo(nc, dram)
    r = run_bass_kernel_spmd(nc, [arrays], core_ids=[0])
    return r.results[0]["out_x"].reshape(NB, T, D)
```

```python
from contextlib import ExitStack

import numpy as np
import concourse.bass as bass
from concourse import mybir

F32, BF16 = mybir.dt.float32, mybir.dt.bfloat16
ACT = mybir.ActivationFunctionType
ALU = mybir.AluOpType
AX = mybir.AxisListType

NB, T, D = 8, 256, 128
P = 128
NT = T // P
H, HD = 16, 8
PAD = 32
HG = P // PAD
NG = H // HG
M_RF = 32
H1, HD1 = 8, 64
E8, E16 = 8, 16
PARTS = 3
FF2 = 4
SENT, GONE = -1.0e38, -3.0e38
RF_SCALE = float(D) ** -0.25

CONST = [("ident", 128), ("tri", 128), ("ones", 128), ("hsum", NG * 128), ("head_rows", H), ("group_rows", HG), ("part_rows", E16),
         ("sim", E16), ("bq0", 1), ("bk0", 1), ("bq2", 1), ("bk2", 1), ("bq3", 1), ("bk3", 1)]
PACK1 = [("rf", NG * 128), ("wq0", D), ("wk0", D), ("wv0", 128), ("gate0", E8), ("exp0", E8 * D), ("bias0", D)]
PACK2 = [("wq1", H1 * HD1), ("wk1", H1 * HD1), ("wv1", H1 * HD1), ("wo1", 4 * D)]
PACK3 = [("router1", E8), ("fc1", E8 * 2 * D), ("fc2", E8 * D), ("gate_w", 2 * D), ("up_w", 2 * D), ("down_w", 2 * D),
         ("wq2", D), ("wk2", D), ("wv2", 128), ("wo2", 128),
         ("router2", E8), ("b1", (E8 + 1) * FF2), ("bias2", D)]
PACK3W = [("w1", (E8 + 1) * FF2 * 128), ("w2", (E8 + 1) * FF2 * 128)]
PACK4 = [("wq3", D), ("wk3", D), ("wv3", 128), ("wo3", 128)]
PACK4W = [("qp", E16 * D), ("kp", E16 * D), ("vp", E16 * D), ("op", E16 * D)]
ROWS = [("bgate0", E8), ("br2", E8), ("gates", E16), ("g", 8)]
BELOW = {"bias0": ["bv0", "bout1", "bv2"], "bias2": ["bo2", "bv3", "bo3"]}
FIRST = [("const", CONST), ("pack1", PACK1)]
LATER = [("pack2", PACK2), ("pack3", PACK3), ("pack3w", PACK3W),
         ("pack4", PACK4), ("pack4w", PACK4W)]
PACKS = FIRST + LATER

PACE_1_2 = {"wide": (1.929, 1.4, 1.552, 1.4, 0.84), "gated": (1.4, 2.154, 1.083, 1.904, 0.246),
            "heads2": (3.2, 1.737, 1.914, 1.549, 1.82), "gelu": (2.026, 2.169, 3.93, 1.8, 0.785)}
PACE_3_2 = {"heads3": (2, 1.515, 1.515, 1.515, 1.4), "gated": (1.4, 2.082, 1.899, 1.899, 0.563),
            "heads2": (3.2, 2.182, 1.914, 1.914, 1.82), "gelu": (1.949, 1.8, 1.8, 1.8, 1.288)}
PACE_3_0 = {"heads3": (2, 1.4, 1.4, 1.4, 1.4), "mixed": (1.6, 3.4, 3.4, 3.4, 0.505),
            "performer": (2.303, 0.9, 0.966, 0.9, 1.17), "heads0": (2, 1.65, 1.65, 1.65, 1.302),
            "linear": (1.231, 0.919, 0.84, 0.724, 0.87)}
PACE_1_0 = {"wide": (2.149, 1.4, 1.935, 1.585, 0.84), "mixed": (1.6, 3.679, 3.4, 3.444, 1.255),
            "performer": (2.314, 0.928, 0.927, 0.9, 1.589), "heads0": (3.145, 1.65, 2.041, 1.655, 2.144),
            "linear": (0.283, 0.549, 0.84, 0.669, 1.536)}
PACE_FIRST = {"wide": (1.807, 1.4, 2.491, 1.4, 0.84), "performer": (1.394, 0.9, 0.762, 0.9, 2.003),
              "heads0": (2.774, 1.65, 1.65, 2.126, 1.29), "linear": (0.86, 3.221, 0.65, 0.84, 0.895)}
PACE_LAST = {"heads3": (2.009, 1.945, 1.237, 1.332, 1.051), "mixed": (1.465, 3.618, 2.024, 3.593, 0.649)}


def cols(pack):
    return sum(n for _, n in pack)


class Chain:

    def __init__(self, sem):
        self.sem, self.n = sem, 0

    def link(self, eng, ins):
        self.n += 1
        ins.then_inc(self.sem, 1)
        eng.wait_ge(self.sem, self.n)

    def group(self, eng, instructions):
        self.n += len(instructions)
        for ins in instructions:
            ins.then_inc(self.sem, 1)
        eng.wait_ge(self.sem, self.n)


class Shared:

    def __init__(self, nc, ctx):
        self.nc, self.ctx = nc, ctx
        self.sems, self.bufs, self.w = {}, {}, {}
        self.first = self.last = None
        self.psum = [ctx.enter_context(nc.psum_tensor(f"bank{i}", [P, 512], F32)) for i in range(8)]

    def sb(self, name, shape, dtype=F32):
        if name not in self.bufs:
            self.bufs[name] = self.ctx.enter_context(self.nc.sbuf_tensor(name, shape, dtype))
        return self.bufs[name]

    def one(self, name):
        r = max((32 * (names.index(name) + 1) for names in BELOW.values() if name in names), default=0)
        return self.w["ones"][r:r + 1, :]

    def turn(self, out, tile):
        return self.nc.tensor.transpose(out, tile, self.w["ident"])

    def lasting_sem(self, name):
        return self.ctx.enter_context(self.nc.semaphore(name))

    def sem(self, name):
        if name not in self.sems:
            s = self.ctx.enter_context(self.nc.semaphore(name))
            self.first = s.num if self.first is None else min(self.first, s.num)
            self.last = s.num if self.last is None else max(self.last, s.num)
            self.sems[name] = s
        return self.sems[name]


class Workspace:

    def __init__(self, k, side):
        self.whole = k.sb(f"work{side}", [P, 4 * NG, T])
        self.kT, self.qT, self.oT, self.extra = (self.whole[:, i * NG:(i + 1) * NG, :] for i in range(4))
        self.work = self.extra.rearrange("p (u j) t -> p u j t", j=NT)
        self.v = k.sb(f"att_v{side}", [P, NT, H, PAD])
        self.p, self.pT = k.sb(f"att_p{side}", [P, 2, NT, T])[:, :, :, :], k.sb(f"att_pT{side}", [P, 2, NT, T])[:, :, :, :]


class Units:

    def units(self, first, count, rounds, tail, closing):
        self.first, self.count, self.rounds = first, count, rounds
        self.closing_from = first + count * rounds + tail
        self.steps = self.closing_from + closing

    def at(self, s, lag, r):
        u, rest = divmod(s - self.first - r, self.rounds)
        return u - lag if s >= self.first and rest == 0 and 0 <= u - lag < self.count else -1

    def close(self, s):
        return s - self.closing_from if s >= self.closing_from else -1

    def phase(self, s):
        if s >= self.closing_from:
            return 4
        return 0 if s < self.first else 1 + 3 * (s - self.first) // (self.closing_from - self.first)


class TopSelect(Units):
    OPS = 4

    def top_buffers(self, k, buf, n):
        self.work, self.rest = buf.work, k.sb("top_rest", [P, NT, T])
        self.lead, self.eight = k.sb("top_lead", [P, 2, NT, 8]), k.sb("top_eight", [P, NT, 8])
        self.top, self.rest_done = k.sem(n + "top"), k.sem(n + "rest")
        self.topn = 0

    def top_count(self, u, r):
        return self.OPS * (u * self.rounds + r + 1)

    def select(self, dve, u, r):
        nc, sc = self.k.nc, self.banks[u % 2]
        if r == 0:
            dve.wait_ge(self.scores, u + 1)
            if u >= 2:
                dve.wait_ge(self.rest_done, u - 1)
        for replace in range(2):
            for j in range(NT):
                if self.topn >= 2:
                    dve.wait_ge(self.top, self.topn - 1)
                src = sc[:, j * T:(j + 1) * T] if r == 0 else self.work[:, u % 2, j, :]
                eight = self.lead[:, u % 2, j, :] if r == 0 else self.eight[:, j, :]
                if replace:
                    ins = nc.vector.match_replace(self.work[:, u % 2, j, :], eight, src, GONE)
                else:
                    ins = nc.vector.max(eight, src)
                ins.then_inc(self.top, 1)
                self.topn += 1

    def negative_max(self, pool, u):
        pool.wait_ge(self.top, self.top_count(u, 0) - NT)
        self.k.nc.gpsimd.tensor_scalar(self.nmax[:, u, :], self.lead[:, u % 2, :, 0], -1.0, 1.0, ALU.mult,
                                       ALU.mult).then_inc(self.max_ready, 1)

    def exp_scores(self, act, u):
        act.wait_ge(self.max_ready, u + 1)
        if self.topk:
            act.wait_ge(self.top, self.top_count(u, 0))
        if u >= 2:
            act.wait_ge(self.pT_ps, u - 1)
        for j in range(NT):
            e = self.k.nc.scalar.activation(self.p[:, u % 2, j, :], self.banks[u % 2][:, j * T:(j + 1) * T], ACT.Exp,
                                            bias=self.nmax[:, u, j:j + 1])
        e.then_inc(self.exp_done, 1)

    def exp_rest(self, act, u):
        act.wait_ge(self.top, self.top_count(u, self.rounds - 1))
        if u >= 1:
            act.wait_ge(self.p_ready, u)
        for j in range(NT):
            e = self.k.nc.scalar.activation(self.rest[:, j, :], self.work[:, u % 2, j, :], ACT.Exp, bias=self.nmax[:, u, j:j + 1])
        e.then_inc(self.rest_done, 1)

    def keep_top(self, pool, u):
        pool.wait_ge(self.rest_done, u + 1)
        v = self.p[:, u % 2, :, :]
        self.k.nc.gpsimd.tensor_tensor(v, v, self.rest[:, :, :], ALU.subtract).then_inc(self.p_ready, 1)

    def turn_p(self, pe, u):
        pe.wait_ge(self.p_ready, u + 1)
        if u >= 1:
            pe.wait_ge(self.pT_copied, u)
        for kt in range(NT):
            for j in range(NT):
                tr = self.k.turn(self.banks[2][:, kt * T + j * P:kt * T + (j + 1) * P], self.p[:, u % 2, j, kt * P:(kt + 1) * P])
        tr.then_inc(self.pT_ps, 1)

    def copy_pT(self, act, u):
        act.wait_ge(self.pT_ps, u + 1)
        if u >= 2:
            act.wait_ge(self.pv_done, u - 1)
        self.k.nc.scalar.activation(self.pT[:, u % 2, :, :], self.banks[2][:, :], ACT.Copy).then_inc(self.pT_copied, 1)


class LayerNorm:

    def __init__(self, k, side, tag, x, bank):
        self.k, self.x, self.bank = k, x, bank
        self.y, self.yT = k.sb(f"y{side}", [P, NT, D]), k.sb(f"yT{side}", [P, T])
        self.stats, self.mv = k.sb(f"ln_stats{side}", [P, NT, 6]), k.sb(f"ln_mv{side}", [P, NT, 2])
        self.var, self.rstd = k.sb(f"ln_var{side}", [P, NT]), k.sb(f"ln_rstd{side}", [P, NT])
        n = f"ln{side}{tag}_"
        self.chain = Chain(k.sem(n + "dve"))
        self.var_ready, self.rstd_ready = k.sem(n + "var_ready"), k.sem(n + "rstd_ready")
        self.y_ready, self.turned, self.yT_ready = k.sem(n + "y_ready"), k.sem(n + "turned"), k.sem(n + "yT_ready")

    def dve_stats(self, dve):
        nc = self.k.nc
        self.chain.group(dve, [nc.vector.bn_stats(self.stats[:, j, :], self.x[:, j, :]) for j in range(NT)])
        self.chain.group(dve, [nc.vector.bn_aggr(self.mv[:, j, :], self.stats[:, j, :]) for j in range(NT)])
        nc.vector.tensor_scalar(self.var[:, :], self.mv[:, :, 1], 1e-5, None, ALU.add).then_inc(self.var_ready, 1)

    def dve_scale(self, dve):
        dve.wait_ge(self.rstd_ready, 1)
        for j in range(NT):
            self.k.nc.vector.tensor_scalar(self.y[:, j, :], self.x[:, j, :], self.mv[:, j, 0:1], self.rstd[:, j:j + 1],
                                           ALU.subtract, ALU.mult).then_inc(self.y_ready, 1)

    def pool(self, pool):
        pool.wait_ge(self.var_ready, 1)
        self.k.nc.gpsimd.tensor_tensor(self.rstd[:, :], self.var[:, :], self.k.half[:, 0:NT],
                                       ALU.pow).then_inc(self.rstd_ready, 1)

    def pe(self, pe):
        for j in range(NT):
            pe.wait_ge(self.y_ready, j + 1)
            self.k.turn(self.bank[:, j * P:(j + 1) * P], self.y[:, j, :]).then_inc(self.turned, 1)

    def act(self, act):
        act.wait_ge(self.turned, NT)
        self.k.nc.scalar.activation(self.yT[:, :], self.bank[:, 0:T], ACT.Copy).then_inc(self.yT_ready, 1)


class Performer(Units):
    RING = 4

    def __init__(self, k, side, x, ctxT, ctx_tok, banks, load, before):
        self.name = "performer"
        self.k, self.x, self.ctxT, self.ctx_tok, self.banks, self.load = k, x, ctxT, ctx_tok, banks, load
        self.before = before
        self.ln = LayerNorm(k, side, "a", x, banks[0])
        work = Workspace(k, side)
        self.ksq = work.pT[:, 0, 0, :]
        self.qf, self.kf, self.q1 = work.qT, work.kT, work.extra
        self.v = work.v
        self.a = [t.rearrange("p u j t -> p u (j t)")[:, u, 0:3 * P] for t in (work.p, work.pT) for u in range(2)]
        self.oT = work.oT
        self.den, self.tiny, self.o = k.sb("perf_den", [P, NT, H]), k.sb("perf_tiny", [P, NT, H]), self.ln.y
        n = "perf_"
        self.chain = Chain(k.sem(n + "dve"))
        self.ksq_ready, self.v_ready = k.sem(n + "ksq_ready"), k.sem(n + "v_ready")
        self.proj_ready, self.exp_ready, self.kf_ready = k.sem(n + "proj"), k.sem(n + "exp"), k.sem(n + "kf")
        self.q1_ready = k.sem(n + "q1")
        self.a_ps, self.a_copied, self.a_masked = k.sem(n + "a_ps"), k.sem(n + "a_copied"), k.sem(n + "a_masked")
        self.pv_done, self.oT_copied, self.back = k.sem(n + "pv"), k.sem(n + "oT"), k.sem(n + "back")
        self.units(4, H, 1, 3, 3)

    def pe(self, pe, s):
        nc, w, b = self.k.nc, self.k.w, self.banks
        if s == 0:
            pe.wait_ge(self.load, 3 * 16)
            pe.wait_ge(self.ksq_ready, 1)
            if self.before is not None:
                pe.wait_ge(self.before.o_copied, 1)
            for g in range(NG):
                out = b[2 + g // 2][:, (g % 2) * T:(g % 2 + 1) * T]
                nc.tensor.matmul(out, w["rf"][:, g * P:(g + 1) * P], self.ctxT[:, :], start=True, stop=False)
                nc.tensor.matmul(out, w["hsum"][:, g * P:(g + 1) * P], self.ksq, start=False,
                                 stop=True).then_inc(self.proj_ready, 1)
        if s == 1:
            if self.before is not None:
                pe.wait_ge(self.before.x_done, NT)
            self.ln.pe(pe)
        if s == 2:
            pe.wait_ge(self.ln.yT_ready, 1)
            for g in range(NG):
                nc.tensor.matmul(b[g // 2][:, (g % 2) * T:(g % 2 + 1) * T], w["rf"][:, g * P:(g + 1) * P], self.ln.yT[:, :],
                                 start=True, stop=True).then_inc(self.proj_ready, 1)
        u = self.at(s, 0, 0)
        if u >= 0:
            if u == 0:
                pe.wait_ge(self.kf_ready, 2)
                pe.wait_ge(self.exp_ready, 4)
            pe.wait_ge(self.q1_ready, u + 1)
            if u >= 2:
                pe.wait_ge(self.a_copied, u - 1)
            out, kf, q1 = b[u % 2], self.kf[:, u // HG, :], self.q1[:, u % self.RING, :]
            nc.tensor.matmul(out[:, 0:T], kf[:, 0:P], q1, start=True, stop=True)
            nc.tensor.matmul(out[:, T:T + P], kf[:, P:T], q1[:, P:T], start=True, stop=True).then_inc(self.a_ps, 1)
        u = self.at(s, 3, 0)
        if u >= 0:
            g, a = divmod(u, HG)
            pe.wait_ge(self.a_masked, u + 1)
            if u == 0:
                pe.wait_ge(self.v_ready, 1)
            if a == 0 and g > 0:
                pe.wait_ge(self.oT_copied, g)
            out = b[2][PAD * a:PAD * (a + 1), (g % 2) * T:(g % 2 + 1) * T]
            nc.tensor.matmul(out, self.v[:, 0, u, :], self.a[u % 4][:, 0:T], start=True, stop=False)
            nc.tensor.matmul(out[:, P:T], self.v[:, 1, u, :], self.a[u % 4][:, T:T + P], start=False,
                             stop=True).then_inc(self.pv_done, 1)
        if self.close(s) == 0:
            pe.wait_ge(self.oT_copied, NG)
            for j in range(NT):
                for g in range(NG):
                    self.k.turn(b[j][:, g * P:(g + 1) * P], self.oT[:, g, j * P:(j + 1) * P]).then_inc(self.back, 1)

    def act(self, act, s):
        nc, b = self.k.nc, self.banks
        if s == 1:
            if self.before is not None:
                act.wait_ge(self.before.out_ps, 1)
            self.ln.act(act)
            for half in range(2):
                act.wait_ge(self.proj_ready, 2 * half + 2)
                nc.scalar.activation(self.kf[:, 2 * half:2 * half + 2, :], b[2 + half][:, :], ACT.Exp, bias=self.k.kbias[:, 0:1],
                                     scale=RF_SCALE).then_inc(self.exp_ready, 1)
        if s == 2:
            for half in range(2):
                act.wait_ge(self.proj_ready, NG + 2 * half + 2)
                nc.scalar.activation(self.qf[:, 2 * half:2 * half + 2, :], b[half][:, :], ACT.Exp,
                                     scale=RF_SCALE).then_inc(self.exp_ready, 1)
        u = self.at(s, 1, 0)
        if u >= 0:
            act.wait_ge(self.a_ps, u + 1)
            if u >= 4:
                act.wait_ge(self.pv_done, u - 3)
            nc.scalar.activation(self.a[u % 4], b[u % 2][:, 0:3 * P], ACT.Copy).then_inc(self.a_copied, 1)
        u = self.at(s, 3, 0)
        if u >= 0 and u % HG == HG - 1:
            g = u // HG
            act.wait_ge(self.pv_done, u + 1)
            nc.scalar.activation(self.oT[:, g, :], b[2][:, (g % 2) * T:(g % 2 + 1) * T], ACT.Copy).then_inc(self.oT_copied, 1)

    def pool_q1(self, pool, u):
        if u >= self.RING:
            pool.wait_ge(self.a_ps, u - self.RING + 1)
        g, a = divmod(u, HG)
        self.k.nc.gpsimd.tensor_scalar(self.q1[:, u % self.RING, :], self.qf[:, g, :], 1e-4,
                                       self.k.w["group_rows"][:, a:a + 1], ALU.add, ALU.mult).then_inc(self.q1_ready, 1)

    def pool(self, pool, s):
        nc = self.k.nc
        if s == 0:
            self.ln.pool(pool)
            pool.wait_ge(self.load, 3 * 16)
            if self.before is not None:
                pool.wait_ge(self.before.o_copied, 1)
            nc.gpsimd.tensor_tensor(self.ksq, self.ctxT[:, :], self.ctxT[:, :], ALU.mult).then_inc(self.ksq_ready, 1)
            nc.gpsimd.tensor_copy(self.v[:, :, :, 0:HD],
                                  self.ctx_tok[:, :, :].rearrange("p j (h d) -> p j h d", d=HD)).then_inc(self.v_ready, 1)
        if s == 2:
            for half in range(2):
                pool.wait_ge(self.exp_ready, half + 1)
                v = self.kf[:, 2 * half:2 * half + 2, :]
                nc.gpsimd.tensor_scalar(v, v, 1e-4, 1.0, ALU.add, ALU.mult).then_inc(self.kf_ready, 1)
            pool.wait_ge(self.exp_ready, 4)
            for u in range(2):
                self.pool_q1(pool, u)
        u = self.at(s, 0, 0) + 2
        if 2 <= u < H:
            self.pool_q1(pool, u)
        u = self.at(s, 2, 0)
        if u >= 0:
            pool.wait_ge(self.a_copied, u + 1)
            v = self.a[u % 4].rearrange("p (b t) -> p b t", t=P)[:, 0:3:2, :]
            nc.gpsimd.tensor_tensor(v, v, self.k.w["tri"].unsqueeze(1).broadcast_to([P, 2, P]),
                                    ALU.mult).then_inc(self.a_masked, 1)

    def dve(self, dve, s):
        nc = self.k.nc
        if s == 0:
            dve.wait_ge(self.load, 3 * 16)
            self.ln.dve_stats(dve)
        if s == 1:
            self.ln.dve_scale(dve)
        if self.close(s) == 2:
            v, link = nc.vector, lambda ins: self.chain.link(dve, ins)
            dve.wait_ge(self.back, NT * NG)
            t = [self.banks[j][:, :].rearrange("p (h c) -> p h c", c=PAD) for j in range(NT)]
            self.chain.group(dve, [v.tensor_scalar(self.den[:, j, :], t[j][:, :, HD], 1.0 / M_RF, None, ALU.mult) for j in range(NT)])
            link(v.tensor_scalar(self.tiny[:, :, :], self.den[:, :, :], 1e-6, 2e-6, ALU.is_le, ALU.mult))
            link(v.tensor_tensor(self.den[:, :, :], self.den[:, :, :], self.tiny[:, :, :], ALU.add))
            link(v.reciprocal(self.den[:, :, :], self.den[:, :, :]))
            self.chain.group(dve, [v.scalar_tensor_tensor(
                out=self.o[:, j, :].rearrange("p (h d) -> p h d", d=HD), in0=t[j][:, :, 0:HD], scalar=1.0 / M_RF,
                in1=self.den[:, j, :].unsqueeze(2).broadcast_to([P, H, HD]), op0=ALU.mult, op1=ALU.mult) for j in range(NT)])
            link(v.scalar_tensor_tensor(out=self.x[:, :, :], in0=self.o[:, :, :], scalar=self.k.tg[:, 0:1],
                                        in1=self.x[:, :, :], op0=ALU.mult, op1=ALU.add))


class HeadAttention(TopSelect):

    RING = 4

    def __init__(self, k, side, layer, x, ctxT, banks, tag, topk=0, gate=None, router=None, before=None):
        self.name = f"heads{layer}"
        self.k, self.x, self.banks, self.topk, self.layer, self.gate = k, x, banks, topk, layer, gate
        self.before = before
        self.order = "kqv" if ctxT is None else "kvq"
        self.ln = LayerNorm(k, side, tag, x, banks[0])
        self.rt = None if router is None else Router(k, side, "a", router[0], self.ln.yT, *router[1:], banks[0], banks[3])
        self.kvT = self.ln.yT if ctxT is None else ctxT
        buf = Workspace(k, side)
        self.kT, self.qT, self.q1 = buf.kT[:, 0, :], buf.kT[:, 1, :], buf.qT
        self.v, self.p, self.pT, self.oT = buf.v, buf.p, buf.pT, buf.oT
        self.nmax = k.sb(f"att_nmax{side}", [P, H, NT])
        self.rden, self.o = k.sb(f"att_rden{side}", [P, NT, H]), self.ln.y
        self.otT = self.ln.yT
        n = f"att{side}_"
        self.chain = Chain(k.sem(n + "dve"))
        self.proj, self.proj_copied = k.sem(n + "proj"), k.sem(n + "proj_copied")
        self.scores, self.max_ready, self.exp_done = k.sem(n + "scores"), k.sem(n + "max"), k.sem(n + "exp")
        self.pT_ps, self.pT_copied = k.sem(n + "pT_ps"), k.sem(n + "pT")
        self.pv_done, self.oT_copied, self.back = k.sem(n + "pv"), k.sem(n + "oT"), k.sem(n + "back")
        self.o_ready, self.o_turned, self.otT_ready = k.sem(n + "o"), k.sem(n + "o_turned"), k.sem(n + "otT")
        self.out_ps, self.q1_ready = k.sem(n + "out"), k.sem(n + "q1")
        closing = 0 if gate is None else 6
        if topk:
            self.top_buffers(k, buf, n)
            self.p_ready = k.sem(n + "p")
            self.units(3, H, topk // 8, 5, closing)
            self.EXP, self.TURN, self.COPY, self.PV = (0, 1), (1, 3), (1, 3), (2, 0)
        else:
            self.p_ready = self.exp_done
            self.units(4, H, 1, 3, closing)
            self.EXP, self.TURN, self.COPY, self.PV = (1, 0), (2, 0), (2, 0), (3, 0)

    def score(self, pe, u):
        if u == 0:
            pe.wait_ge(self.proj_copied, 3)
            if self.rt is not None:
                pe.wait_ge(self.rt.e_ready, 1)
        pe.wait_ge(self.q1_ready, u + 1)
        if u >= 2:
            pe.wait_ge(self.exp_done, u - 1)
        for j in range(NT):
            mm = self.k.nc.tensor.matmul(self.banks[u % 2][:, j * T:(j + 1) * T], self.q1[:, u % self.RING, j * P:(j + 1) * P],
                                         self.kT, start=True, stop=True)
        mm.then_inc(self.scores, 1)

    def projected(self, s):
        early = self.order[0:2] if self.order == "kvq" else ""
        return early if s == 0 else self.order[len(early):] if s == 2 else ""

    def project(self, pe, what):
        nc, w, b, L = self.k.nc, self.k.w, self.banks, self.layer
        if what == "k":
            mm = nc.tensor.matmul(b[2][:, 0:T], w[f"wk{L}"], self.kvT[:, :], start=True, stop=True)
        elif what == "q":
            mm = nc.tensor.matmul(b[3][:, 0:T], w[f"wq{L}"], self.ln.yT[:, :], start=True, stop=True)
        else:
            for j in range(NT):
                out = b[1][:, j * D:(j + 1) * D]
                nc.tensor.matmul(out, self.kvT[:, j * P:(j + 1) * P], w[f"wv{L}"], start=True, stop=False)
                mm = nc.tensor.matmul(out, self.k.one(f"bv{L}"), w[f"bv{L}"], start=False, stop=True)
        mm.then_inc(self.proj, 1)

    def pe(self, pe, s):
        nc, w, b, L = self.k.nc, self.k.w, self.banks, self.layer
        if s == 1:
            self.ln.pe(pe)
        if s == 0 and self.before is not None:
            self.before.wait_banks(pe)
        if s == 2:
            pe.wait_ge(self.ln.yT_ready, 1)
        for what in self.projected(s):
            self.project(pe, what)
        if s == 2:
            if self.rt is not None:
                self.rt.pe_logits(pe)
        if s == 5 and self.rt is not None:
            self.rt.pe_turn(pe)
        if self.topk:
            if s == 2:
                self.score(pe, 0)
                self.score(pe, 1)
            u = self.at(s, 0, 2) + 2
            if 2 <= u < H:
                self.score(pe, u)
        else:
            u = self.at(s, 0, 0)
            if u >= 0:
                self.score(pe, u)
        u = self.at(s, *self.TURN)
        if u >= 0:
            self.turn_p(pe, u)
        u = self.at(s, *self.PV)
        if u >= 0:
            g, a = divmod(u, HG)
            pe.wait_ge(self.pT_copied, u + 1)
            if u == 0 and self.rt is not None:
                pe.wait_ge(self.rt.combT_ready, 1)
            if a == 0 and g > 0:
                pe.wait_ge(self.oT_copied, g)
            for kt in range(NT):
                mm = nc.tensor.matmul(b[3][PAD * a:PAD * (a + 1), (g % 2) * T:(g % 2 + 1) * T], self.v[:, kt, u, :],
                                      self.pT[:, u % 2, kt, :], start=(kt == 0), stop=(kt == NT - 1))
            mm.then_inc(self.pv_done, 1)
        c = self.close(s)
        if c == 0:
            self.pe_back(pe)
        if c == 3:
            pe.wait_ge(self.o_ready, 2)
            for j in range(NT):
                tr = self.k.turn(b[2][:, j * P:(j + 1) * P], self.o[:, j, :])
            tr.then_inc(self.o_turned, 1)
        if c == 4:
            pe.wait_ge(self.otT_ready, 1)
            for j in range(NT):
                out = b[3][:, j * D:(j + 1) * D]
                nc.tensor.matmul(out, self.otT[:, j * P:(j + 1) * P], w[f"wo{L}"], start=True, stop=False)
                mm = nc.tensor.matmul(out, self.k.one(f"bo{L}"), w[f"bo{L}"], start=False, stop=True)
            mm.then_inc(self.out_ps, 1)

    def pe_back(self, pe):
        pe.wait_ge(self.oT_copied, NG)
        for j in range(NT):
            for g in range(NG):
                tr = self.k.turn(self.banks[j][:, g * P:(g + 1) * P], self.oT[:, g, j * P:(j + 1) * P])
        tr.then_inc(self.back, 1)

    def dve_normalise(self, dve):
        nc = self.k.nc
        dve.wait_ge(self.back, 1)
        for j in range(NT):
            t = self.banks[j][:, :].rearrange("p (h c) -> p h c", c=PAD)
            self.chain.link(dve, nc.vector.reciprocal(self.rden[:, j, :], t[:, :, HD]))
            nc.vector.tensor_tensor(self.o[:, j, :].rearrange("p (h d) -> p h d", d=HD), t[:, :, 0:HD],
                                    self.rden[:, j, :].unsqueeze(2).broadcast_to([P, H, HD]),
                                    ALU.mult).then_inc(self.o_ready, 1)

    def act(self, act, s):
        nc, b, L = self.k.nc, self.banks, self.layer
        if s == 1:
            self.ln.act(act)
        for what in self.projected(s):
            act.wait_ge(self.proj, self.order.index(what) + 1)
            if what == "v":
                e = nc.scalar.activation(self.v[:, :, :, 0:HD], b[1][:, 0:NT * D].rearrange("p (j h d) -> p j h d", j=NT, d=HD),
                                         ACT.Copy)
            elif what == "k":
                e = nc.scalar.activation(self.kT, b[2][:, 0:T], ACT.Identity, bias=self.k.w[f"bk{L}"])
            else:
                e = nc.scalar.activation(self.qT, b[3][:, 0:T], ACT.Identity, bias=self.k.bq_scaled[f"bq{L}"][:, :], scale=HD ** -0.5)
            e.then_inc(self.proj_copied, 1)
        if self.rt is not None and s == 3:
            self.rt.act_exp(act)
        if self.rt is not None and s == 5:
            self.rt.act_turn(act)
        if self.topk:
            u = self.at(s, 1, 1)
            if u >= 0:
                self.exp_rest(act, u)
        u = self.at(s, *self.EXP)
        if u >= 0:
            self.exp_scores(act, u)
        u = self.at(s, *self.COPY)
        if u >= 0:
            self.copy_pT(act, u)
        u = self.at(s, *self.PV)
        if u >= 0 and u % HG == HG - 1:
            g = u // HG
            act.wait_ge(self.pv_done, u + 1)
            nc.scalar.activation(self.oT[:, g, :], b[3][:, (g % 2) * T:(g % 2 + 1) * T], ACT.Copy).then_inc(self.oT_copied, 1)
        if self.close(s) == 3:
            act.wait_ge(self.o_turned, 1)
            nc.scalar.activation(self.otT[:, :], b[2][:, 0:T], ACT.Copy).then_inc(self.otT_ready, 1)

    def pool_q1(self, pool, u):
        if u >= self.RING:
            pool.wait_ge(self.scores, u - self.RING + 1)
        self.k.nc.gpsimd.tensor_scalar(self.q1[:, u % self.RING, :], self.qT, self.k.w["head_rows"][:, u:u + 1], 1.0,
                                       ALU.mult, ALU.mult).then_inc(self.q1_ready, 1)

    def pool(self, pool, s):
        if s == 0:
            self.ln.pool(pool)
        if s == 2:
            pool.wait_ge(self.proj_copied, self.order.index("q") + 1)
            for u in range(3):
                self.pool_q1(pool, u)
        if self.topk:
            u = self.at(s, 0, 0)
            if u >= 0:
                self.negative_max(pool, u)
            u = self.at(s, 1, 2)
            if u >= 0:
                self.keep_top(pool, u)
        u = self.at(s, 0, 0) + 3
        if 3 <= u < H:
            self.pool_q1(pool, u)

    def dve(self, dve, s):
        nc = self.k.nc
        if s == 0:
            self.ln.dve_stats(dve)
        if s == 1:
            self.ln.dve_scale(dve)
        if self.rt is not None and s == 3:
            self.rt.dve_max(dve)
        if self.rt is not None and s == 4:
            self.rt.dve_choose(dve)
        for r in range(self.rounds):
            u = self.at(s, 0, r)
            if u >= 0 and self.topk:
                self.select(dve, u, r)
            u = self.at(s, 1, r)
            if u >= 0 and not self.topk:
                dve.wait_ge(self.scores, u + 1)
                nc.vector.tensor_reduce(self.nmax[:, u, :], self.banks[u % 2][:, :].rearrange("p (j t) -> p j t", j=NT),
                                        AX.X, ALU.max, negate=True).then_inc(self.max_ready, 1)
        c = self.close(s)
        if c == 2:
            self.dve_normalise(dve)
        if c == 5:
            dve.wait_ge(self.out_ps, 1)
            self.chain.link(dve, nc.vector.scalar_tensor_tensor(
                out=self.x[:, :, :], in0=self.banks[3][:, 0:NT * D].rearrange("p (j d) -> p j d", j=NT),
                scalar=self.k.tg[:, self.gate:self.gate + 1], in1=self.x[:, :, :], op0=ALU.mult, op1=ALU.add))


class WideAttention(TopSelect):
    topk = 64

    def __init__(self, k, side, x, ctxT, banks, gate):
        self.name = "wide"
        self.k, self.x, self.ctxT, self.banks, self.gate = k, x, ctxT, banks, gate
        self.ln = LayerNorm(k, side, "a", x, banks[0])
        buf = Workspace(k, side)
        self.qT, self.kT, self.p, self.pT = buf.qT, buf.kT, buf.p, buf.pT
        self.v = k.sb("wide_v", [P, NT, H1, HD1 + 1])
        self.nmax = k.sb(f"att_nmax{side}", [P, H, NT])
        self.rden, self.o = k.sb("wide_rden", [P, H1, NT]), buf.oT.rearrange("p (j c) t -> p j (c t)", j=NT)
        self.otT = buf.kT.rearrange("p (j a) (b t) -> p j (a b) t", j=NT, t=P)
        n = f"att{side}_"
        self.chain = Chain(k.sem(n + "dve"))
        self.proj, self.proj_copied = k.sem(n + "proj"), k.sem(n + "proj_copied")
        self.scores, self.max_ready, self.exp_done = k.sem(n + "scores"), k.sem(n + "max"), k.sem(n + "exp")
        self.p_ready, self.pT_ps, self.pT_copied = k.sem(n + "p"), k.sem(n + "pT_ps"), k.sem(n + "pT")
        self.pv_done, self.rden_ready, self.o_ready = k.sem(n + "pv"), k.sem(n + "rden"), k.sem(n + "o")
        self.back, self.otT_ready, self.out_ps = k.sem(n + "back"), k.sem(n + "otT"), k.sem(n + "out")
        self.top_buffers(k, buf, n)
        self.units(3, H1, self.topk // 8, 9, 4)

    def score(self, pe, u):
        c, a = divmod(u, 2)
        r = slice(HD1 * a, HD1 * (a + 1))
        if u == 0:
            pe.wait_ge(self.proj_copied, 6)
        if u >= 2:
            pe.wait_ge(self.exp_done, u - 1)
        for j in range(NT):
            mm = self.k.nc.tensor.matmul(self.banks[u % 2][:, j * T:(j + 1) * T], self.qT[r, c, j * P:(j + 1) * P],
                                         self.kT[r, c, :], start=True, stop=True)
        mm.then_inc(self.scores, 1)

    def pe(self, pe, s):
        nc, w, b = self.k.nc, self.k.w, self.banks
        if s == 0:
            for c in range(4):
                nc.tensor.matmul(b[2 + c // 2][:, (c % 2) * T:(c % 2 + 1) * T], w["wk1"][:, c * P:(c + 1) * P], self.ctxT[:, :],
                                 start=True, stop=True).then_inc(self.proj, 1)
        if s == 1:
            self.ln.pe(pe)
            for j in range(NT):
                pe.wait_ge(self.proj_copied, j + 1)
                nc.tensor.matmul(b[2 + j][:, :], self.ctxT[:, j * P:(j + 1) * P], w["wv1"], start=True,
                                 stop=True).then_inc(self.proj, 1)
        if s == 2:
            pe.wait_ge(self.ln.yT_ready, 1)
            for c in range(4):
                nc.tensor.matmul(b[c // 2][:, (c % 2) * T:(c % 2 + 1) * T], w["wq1"][:, c * P:(c + 1) * P], self.ln.yT[:, :],
                                 start=True, stop=True).then_inc(self.proj, 1)
            self.score(pe, 0)
            self.score(pe, 1)
        u = self.at(s, 0, 3) + 2
        if 2 <= u < H1:
            self.score(pe, u)
        u = self.at(s, 1, 4)
        if u >= 0:
            self.turn_p(pe, u)
        u = self.at(s, 1, 6)
        if u >= 0:
            pe.wait_ge(self.pT_copied, u + 1)
            if u >= 1:
                pe.wait_ge(self.o_ready, u)
            for j in range(NT):
                for kt in range(NT):
                    mm = nc.tensor.matmul(b[3][:, j * (HD1 + 1):(j + 1) * (HD1 + 1)], self.pT[:, u % 2, kt, j * P:(j + 1) * P],
                                          self.v[:, kt, u, :], start=(kt == 0), stop=(kt == NT - 1))
            mm.then_inc(self.pv_done, 1)
        c = self.close(s)
        if c == 0:
            pe.wait_ge(self.o_ready, H1)
            for j in range(NT):
                for i in range(4):
                    tr = self.k.turn(b[j][:, i * P:(i + 1) * P], self.o[:, j, i * P:(i + 1) * P])
                tr.then_inc(self.back, 1)
        if c == 1:
            for j in range(NT):
                pe.wait_ge(self.otT_ready, j + 1)
                out = b[2][:, j * D:(j + 1) * D]
                nc.tensor.matmul(out, self.k.one("bout1"), w["bout1"], start=True, stop=False)
                for i in range(4):
                    mm = nc.tensor.matmul(out, self.otT[:, j, i, :], w["wo1"][:, i * D:(i + 1) * D], start=False, stop=(i == 3))
            mm.then_inc(self.out_ps, 1)

    def act(self, act, s):
        nc, b = self.k.nc, self.banks
        if s == 0:
            for half in range(2):
                act.wait_ge(self.proj, 2 * half + 2)
                nc.scalar.activation(self.kT[:, 2 * half:2 * half + 2, :], b[2 + half][:, :], ACT.Copy).then_inc(self.proj_copied, 1)
        if s == 1:
            self.ln.act(act)
            for j in range(NT):
                act.wait_ge(self.proj, 4 + j + 1)
                nc.scalar.activation(self.v[:, j, :, 0:HD1], b[2 + j][:, :].rearrange("p (h d) -> p h d", d=HD1),
                                     ACT.Copy).then_inc(self.proj_copied, 1)
        if s == 2:
            for half in range(2):
                act.wait_ge(self.proj, 6 + 2 * half + 2)
                nc.scalar.activation(self.qT[:, 2 * half:2 * half + 2, :], b[half][:, :], ACT.Copy,
                                     scale=HD1 ** -0.5).then_inc(self.proj_copied, 1)
        u = self.at(s, 1, 1)
        if u >= 0:
            self.exp_rest(act, u)
        u = self.at(s, 0, 1)
        if u >= 0:
            self.exp_scores(act, u)
        u = self.at(s, 1, 4)
        if u >= 0:
            self.copy_pT(act, u)
        u = self.at(s, 2, 0)
        if u >= 0:
            act.wait_ge(self.rden_ready, u + 1)
            for j in range(NT):
                e = nc.scalar.activation(self.o[:, j, u * HD1:(u + 1) * HD1], b[3][:, j * (HD1 + 1):j * (HD1 + 1) + HD1],
                                         ACT.Copy, scale=self.rden[:, u, j:j + 1])
            e.then_inc(self.o_ready, 1)
        if self.close(s) == 0:
            for j in range(NT):
                act.wait_ge(self.back, j + 1)
                nc.scalar.activation(self.otT[:, j, :, :], b[j][:, :], ACT.Copy).then_inc(self.otT_ready, 1)

    def pool(self, pool, s):
        if s == 0:
            self.ln.pool(pool)
        u = self.at(s, 0, 0)
        if u >= 0:
            self.negative_max(pool, u)
        u = self.at(s, 1, 2)
        if u >= 0:
            self.keep_top(pool, u)

    def dve(self, dve, s):
        nc = self.k.nc
        if s == 0:
            self.ln.dve_stats(dve)
        if s == 1:
            self.ln.dve_scale(dve)
        for r in range(self.rounds):
            u = self.at(s, 0, r)
            if u >= 0:
                self.select(dve, u, r)
        u = self.at(s, 2, 0)
        if u >= 0:
            dve.wait_ge(self.pv_done, u + 1)
            nc.vector.reciprocal(self.rden[:, u, :], self.banks[3][:, 0:NT * (HD1 + 1)].rearrange("p (j c) -> p j c", j=NT)[:, :, HD1]).then_inc(self.rden_ready, 1)
        if self.close(s) == 3:
            dve.wait_ge(self.out_ps, 1)
            self.chain.link(dve, nc.vector.scalar_tensor_tensor(
                out=self.x[:, :, :], in0=self.banks[2][:, 0:NT * D].rearrange("p (j d) -> p j d", j=NT),
                scalar=self.k.tg[:, self.gate:self.gate + 1], in1=self.x[:, :, :], op0=ALU.mult, op1=ALU.add))


class Router:

    def __init__(self, k, side, tag, kind, lhsT, weight, bias, bank, t_bank):
        self.k, self.kind, self.lhsT, self.weight, self.bias, self.bank, self.t_bank = k, kind, lhsT, weight, bias, bank, t_bank
        self.nmax, self.sum = k.sb(f"rt_nmax{side}", [P, NT]), k.sb(f"rt_sum{side}", [P, NT])
        self.e = k.sb(f"rt_e{side}", [P, NT, E8])
        self.pr, self.wk = k.sb(f"rt_pr{side}", [P, NT, E8 + 6]), k.sb(f"rt_wk{side}", [P, NT, E8 + 6])
        self.m8 = k.sb(f"rt_m8{side}", [P, NT, 8])
        self.comb, self.combT = k.sb(f"rt_comb{side}", [P, NT, E8 + 1]), k.sb(f"rt_combT{side}", [E8 + 1, T])
        n = f"rt{side}{tag}_"
        self.chain = Chain(k.sem(n + "dve"))
        self.logits, self.nmax_ready, self.e_ready = k.sem(n + "logits"), k.sem(n + "nmax"), k.sem(n + "e")
        self.pr_ready = k.sem(n + "pr")
        self.comb_ready, self.turned, self.combT_ready = k.sem(n + "comb"), k.sem(n + "turned"), k.sem(n + "combT")

    def pe_logits(self, pe):
        nc, w = self.k.nc, self.k.w
        for j in range(NT):
            out = self.bank[:, j * E8:(j + 1) * E8]
            mm = nc.tensor.matmul(out, self.lhsT[:, j * P:(j + 1) * P], w[self.weight], start=True, stop=self.bias is None)
            if self.bias is not None:
                mm = nc.tensor.matmul(out, w["ones"][0:1, :], w[self.bias], start=False, stop=True)
        mm.then_inc(self.logits, 1)

    def pe_turn(self, pe):
        pe.wait_ge(self.comb_ready, 1)
        for j in range(NT):
            tr = self.k.turn(self.t_bank[0:E8 + 1, j * P:(j + 1) * P], self.comb[:, j, :])
        tr.then_inc(self.turned, 1)

    def act_exp(self, act):
        act.wait_ge(self.nmax_ready, 1)
        for j in range(NT):
            e = self.k.nc.scalar.activation(self.e[:, j, :], self.bank[:, j * E8:(j + 1) * E8], ACT.Exp, bias=self.nmax[:, j:j + 1])
        e.then_inc(self.e_ready, 1)

    def act_turn(self, act):
        act.wait_ge(self.turned, 1)
        self.k.nc.scalar.activation(self.combT[:, :], self.t_bank[0:E8 + 1, 0:T], ACT.Copy).then_inc(self.combT_ready, 1)

    def dve_max(self, dve):
        v = self.k.nc.vector
        lg = self.bank[:, 0:NT * E8].rearrange("p (j e) -> p j e", j=NT)
        dve.wait_ge(self.logits, 1)
        if self.kind == "top":
            v.tensor_copy(self.pr[:, :, 0:E8], lg).then_inc(self.pr_ready, 1)
        v.tensor_reduce(self.nmax[:, :], lg, AX.X, ALU.max, negate=True).then_inc(self.nmax_ready, 1)

    def dve_choose(self, dve):
        nc = self.k.nc
        v = nc.vector
        link = lambda ins: self.chain.link(dve, ins)
        pr = self.pr[:, :, 0:E8]
        wide = lambda t: t.unsqueeze(2).broadcast_to([P, NT, E8])
        if self.kind == "top":
            dve.wait_ge(self.pr_ready, 1)
        dve.wait_ge(self.e_ready, 1)
        if self.kind != "top":
            link(v.tensor_reduce(self.sum[:, :], self.e[:, :, :], AX.X, ALU.add))
            link(v.reciprocal(self.sum[:, :], self.sum[:, :]))
            link(v.tensor_tensor(pr, self.e[:, :, :], wide(self.sum[:, :]), ALU.mult))
        for j in range(NT):
            link(v.max(self.m8[:, j, :], self.pr[:, j, 0:E8]))
        link(v.memset(self.m8[:, :, 2:8], SENT))
        for j in range(NT):
            link(v.match_replace(self.wk[:, j, :], self.m8[:, j, :], self.pr[:, j, :], GONE))
        link(v.tensor_scalar(self.wk[:, :, 0:E8], self.wk[:, :, 0:E8], 0.5 * (SENT + GONE), None, ALU.is_le))
        comb, chosen = self.comb[:, :, 0:E8], self.wk[:, :, 0:E8]
        if self.kind == "prob":
            v.tensor_tensor(comb, chosen, pr, ALU.mult).then_inc(self.comb_ready, 1)
        else:
            src = self.e[:, :, :] if self.kind == "top" else pr
            link(v.tensor_tensor(comb, chosen, src, ALU.mult))
            link(v.tensor_reduce(self.sum[:, :], comb, AX.X, ALU.add))
            if self.kind == "renorm":
                link(v.tensor_scalar(self.sum[:, :], self.sum[:, :], 1e-9, None, ALU.add))
            link(v.reciprocal(self.sum[:, :], self.sum[:, :]))
            v.tensor_tensor(comb, comb, wide(self.sum[:, :]), ALU.mult).then_inc(self.comb_ready, 1)
        dve.wait_ge(self.comb_ready, 1)


class LinearExperts(Units):
    PART = 4

    def __init__(self, k, side, x, out, att, banks, gate, before):
        self.name = "linear"
        self.k, self.x, self.out, self.att, self.banks, self.gate, self.before = k, x, out, att, banks, gate, before
        self.yT, self.rt = att.ln.yT, att.rt
        self.acc = k.sb(f"moe_acc{side}", [P, NT, D])
        n = f"moe{side}_"
        self.chain = Chain(k.sem(n + "dve"))
        self.y_ps, self.bias_ps, self.acc_ready = k.sem(n + "y_ps"), k.sem(n + "bias_ps"), k.sem(n + "acc")
        self.parts = E8 // self.PART
        self.units(2, NT * self.parts, 1, 0, 1)

    def products(self, pe, u):
        j, part = divmod(u, self.parts)
        self.k.nc.tensor.matmul(self.banks[2 + part][:, :], self.yT[:, j * P:(j + 1) * P],
                                self.k.w["exp0"][:, part * 512:(part + 1) * 512], start=True, stop=True).then_inc(self.y_ps, 1)

    def pe(self, pe, s):
        nc, w, b = self.k.nc, self.k.w, self.banks
        if s == 0:
            self.att.pe_back(pe)
            for u in range(self.parts):
                self.products(pe, u)
        if s == 2:
            pe.wait_ge(self.att.o_ready, NT)
            for j in range(NT):
                mm = nc.tensor.matmul(b[0][:, j * D:(j + 1) * D], self.rt.combT[:, j * P:(j + 1) * P], w["bias0"][0:E8 + 1, :],
                                      start=True, stop=True)
            mm.then_inc(self.bias_ps, 1)
        u = self.at(s, 1, 0) + self.parts
        if self.parts <= u < self.count:
            pe.wait_ge(self.acc_ready, self.PART * (u - self.parts + 1))
            self.products(pe, u)

    def act(self, act, s):
        pass

    def pool(self, pool, s):
        pass

    def dve(self, dve, s):
        nc = self.k.nc
        if s == 1:
            self.att.dve_normalise(dve)
        u = self.at(s, 0, 0)
        if u >= 0:
            j, part = divmod(u, self.parts)
            if u == 0:
                dve.wait_ge(self.att.o_ready, NT)
            dve.wait_ge(self.y_ps, u + 1)
            for i in range(self.PART):
                e = self.PART * part + i
                if u > 0 or i > 0:
                    dve.wait_ge(self.acc_ready, self.PART * u + i)
                first = self.att.o if e == 0 else self.acc
                nc.vector.scalar_tensor_tensor(out=self.acc[:, j, :], in0=self.banks[2 + part][:, i * D:(i + 1) * D],
                                               scalar=self.rt.comb[:, j, e:e + 1], in1=first[:, j, :], op0=ALU.mult,
                                               op1=ALU.add).then_inc(self.acc_ready, 1)
        if self.close(s) == 0:
            dve.wait_ge(self.acc_ready, E8 * NT)
            dve.wait_ge(self.bias_ps, 1)
            self.chain.link(dve, nc.vector.tensor_tensor(
                self.acc[:, :, :], self.acc[:, :, :], self.banks[0][:, 0:NT * D].rearrange("p (j d) -> p j d", j=NT), ALU.add))
            if self.before is not None:
                dve.wait_ge(self.before.stored, 16)
            self.chain.link(dve, nc.vector.scalar_tensor_tensor(out=self.out[:, :, :], in0=self.acc[:, :, :],
                                                                scalar=self.k.tg[:, self.gate:self.gate + 1], in1=self.x[:, :, :],
                                                                op0=ALU.mult, op1=ALU.add))


class WeightedSum:

    def __init__(self, k, side, tag, comb):
        self.k, self.comb = k, comb
        self.acc, self.part = k.sb(f"moe_acc{side}", [P, NT, D]), k.sb(f"moe_part{side}", [P, 2, NT, D])
        n = f"sum{side}{tag}_"
        self.taken, self.added = k.sem(n + "taken"), k.sem(n + "added")

    def act_first(self, y):
        self.k.nc.scalar.activation(self.acc[:, :, :], y, ACT.Copy).then_inc(self.taken, 1)

    def act_expert(self, act, e, y):
        if e >= 2:
            act.wait_ge(self.added, e - 1)
        for j in range(NT):
            ins = self.k.nc.scalar.activation(self.part[:, e % 2, j, :], y[:, j * D:(j + 1) * D], ACT.Copy,
                                              scale=self.comb[:, j, e:e + 1])
        ins.then_inc(self.taken, 1)

    def pool_expert(self, pool, e):
        pool.wait_ge(self.taken, e + 2)
        if e >= 1:
            pool.wait_ge(self.added, e)
        self.k.nc.gpsimd.tensor_tensor(self.acc[:, :, :], self.acc[:, :, :], self.part[:, e % 2, :, :],
                                       ALU.add).then_inc(self.added, 1)


class GatedExperts(Units):

    def __init__(self, k, side, x, banks, gate):
        self.name = "gated"
        self.k, self.x, self.banks, self.gate = k, x, banks, gate
        self.ln = LayerNorm(k, side, "a", x, banks[0])
        self.rt = Router(k, side, "a", "top", self.ln.yT, "router1", None, banks[2], banks[3])
        buf = Workspace(k, side)
        self.th, self.hT = buf.p[:, 0, :, :], buf.p[:, 1, :, :]
        self.sum = WeightedSum(k, side, "a", self.rt.comb)
        n = f"moe{side}_"
        self.chain = Chain(k.sem(n + "dve"))
        self.h_ps, self.th_ready, self.u_ready = k.sem(n + "h_ps"), k.sem(n + "th"), k.sem(n + "u")
        self.hT_ready, self.y_ps = k.sem(n + "hT"), k.sem(n + "y_ps")
        self.N = 2 + E8
        self.units(3, self.N, 1, 3, 1)

    def wait_banks(self, pe):
        pe.wait_ge(self.hT_ready, self.N)
        pe.wait_ge(self.sum.taken, E8 + 1)

    def pe(self, pe, s):
        nc, w, b = self.k.nc, self.k.w, self.banks
        if s == 1:
            self.ln.pe(pe)
        if s == 2:
            pe.wait_ge(self.ln.yT_ready, 1)
            self.rt.pe_logits(pe)
        u = self.at(s, 0, 0)
        if u >= 0:
            if u >= 2:
                pe.wait_ge(self.hT_ready, u - 1)
            if u < 2:
                pw, gw = w["gate_w"][:, u * D:(u + 1) * D], w["up_w"][:, u * D:(u + 1) * D]
            else:
                pw, gw = (w["fc1"][:, (2 * (u - 2) + i) * D:(2 * (u - 2) + i + 1) * D] for i in range(2))
            nc.tensor.matmul(b[u % 2][:, 0:T], pw, self.ln.yT[:, :], start=True, stop=True)
            nc.tensor.matmul(b[u % 2][:, T:2 * T], gw, self.ln.yT[:, :], start=True, stop=True).then_inc(self.h_ps, 1)
        if s == 5:
            self.rt.pe_turn(pe)
        u = self.at(s, 2, 0)
        if u == 1:
            pe.wait_ge(self.rt.combT_ready, 1)
            pe.wait_ge(self.hT_ready, 2)
            for j in range(NT):
                for c in range(2):
                    mm = nc.tensor.matmul(b[2][:, j * D:(j + 1) * D], self.hT[:, c, j * P:(j + 1) * P],
                                          w["down_w"][:, c * D:(c + 1) * D], start=(c == 0), stop=(c == 1))
            mm.then_inc(self.y_ps, 1)
        if u >= 2:
            pe.wait_ge(self.hT_ready, u + 1)
            if u >= 3:
                pe.wait_ge(self.sum.taken, u - 2)
            for j in range(NT):
                mm = nc.tensor.matmul(b[3 - u % 2][:, j * D:(j + 1) * D], self.hT[:, u % 2, j * P:(j + 1) * P],
                                      w["fc2"][:, (u - 2) * D:(u - 1) * D], start=True, stop=True)
            mm.then_inc(self.y_ps, 1)

    def act(self, act, s):
        nc = self.k.nc
        if s == 1:
            self.ln.act(act)
        if s == 3:
            self.rt.act_exp(act)
        if s == 5:
            self.rt.act_turn(act)
        u = self.at(s, 0, 0)
        if u >= 0:
            act.wait_ge(self.h_ps, u + 1)
            if u >= 2:
                act.wait_ge(self.hT_ready, u - 1)
            nc.scalar.activation(self.th[:, u % 2, :], self.banks[u % 2][:, 0:T], ACT.Tanh, scale=0.5).then_inc(self.th_ready, 1)

        u = self.at(s, 2, 0)
        if u == 1:
            act.wait_ge(self.y_ps, 1)
            self.sum.act_first(self.banks[2][:, 0:NT * D])
        if u >= 2:
            act.wait_ge(self.y_ps, u)
            self.sum.act_expert(act, u - 2, self.banks[3 - u % 2])

    def pool(self, pool, s):
        if s == 0:
            self.ln.pool(pool)
        u = self.at(s, 3, 0)
        if u >= 2:
            self.sum.pool_expert(pool, u - 2)

    def dve(self, dve, s):
        nc, b = self.k.nc, self.banks
        if s == 0:
            self.ln.dve_stats(dve)
        if s == 1:
            self.ln.dve_scale(dve)
        if s == 3:
            self.rt.dve_max(dve)
        if s == 4:
            self.rt.dve_choose(dve)
        u = self.at(s, 1, 0)
        if u >= 0:
            dve.wait_ge(self.th_ready, u + 1)
            th = self.th[:, u % 2, :]
            nc.vector.scalar_tensor_tensor(out=th, in0=th, scalar=1.0, in1=b[u % 2][:, 0:T], op0=ALU.add,
                                           op1=ALU.mult).then_inc(self.u_ready, 1)
            dve.wait_ge(self.u_ready, u + 1)
            if u >= 2:
                dve.wait_ge(self.y_ps, u - 2 if u > 3 else 1)
            nc.vector.scalar_tensor_tensor(out=self.hT[:, u % 2, :], in0=th, scalar=0.5, in1=b[u % 2][:, T:2 * T],
                                           op0=ALU.mult, op1=ALU.mult).then_inc(self.hT_ready, 1)
        if self.close(s) == 0:
            dve.wait_ge(self.sum.added, E8)
            self.chain.link(dve, nc.vector.scalar_tensor_tensor(out=self.x[:, :, :], in0=self.sum.acc[:, :, :],
                                                                scalar=self.k.tg[:, self.gate:self.gate + 1], in1=self.x[:, :, :],
                                                                op0=ALU.mult, op1=ALU.add))


class GeluExperts(Units):

    def __init__(self, k, side, x, banks, gate):
        self.name = "gelu"
        self.k, self.x, self.banks, self.gate = k, x, banks, gate
        self.ln = LayerNorm(k, side, "c", x, banks[0])
        self.rt = Router(k, side, "b", "renorm", self.ln.yT, "router2", "br2", banks[2], banks[3])
        buf = Workspace(k, side)
        self.hT = [buf.kT, buf.qT]
        self.sum = WeightedSum(k, side, "b", self.rt.comb)
        n = f"gelu{side}_"
        self.chain = Chain(k.sem(n + "dve"))
        self.h_ps, self.hT_ready, self.y_ps = k.sem(n + "h_ps"), k.sem(n + "hT"), k.sem(n + "y_ps")
        self.N = 1 + E8
        self.units(3, self.N, 2, 4, 1)

    def pe(self, pe, s):
        nc, w, b = self.k.nc, self.k.w, self.banks
        if s == 1:
            self.ln.pe(pe)
        if s == 2:
            pe.wait_ge(self.ln.yT_ready, 1)
            self.rt.pe_logits(pe)
        u = self.at(s, 0, 0)
        if u >= 0:
            for c in range(FF2):
                if u >= 1 and c % 2 == 0:
                    pe.wait_ge(self.hT_ready, FF2 * (u - 1) + c + 2)
                mm = nc.tensor.matmul(b[c // 2][:, (c % 2) * T:(c % 2 + 1) * T], w["w1"][:, (u * FF2 + c) * 128:(u * FF2 + c + 1) * 128],
                                      self.ln.yT[:, :], start=True, stop=True)
                if c % 2 == 1:
                    mm.then_inc(self.h_ps, 1)
        if s == 5:
            self.rt.pe_turn(pe)
        u = self.at(s, 1, 1)
        if u >= 0:
            if u == 0:
                pe.wait_ge(self.rt.combT_ready, 1)
            if u >= 2:
                pe.wait_ge(self.sum.taken, u - 1)
            pe.wait_ge(self.hT_ready, FF2 * (u + 1))
            for j in range(NT):
                out = b[2 + u % 2][:, j * D:(j + 1) * D]
                if u == 0:
                    nc.tensor.matmul(out, self.rt.combT[:, j * P:(j + 1) * P], w["bias2"][0:E8 + 1, :], start=True, stop=False)
                for c in range(FF2):
                    mm = nc.tensor.matmul(out, self.hT[u % 2][:, c, j * P:(j + 1) * P],
                                          w["w2"][:, (u * FF2 + c) * 128:(u * FF2 + c + 1) * 128],
                                          start=(u > 0 and c == 0), stop=(c == FF2 - 1))
            mm.then_inc(self.y_ps, 1)

    def act(self, act, s):
        nc = self.k.nc
        if s == 1:
            self.ln.act(act)
        if s == 3:
            self.rt.act_exp(act)
        if s == 5:
            self.rt.act_turn(act)
        u = self.at(s, 0, 0)
        if u >= 0:
            for c in range(FF2):
                act.wait_ge(self.h_ps, 2 * u + c // 2 + 1)
                if u >= 2 and c == 0:
                    act.wait_ge(self.y_ps, u - 1)
                nc.scalar.activation(self.hT[u % 2][:, c, :], self.banks[c // 2][:, (c % 2) * T:(c % 2 + 1) * T], ACT.Gelu,
                                     bias=self.k.w["b1"][:, u * FF2 + c:u * FF2 + c + 1]).then_inc(self.hT_ready, 1)

        u = self.at(s, 2, 0)
        if u == 0:
            act.wait_ge(self.y_ps, 1)
            self.sum.act_first(self.banks[2][:, 0:NT * D])
        if u >= 1:
            act.wait_ge(self.y_ps, u + 1)
            self.sum.act_expert(act, u - 1, self.banks[2 + u % 2])

    def pool(self, pool, s):
        if s == 0:
            self.ln.pool(pool)
        u = self.at(s, 2, 1)
        if u >= 1:
            self.sum.pool_expert(pool, u - 1)

    def dve(self, dve, s):
        nc, b = self.k.nc, self.banks
        if s == 0:
            self.ln.dve_stats(dve)
        if s == 1:
            self.ln.dve_scale(dve)
        if s == 3:
            self.rt.dve_max(dve)
        if s == 4:
            self.rt.dve_choose(dve)
        if self.close(s) == 0:
            dve.wait_ge(self.sum.added, E8)
            self.chain.link(dve, nc.vector.scalar_tensor_tensor(out=self.x[:, :, :], in0=self.sum.acc[:, :, :],
                                                                scalar=self.k.tg[:, self.gate:self.gate + 1], in1=self.x[:, :, :],
                                                                op0=ALU.mult, op1=ALU.add))


class MixedAttention(Units):
    SUM = 6

    def __init__(self, k, side, x, batch, banks, gate):
        self.name = "mixed"
        self.k, self.x, self.batch, self.banks, self.gate = k, x, batch, banks, gate
        self.ln = LayerNorm(k, side, "m", x, banks[0])
        self.ssq, self.rn = k.sb("mix_ssq", [P, NT]), k.sb("mix_rn", [P, NT])
        self.lg, self.wk = k.sb("mix_lg", [P, NT, E16 + 6]), k.sb("mix_wk", [P, NT, E16 + 6])
        self.m8, self.none, self.ngm = k.sb("mix_m8", [P, NT, 8]), k.sb("mix_none", [P, NT]), k.sb("mix_ngm", [P, NT])
        self.gt, self.act_mask, self.wt = k.sb("mix_gt", [P, NT, E16]), k.sb("mix_mask", [P, NT, E16]), k.sb("mix_wt", [P, NT, E16])
        self.sum = k.sb("mix_sum", [P, NT])
        buf = Workspace(k, side)
        self.sq = buf.p[:, 0, 0, :].rearrange("p (j d) -> p j d", j=NT)
        self.parts, self.left = k.sb("mix_parts", [P, NT, PARTS * E16], BF16), k.sb("mix_left", [P, NT, E16])
        self.wT, self.wb, self.zT = k.sb("mix_wT", [PARTS * E16, T], BF16), k.sb("mix_wb", [P, E16, T]), buf.whole
        self.qT, self.kT = buf.p[:, 1, 0, :], buf.p[:, 1, 1, :]
        self.v = buf.pT[:, 1, 0, :].rearrange("p (j d) -> p j d", j=NT)
        self.nmax, self.den, self.rden = k.sb("mix_nmax", [P, NT]), k.sb("mix_den", [P, NT]), k.sb("mix_rden", [P, NT])
        self.p, self.pT, self.oT = buf.p[:, 0, :, :], buf.pT[:, 0, :, :], buf.pT[:, 1, 1, :]
        n = "mix_"
        self.chain = Chain(k.sem(n + "dve"))
        self.ssq_ready, self.rn_in, self.rn_ready, self.logits = k.sem(n + "ssq"), k.sem(n + "rn_in"), k.sem(n + "rn"), k.sem(n + "logits")
        self.gt_ready, self.e_ready, self.wt_ready = k.sem(n + "gt"), k.sem(n + "e"), k.sem(n + "wt")
        self.turned, self.wT_ready, self.parts_ready = k.sem(n + "turned"), k.sem(n + "wT"), k.sem(n + "parts")
        self.wb_ps, self.wb_ready, self.z_ready = k.sem(n + "wb_ps"), k.sem(n + "wb"), k.sem(n + "z")
        self.qkv_ps, self.qkv_copied = k.sem(n + "qkv_ps"), k.sem(n + "qkv")
        self.scores, self.max_ready, self.exp_done, self.p_ready = k.sem(n + "scores"), k.sem(n + "max"), k.sem(n + "exp"), k.sem(n + "p")
        self.pT_ps, self.pT_copied, self.o_ps, self.o_copied = k.sem(n + "pT_ps"), k.sem(n + "pT"), k.sem(n + "o_ps"), k.sem(n + "o")
        self.zo_ready, self.zo2_ready, self.out_ps, self.x_done = k.sem(n + "zo"), k.sem(n + "zo2"), k.sem(n + "out"), k.sem(n + "x_done")
        self.stored = k.sem("stored")
        self.PAIRS = E16 // 2
        self.units(6, self.PAIRS, 1, 2, self.SUM + self.PAIRS + 2)

    def pe(self, pe, s):
        nc, w, b = self.k.nc, self.k.w, self.banks
        if s == 1:
            self.ln.pe(pe)
        if s == 2:
            pe.wait_ge(self.ln.yT_ready, 1)
            for j in range(NT):
                mm = nc.tensor.matmul(b[1][:, j * E16:(j + 1) * E16], self.ln.yT[:, j * P:(j + 1) * P], self.k.sn[:, :],
                                      start=True, stop=True)
            mm.then_inc(self.logits, 1)
        if s == 5:
            pe.wait_ge(self.parts_ready, PARTS + 1)
            for j in range(NT):
                tr = nc.tensor.matmul(b[0][0:PARTS * E16, j * P:(j + 1) * P], self.parts[:, j, :], self.k.ident16[:, :],
                                      start=True, stop=True)
            tr.then_inc(self.turned, 1)
        i = self.at(s, 0, 0)
        if i >= 0:
            if i == 0:
                pe.wait_ge(self.wT_ready, 1)
            if i >= 2:
                pe.wait_ge(self.wb_ready, i - 1)
            for e in (2 * i, 2 * i + 1):
                mm = nc.tensor.matmul(b[i % 2][:, (e % 2) * T:(e % 2 + 1) * T],
                                      self.k.part_rows16[0:PARTS * E16, e:e + 1].broadcast_to([PARTS * E16, P]), self.wT[:, :],
                                      start=True, stop=True)
            mm.then_inc(self.wb_ps, 1)
        i = self.at(s, 2, 0)
        if i >= 0:
            pe.wait_ge(self.z_ready, i + 1)
            for e in (2 * i, 2 * i + 1):
                first, last = e == 0, e == E16 - 1
                nc.tensor.matmul(b[2][:, 0:T], w["qp"][:, e * D:(e + 1) * D], self.zT[:, e, :], start=first, stop=False)
                nc.tensor.matmul(b[2][:, T:2 * T], w["kp"][:, e * D:(e + 1) * D], self.zT[:, e, :], start=False, stop=last)
                for j in range(NT):
                    mm = nc.tensor.matmul(b[3][:, j * D:(j + 1) * D], self.zT[:, e, j * P:(j + 1) * P], w["vp"][:, e * D:(e + 1) * D],
                                          start=first and j == 0, stop=last and j == NT - 1)
            if i == self.PAIRS - 1:
                mm.then_inc(self.qkv_ps, 1)
        c = self.close(s)
        if c == 0:
            pe.wait_ge(self.wb_ready, self.PAIRS)
            pe.wait_ge(self.qkv_copied, 2)
            for j in range(NT):
                mm = nc.tensor.matmul(b[0][:, j * T:(j + 1) * T], self.qT[:, j * P:(j + 1) * P], self.kT[:, :],
                                      start=True, stop=True)
            mm.then_inc(self.scores, 1)
        if c == 4:
            pe.wait_ge(self.p_ready, NT)
            for kt in range(NT):
                for j in range(NT):
                    tr = self.k.turn(b[1][:, kt * T + j * P:kt * T + (j + 1) * P], self.p[:, j, kt * P:(kt + 1) * P])
            tr.then_inc(self.pT_ps, 1)
        if c == 5:
            pe.wait_ge(self.pT_copied, 1)
            pe.wait_ge(self.qkv_copied, 3)
            for kt in range(NT):
                mm = nc.tensor.matmul(b[2][:, 0:T], self.v[:, kt, :], self.pT[:, kt, :], start=(kt == 0), stop=(kt == NT - 1))
            mm.then_inc(self.o_ps, 1)
        i = c - self.SUM - 1
        if 0 <= i < self.PAIRS:
            pe.wait_ge(self.zo2_ready if i % 2 else self.zo_ready, i // 2 + 1)
            for e in (2 * i, 2 * i + 1):
                for j in range(NT):
                    mm = nc.tensor.matmul(b[j][:, 0:D], self.zT[:, e, j * P:(j + 1) * P], w["op"][:, e * D:(e + 1) * D],
                                          start=(e == 0), stop=(e == E16 - 1))
            if i == self.PAIRS - 1:
                mm.then_inc(self.out_ps, 1)

    def act(self, act, s):
        nc, b = self.k.nc, self.banks
        if s == 1:
            self.ln.act(act)
            for j in range(NT):
                act.wait_ge(self.ln.y_ready, j + 1)
                nc.scalar.activation(self.sq[:, j, :], self.ln.y[:, j, :], ACT.Square,
                                     accum_out=self.ssq[:, j:j + 1]).then_inc(self.ssq_ready, 1)
        if s == 3:
            act.wait_ge(self.gt_ready, 1)
            for j in range(NT):
                e = nc.scalar.activation(self.wt[:, j, :], self.gt[:, j, :], ACT.Exp, bias=self.ngm[:, j:j + 1])
            e.then_inc(self.e_ready, 1)
        if s == 5:
            act.wait_ge(self.turned, 1)
            nc.scalar.activation(self.wT[:, :], b[0][0:PARTS * E16, 0:T], ACT.Copy).then_inc(self.wT_ready, 1)
        i = self.at(s, 0, 0)
        if i >= 0:
            act.wait_ge(self.wb_ps, i + 1)
            nc.scalar.activation(self.wb[:, 2 * i:2 * i + 2, :], b[i % 2][:, :], ACT.Copy).then_inc(self.wb_ready, 1)
        c = self.close(s)
        if c == 0:
            act.wait_ge(self.qkv_ps, 1)
            nc.scalar.activation(self.qT, b[2][:, 0:T], ACT.Copy, scale=D ** -0.5).then_inc(self.qkv_copied, 1)
            nc.scalar.activation(self.kT, b[2][:, T:2 * T], ACT.Copy).then_inc(self.qkv_copied, 1)
            nc.scalar.activation(self.v[:, :, :], b[3][:, 0:NT * D], ACT.Copy).then_inc(self.qkv_copied, 1)
        if c == 2:
            act.wait_ge(self.max_ready, 1)
            for j in range(NT):
                nc.scalar.activation(self.p[:, j, :], b[0][:, j * T:(j + 1) * T], ACT.Exp, bias=self.nmax[:, j:j + 1],
                                     accum_out=self.den[:, j:j + 1]).then_inc(self.exp_done, 1)
        if c == 4:
            act.wait_ge(self.pT_ps, 1)
            nc.scalar.activation(self.pT[:, :, :], b[1][:, :], ACT.Copy).then_inc(self.pT_copied, 1)
        if c == 5:
            act.wait_ge(self.o_ps, 1)
            nc.scalar.activation(self.oT[:, :], b[2][:, 0:T], ACT.Copy).then_inc(self.o_copied, 1)

    def attended(self, eng, i):
        return eng.tensor_tensor(self.zT[:, 2 * i:2 * i + 2, :], self.wb[:, 2 * i:2 * i + 2, :],
                                 self.oT[:, :].unsqueeze(1).broadcast_to([P, 2, T]), ALU.mult)

    def pool(self, pool, s):
        nc = self.k.nc
        if s == 0:
            self.ln.pool(pool)
        if s == 2:
            pool.wait_ge(self.rn_in, 1)
            nc.gpsimd.tensor_tensor(self.rn[:, :], self.ssq[:, :], self.k.half[:, 0:NT], ALU.pow).then_inc(self.rn_ready, 1)
        if s == 5:
            pool.wait_ge(self.wt_ready, 1)
            part = lambda i: self.parts[:, :, i * E16:(i + 1) * E16]
            nc.gpsimd.tensor_copy(part(0), self.wt[:, :, :]).then_inc(self.parts_ready, 1)
            pool.wait_ge(self.parts_ready, 1)
            nc.gpsimd.tensor_tensor(self.left[:, :, :], self.wt[:, :, :], part(0), ALU.subtract).then_inc(self.parts_ready, 1)
            pool.wait_ge(self.parts_ready, 2)
            nc.gpsimd.tensor_copy(part(1), self.left[:, :, :]).then_inc(self.parts_ready, 1)
            pool.wait_ge(self.parts_ready, 3)
            nc.gpsimd.tensor_tensor(part(2), self.left[:, :, :], part(1), ALU.subtract).then_inc(self.parts_ready, 1)
        i = self.at(s, 0, 0)
        if i >= 0:
            pool.wait_ge(self.wb_ready, i + 1)
            nc.gpsimd.tensor_tensor(self.zT[:, 2 * i:2 * i + 2, :], self.wb[:, 2 * i:2 * i + 2, :],
                                    self.ln.yT[:, :].unsqueeze(1).broadcast_to([P, 2, T]), ALU.mult).then_inc(self.z_ready, 1)
        i = self.close(s) - self.SUM
        if 0 <= i < self.PAIRS and i % 2 == 1:
            pool.wait_ge(self.o_copied, 1)
            self.attended(nc.gpsimd, i).then_inc(self.zo2_ready, 1)

    def dve(self, dve, s):
        nc, b = self.k.nc, self.banks
        v = nc.vector
        link = lambda ins: self.chain.link(dve, ins)
        if s == 0:
            self.ln.dve_stats(dve)
        if s == 1:
            self.ln.dve_scale(dve)
            dve.wait_ge(self.ssq_ready, NT)
            v.tensor_scalar(self.ssq[:, :], self.ssq[:, :], 1e-24, None, ALU.max).then_inc(self.rn_in, 1)
        if s == 3:
            dve.wait_ge(self.rn_ready, 1)
            dve.wait_ge(self.logits, 1)
            for j in range(NT):
                link(v.scalar_tensor_tensor(out=self.lg[:, j, 0:E16], in0=b[1][:, j * E16:(j + 1) * E16], scalar=self.rn[:, j:j + 1],
                                            in1=self.k.sig[:, :], op0=ALU.mult, op1=ALU.subtract))
            for j in range(NT):
                link(v.max(self.m8[:, j, :], self.lg[:, j, 0:E16]))
            link(v.tensor_scalar(self.none[:, :], self.m8[:, :, 0], 0.0, None, ALU.is_le))
            link(v.tensor_scalar(self.ngm[:, :], self.m8[:, :, 0], 0.0, -1.0, ALU.max, ALU.mult))
            v.tensor_scalar(self.gt[:, :, :], self.lg[:, :, 0:E16], 0.0, None, ALU.max).then_inc(self.gt_ready, 1)
        if s == 4:
            link(v.memset(self.m8[:, :, 2:8], SENT))
            for j in range(NT):
                link(v.match_replace(self.wk[:, j, :], self.m8[:, j, :], self.lg[:, j, :], GONE))
            link(v.tensor_scalar(self.wk[:, :, 0:E16], self.wk[:, :, 0:E16], 0.5 * (SENT + GONE), None, ALU.is_le))
            for j in range(NT):
                link(v.tensor_scalar(self.act_mask[:, j, :], self.wk[:, j, 0:E16], self.none[:, j:j + 1], None, ALU.mult))
            link(v.tensor_scalar(self.wk[:, :, 0:E16], self.lg[:, :, 0:E16], 0.0, None, ALU.is_gt))
            link(v.tensor_tensor(self.act_mask[:, :, :], self.act_mask[:, :, :], self.wk[:, :, 0:E16], ALU.max))
            dve.wait_ge(self.e_ready, 1)
            link(v.tensor_tensor(self.wt[:, :, :], self.wt[:, :, :], self.act_mask[:, :, :], ALU.mult))
            link(v.tensor_reduce(self.sum[:, :], self.wt[:, :, :], AX.X, ALU.add))
            link(v.reciprocal(self.sum[:, :], self.sum[:, :]))
            v.tensor_tensor(self.wt[:, :, :], self.wt[:, :, :], self.sum[:, :].unsqueeze(2).broadcast_to([P, NT, E16]),
                            ALU.mult).then_inc(self.wt_ready, 1)
        c = self.close(s)
        if c == 2:
            dve.wait_ge(self.scores, 1)
            v.tensor_reduce(self.nmax[:, :], b[0][:, :].rearrange("p (j t) -> p j t", j=NT), AX.X, ALU.max,
                            negate=True).then_inc(self.max_ready, 1)
        if c == 3:
            dve.wait_ge(self.exp_done, NT)
            link(v.reciprocal(self.rden[:, :], self.den[:, :]))
            for j in range(NT):
                v.tensor_scalar(self.p[:, j, :], self.p[:, j, :], self.rden[:, j:j + 1], None, ALU.mult).then_inc(self.p_ready, 1)
        i = c - self.SUM
        if 0 <= i < self.PAIRS and i % 2 == 0:
            dve.wait_ge(self.o_copied, 1)
            self.attended(v, i).then_inc(self.zo_ready, 1)
        if i == self.PAIRS + 1:
            dve.wait_ge(self.out_ps, 1)
            for j in range(NT):
                v.scalar_tensor_tensor(out=self.x[:, j, :], in0=b[j][:, 0:D], scalar=self.k.tg[:, self.gate:self.gate + 1],
                                       in1=self.x[:, j, :], op0=ALU.mult, op1=ALU.add).then_inc(self.x_done, 1)

    def sync(self, sp):
        sp.wait_ge(self.x_done, NT)
        sp.dma_start(self.k.out_dram[bass.ds(self.batch * T, T), :].rearrange("(j p) d -> p j d", p=P),
                     self.x[:, :, :]).then_inc(self.stored, 16)
        sp.wait_ge(self.stored, 16)


class Chunk:
    stages = []

    def steps(self):
        return [(stage, s) for stage in self.stages for s in range(stage.steps)]

    def sync(self, sp):
        pass


class Chunk0(Chunk):

    def __init__(self, k, lane, old, batch):
        self.k, self.batch, b = k, batch, k.psum[0:4]
        self.mix = None if old is None else MixedAttention(k, "P", k.x[lane], old, b, 7)
        self.stages = [] if old is None else [self.mix]
        if batch is not None:
            self.ctxT, self.load = k.ctxT[lane], k.sem("load")
            att = HeadAttention(k, "P", 0, k.x_in, None, b, "b", router=("prob", "gate0", "bgate0"))
            self.stages += [Performer(k, "P", k.x_in, self.ctxT, k.ctx_tok, b, self.load, self.mix), att,
                            LinearExperts(k, "P", k.x_in, k.x[lane], att, b, 4, self.mix)]

    def steps(self):
        steps = super().steps()
        if len(self.stages) > 1 and self.mix is not None:
            n = self.mix.steps
            steps[n - 1], steps[n] = steps[n], steps[n - 1]
        return steps

    def sync(self, sp):
        k, i = self.k, self.batch
        if i is not None:
            sp.dma_start(k.x_in[:, :, :], k.x_dram[bass.ds(i * T, T), :].rearrange("(j p) d -> p j d", p=P)).then_inc(self.load, 16)
            sp.dma_start(k.ctx_tok[:, :, :], k.ctx_dram[bass.ds(i * T, T), :].rearrange("(j p) d -> p j d", p=P)).then_inc(self.load, 16)
            sp.dma_start(self.ctxT[:, :], k.ctxT_dram[:, bass.ds(i * T, T)]).then_inc(self.load, 16)
        if self.mix is not None:
            self.mix.sync(sp)


class LaterWeights(Chunk):

    def __init__(self, k, dram, weights_in):
        self.k, self.dram, self.weights_in = k, dram, weights_in

    def sync(self, sp):
        for name, _ in LATER:
            sp.dma_start(self.k.bufs[name][:, :], self.dram[name]).then_inc(self.weights_in[name], 16)
        for name, _ in LATER:
            sp.wait_ge(self.weights_in[name], 16)


class Chunk1(Chunk):

    def __init__(self, k, lane):
        self.stages = [WideAttention(k, "Q", k.x[lane], k.ctxT[lane], k.psum[4:8], 1)]


class Chunk2(Chunk):

    def __init__(self, k, lane):
        x, b = k.x[lane], k.psum[0:4]
        gated = GatedExperts(k, "P", x, b, 5)
        self.stages = [gated, HeadAttention(k, "P", 2, x, k.ctxT[lane], b, "b", gate=2, before=gated), GeluExperts(k, "P", x, b, 6)]


class Chunk3(Chunk):

    def __init__(self, k, lane):
        self.stages = [HeadAttention(k, "Q", 3, k.x[lane], k.ctxT[lane], k.psum[4:8], "a", topk=32, gate=3)]


def interleaved(chunks, pace):
    order = []
    for n, c in enumerate(chunks):
        steps = [(stage, s, pace[stage.name][stage.phase(s)]) for stage, s in c.steps()]
        total, at = sum(share for _, _, share in steps), 0.0
        for i, (stage, s, share) in enumerate(steps):
            order.append((at / total, n, i, stage, s))
            at += share
    return [o[3:] for o in sorted(order, key=lambda o: o[:3])]


def run_block(k, chunks, pace):
    nc = k.nc
    steps = interleaved(chunks, pace)
    with nc.Block() as block:
        @block.sync
        def _(sp):
            for c in chunks:
                c.sync(sp)

        @block.tensor
        def _(pe):
            for stage, s in steps:
                stage.pe(pe, s)

        @block.scalar
        def _(act):
            for stage, s in steps:
                stage.act(act, s)

        @block.vector
        def _(dve):
            for stage, s in steps:
                stage.dve(dve, s)

        @block.gpsimd
        def _(pool):
            for stage, s in steps:
                stage.pool(pool, s)
    nc.all_engine_barrier(sems_to_clear=range(k.first, k.last + 1))


def flamingo(nc, dram):
    with ExitStack() as ctx:
        k = Shared(nc, ctx)
        weights_in = {name: k.lasting_sem(f"{name}_in") for name, _ in PACKS}
        rows_in, all_ctx_in = k.lasting_sem("rows_in"), k.lasting_sem("all_ctx_in")
        for name, pack in PACKS:
            tile = k.sb(name, [P, cols(pack)])
            at = 0
            for what, n in pack:
                k.w[what] = tile[:, at:at + n]
                at += n
        row = k.sb("rows", [1, cols(ROWS)])
        at = 0
        for what, n in ROWS:
            k.w[what] = row[:, at:at + n]
            at += n
        for what, names in BELOW.items():
            for i, name in enumerate(names):
                k.w[name] = k.w[what][32 * (i + 1):32 * (i + 1) + 1, :]
        k.x_dram, k.ctx_dram, k.ctxT_dram, k.out_dram = dram["x"], dram["ctx"], dram["ctxT"], dram["out"]
        k.x = [k.sb(f"x{i}", [P, NT, D]) for i in range(2)]
        k.ctxT = [k.sb(f"ctxT{i}", [P, T]) for i in range(2)]
        k.ident16, k.part_rows16 = k.sb("ident16", [P, P], BF16), k.sb("part_rows16", [P, E16], BF16)
        k.x_in = k.sb("x_in", [P, NT, D])
        k.ctx_tok = k.sb("ctx_tok", [P, NT, D])
        k.half, k.tg, k.kbias = k.sb("minus_half", [P, E16]), k.sb("tanh_g", [P, 8]), k.sb("k_stab", [P, 1])
        k.sn, k.sig = k.sb("sim_unit", [P, E16]), k.sb("sigmoid_gates", [P, E16])
        k.bq_scaled = {f"bq{L}": k.sb(f"bq{L}_scaled", [P, 1]) for L in (0, 2, 3)}

        all_ctx, sq = k.sb("mix_wb", [P, E16, T]), Workspace(k, "Q").whole
        ctx16, sq16 = all_ctx[:, 0:8, :].rearrange("p a b -> p (a b)"), sq[:, 0:8, :].rearrange("p a b -> p (a b)")
        head_sq, least = Workspace(k, "P").p[:, 0, 0, :], k.sb("setup_least", [P, 1])
        least1, simsq, simn = k.sb("setup_least1", [1, 1]), k.sb("setup_simsq", [P, E16]), k.sb("setup_simn", [P, E16])
        th = k.sb("setup_tanh", [P, E16])
        setup = ctx.enter_context(ExitStack())
        setup_sems = {n: setup.enter_context(nc.semaphore(f"setup_{n}")) for n in (
            "preset", "dve", "least", "least_row", "least1", "least_bc", "g_ps", "gates_ps", "gates_th", "simsq", "sim_ps",
            "simn_in", "simn")}
        preset, chain = setup_sems["preset"], Chain(setup_sems["dve"])
        least_ready, least_row, least1_ready, least_bc = (setup_sems[n] for n in ("least", "least_row", "least1", "least_bc"))
        g_ps, gates_ps, gates_th, simsq_ready, sim_ps, simn_in, simn_ready = (
            setup_sems[n] for n in ("g_ps", "gates_ps", "gates_th", "simsq", "sim_ps", "simn_in", "simn"))
        lg, prP = k.sb("mix_lg", [P, NT, E16 + 6]), k.sb("rt_prP", [P, NT, E8 + 6])
        combP = k.sb("rt_combP", [P, NT, E8 + 1])
        heads_v = [k.sb(n, [P, NT, H, PAD]) for n in ("att_vP", "att_vQ")]
        wide_v = k.sb("wide_v", [P, NT, H1, HD1 + 1])
        with nc.Block() as block:
            @block.sync
            def _(sp):
                sp.dma_start(ctx16, dram["ctx"].rearrange("(p n) d -> p (n d)", p=P)).then_inc(all_ctx_in, 16)
                sp.dma_start(row[:, :], dram["rows"]).then_inc(rows_in, 16)
                for name, pack in FIRST:
                    sp.dma_start(k.bufs[name][:, :], dram[name]).then_inc(weights_in[name], 16)
                for name, pack in FIRST:
                    sp.wait_ge(weights_in[name], 16)

            @block.gpsimd
            def _(pool):
                nc.gpsimd.memset(k.half[:, :], -0.5).then_inc(preset, 1)
                nc.gpsimd.memset(lg[:, :, E16:], SENT).then_inc(preset, 1)
                nc.gpsimd.memset(prP[:, :, E8:], SENT).then_inc(preset, 1)
                nc.gpsimd.memset(combP[:, :, E8:], 1.0).then_inc(preset, 1)
                for n, v in enumerate(heads_v):
                    nc.gpsimd.memset(v[:, :, :, HD:HD + 1], 1.0).then_inc(preset, 1)
                    nc.gpsimd.memset(v[:, :, :, HD + 1:], 0.0).then_inc(preset, 1)
                nc.gpsimd.memset(wide_v[:, :, :, HD1:], 1.0).then_inc(preset, 1)
                pool.wait_ge(preset, 1)
                pool.wait_ge(simn_in, 1)
                nc.gpsimd.tensor_tensor(simn[:, :], simsq[:, :], k.half[:, :], ALU.pow).then_inc(simn_ready, 1)

            @block.vector
            def _(dve):
                v = nc.vector
                dve.wait_ge(all_ctx_in, 16)
                chain.link(dve, v.tensor_tensor(sq16, ctx16, ctx16, ALU.mult))
                chain.link(dve, v.tensor_reduce(head_sq, sq16.rearrange("p (n d) -> p n d", d=HD), AX.X, ALU.add))
                v.tensor_reduce(least[:, :], head_sq, AX.X, ALU.min).then_inc(least_ready, 1)
                dve.wait_ge(least_row, 1)
                v.tensor_reduce(least1[:, :], k.psum[0][0:1, 0:P], AX.X, ALU.min).then_inc(least1_ready, 1)
                dve.wait_ge(least_bc, 1)
                v.tensor_scalar(k.kbias[:, :], k.psum[1][:, 0:1], 0.5 * RF_SCALE ** 2, None, ALU.mult)
                dve.wait_ge(weights_in["const"], 16)
                v.tensor_tensor(simsq[:, :], k.w["sim"], k.w["sim"], ALU.mult).then_inc(simsq_ready, 1)
                dve.wait_ge(sim_ps, 1)
                v.tensor_scalar(simsq[:, :], k.psum[4][:, 0:E16], 1e-24, None, ALU.max).then_inc(simn_in, 1)
                dve.wait_ge(simn_ready, 1)
                v.tensor_tensor(k.sn[:, :], k.w["sim"], simn[:, :], ALU.mult)
                dve.wait_ge(gates_th, 1)
                v.tensor_scalar(k.sig[:, :], th[:, :], 0.5, 0.5, ALU.mult, ALU.add)
                for L in (0, 2, 3):
                    v.tensor_scalar(k.bq_scaled[f"bq{L}"][:, :], k.w[f"bq{L}"], HD ** -0.5, None, ALU.mult)

            @block.tensor
            def _(pe):
                pe.wait_ge(weights_in["const"], 16)
                pe.wait_ge(least_ready, 1)
                k.turn(k.psum[0][0:1, 0:P], least[:, :]).then_inc(least_row, 1)
                pe.wait_ge(least1_ready, 1)
                nc.tensor.matmul(k.psum[1][:, 0:1], k.w["ones"][0:1, :], least1[:, :], start=True, stop=True).then_inc(least_bc, 1)
                pe.wait_ge(rows_in, 16)
                nc.tensor.matmul(k.psum[2][:, 0:8], k.w["ones"][0:1, :], k.w["g"], start=True, stop=True).then_inc(g_ps, 1)
                nc.tensor.matmul(k.psum[3][:, 0:E16], k.w["ones"][0:1, :], k.w["gates"], start=True, stop=True).then_inc(gates_ps, 1)
                pe.wait_ge(simsq_ready, 1)
                nc.tensor.matmul(k.psum[4][:, 0:E16], k.w["ones"], simsq[:, :], start=True, stop=True).then_inc(sim_ps, 1)

            @block.scalar
            def _(act):
                act.wait_ge(weights_in["const"], 16)
                nc.scalar.activation(k.ident16[:, :], k.w["ident"], ACT.Copy)
                nc.scalar.activation(k.part_rows16[:, :], k.w["part_rows"], ACT.Copy)
                act.wait_ge(g_ps, 1)
                nc.scalar.activation(k.tg[:, :], k.psum[2][:, 0:8], ACT.Tanh)
                act.wait_ge(gates_ps, 1)
                nc.scalar.activation(th[:, :], k.psum[3][:, 0:E16], ACT.Tanh, scale=0.5).then_inc(gates_th, 1)
        numbers = [q.num for q in setup_sems.values()]
        nc.all_engine_barrier(sems_to_clear=range(min(numbers), max(numbers) + 1))
        setup.close()
        Chunk0(k, 0, 0, 0)
        for make in (Chunk1, Chunk2, Chunk3):
            make(k, 0)

        run_block(k, [Chunk0(k, 0, None, 0), LaterWeights(k, dram, weights_in)], PACE_FIRST)
        run_block(k, [Chunk1(k, 0), Chunk0(k, 1, None, 1)], PACE_FIRST)
        with nc.Fori(0, NB // 2 - 1) as n:
            i = n * 2
            run_block(k, [Chunk1(k, 1), Chunk2(k, 0)], PACE_1_2)
            run_block(k, [Chunk3(k, 0), Chunk2(k, 1)], PACE_3_2)
            run_block(k, [Chunk3(k, 1), Chunk0(k, 0, i, i + 2)], PACE_3_0)
            run_block(k, [Chunk1(k, 0), Chunk0(k, 1, i + 1, i + 3)], PACE_1_0)
        run_block(k, [Chunk1(k, 1), Chunk2(k, 0)], PACE_1_2)
        run_block(k, [Chunk3(k, 0), Chunk2(k, 1)], PACE_3_2)
        run_block(k, [Chunk3(k, 1), Chunk0(k, 0, NB - 2, None)], PACE_LAST)
        run_block(k, [Chunk0(k, 1, NB - 1, None)], PACE_LAST)


def kernel(**inputs):
    import concourse.bacc as bacc
    from concourse.bass_utils import run_bass_kernel_spmd

    a = {n: np.asarray(v) for n, v in inputs.items()}
    f = np.float32

    def with_rows_below(b, rows):
        out = np.zeros((P, D), f)
        out[:b.shape[0]] = b
        for i, row in enumerate(rows):
            out[32 * (i + 1)] = row
        return out

    def side_by_side(w):
        return w.transpose(1, 0, 2).reshape(w.shape[1], -1)

    rf = np.zeros((NG, HG, HD, NG, HG, PAD), f)
    hsum = np.zeros((NG, HG, HD, NG, HG, PAD), f)
    for g in range(NG):
        for h in range(HG):
            rf[g, h, :, g, h, :] = a["L0_xattn_random_features"]
            hsum[g, h, :, g, h, :] = -0.5 * RF_SCALE
    w_qkv, b_qkv = a["L0_ffn_W_qkv"], a["L0_ffn_b_qkv"]
    parts = {
        "ident": np.eye(P, dtype=f), "tri": np.triu(np.ones((P, P), f)), "ones": np.ones((P, P), f),
        "hsum": hsum.reshape(D, -1), "head_rows": np.kron(np.eye(H, dtype=f), np.ones((HD, 1), f)),
        "group_rows": np.kron(np.eye(HG, dtype=f), np.ones((PAD, 1), f)),
        "part_rows": np.concatenate([np.tile(np.eye(E16, dtype=f), (PARTS, 1)), np.zeros((P - PARTS * E16, E16), f)]),
        "rf": rf.reshape(D, -1), "wq0": w_qkv[:, 0:D], "wk0": w_qkv[:, D:2 * D],
        "wv0": w_qkv[:, 2 * D:], "gate0": a["L0_ffn_W_gate"], "exp0": side_by_side(a["L0_ffn_W_experts"]),
        "bq0": b_qkv[0:D].reshape(D, 1), "bk0": b_qkv[D:2 * D].reshape(D, 1),
        "wq1": a["L1_xattn_Wq"], "wk1": a["L1_xattn_Wkv"][:, :H1 * HD1], "wv1": a["L1_xattn_Wkv"][:, H1 * HD1:],
        "wo1": side_by_side(a["L1_xattn_Wout"].reshape(4, P, D)),
        "router1": a["L1_ffn_w_router"], "fc1": side_by_side(a["L1_ffn_fc1_w"]), "fc2": side_by_side(a["L1_ffn_fc2_w"]),
        "gate_w": a["L1_ffn_gate_w"], "up_w": a["L1_ffn_up_w"], "down_w": side_by_side(a["L1_ffn_down_w"].reshape(2, P, D)),
        "router2": a["L2_ffn_router_w"],
        "b1": np.concatenate([a["L2_ffn_shared_b1"].reshape(1, FF2, P), a["L2_ffn_exp_b1"].reshape(E8, FF2, P)]).transpose(2, 0, 1).reshape(P, -1),
        "w1": side_by_side(np.concatenate([a["L2_ffn_shared_w1"].reshape(1, D, -1), a["L2_ffn_exp_w1"]])),
        "w2": side_by_side(np.concatenate([a["L2_ffn_shared_w2"].reshape(FF2, P, D), a["L2_ffn_exp_w2"].reshape(E8 * FF2, P, D)])),
        "sim": a["L3_ffn_sim_matrix"],
        "qp": side_by_side(a["L3_ffn_q_proj"]), "kp": side_by_side(a["L3_ffn_k_proj"]),
        "vp": side_by_side(a["L3_ffn_v_proj"]), "op": side_by_side(a["L3_ffn_o_proj"]),
        "bv0": b_qkv[2 * D:], "bgate0": a["L0_ffn_b_gate"], "bout1": a["L1_xattn_bout"], "br2": a["L2_ffn_router_b"],
        "gates": a["L3_ffn_gates"], "g": np.concatenate([a["g_xattn"], a["g_ffn"]]),
    }
    for L in (2, 3):
        for c in "qkvo":
            parts[f"w{c}{L}"] = a[f"L{L}_xattn_W{c}"].T
        parts[f"bq{L}"], parts[f"bk{L}"] = (a[f"L{L}_xattn_b{c}"].reshape(D, 1) for c in "qk")
        parts[f"bv{L}"], parts[f"bo{L}"] = (a[f"L{L}_xattn_b{c}"] for c in "vo")
    parts["bias0"] = with_rows_below(a["L0_ffn_b_experts"], [parts[n] for n in BELOW["bias0"]])
    parts["bias2"] = with_rows_below(np.concatenate([a["L2_ffn_exp_b2"], a["L2_ffn_shared_b2"].reshape(1, D)]),
                                     [parts[n] for n in BELOW["bias2"]])
    ctx2d = a["ctx_1024"].reshape(NB * T, D)
    arrays = {name: np.concatenate([parts[n] for n, _ in pack], axis=1) for name, pack in PACKS}
    arrays["rows"] = np.concatenate([parts[n] for n, _ in ROWS]).reshape(1, -1)
    arrays["x"], arrays["ctx"], arrays["ctxT"] = a["x"].reshape(NB * T, D), ctx2d, ctx2d.T
    arrays = {f"in_{n}": np.ascontiguousarray(v) for n, v in arrays.items()}

    nc = bacc.Bacc("TRN2", target_bir_lowering=False, num_devices=1)
    dram = {n[3:]: nc.dram_tensor(n, v.shape, F32, kind="ExternalInput").ap() for n, v in arrays.items()}
    dram["out"] = nc.dram_tensor("out_x", (NB * T, D), F32, kind="ExternalOutput").ap()
    flamingo(nc, dram)
    r = run_bass_kernel_spmd(nc, [arrays], core_ids=[0])
    return r.results[0]["out_x"].reshape(NB, T, D)
```
